# Optimizing a Trainium2 kernel written in Bass

```python
import numpy as np
import jax
import jax.numpy as jnp

def _softmax(x, axis=-1):
    return jax.nn.softmax(x, axis=axis)

def _gelu(x):
    return jax.nn.gelu(x, approximate=True)

def _silu(x):
    return jax.nn.silu(x)

def _sigmoid(x):
    return jax.nn.sigmoid(x)

def _layernorm(x, axis=-1, eps=1e-05):
    m = jnp.mean(x, axis=axis, keepdims=True)
    v = jnp.var(x, axis=axis, keepdims=True)
    return (x - m) / jnp.sqrt(v + eps)

def _scatter_add(tgt, idx, src, axis=0):
    return tgt.at[idx].add(src)

def _segment_sum(src, seg, n):
    return jax.ops.segment_sum(src, seg, n)
kernel_name = 'mk_lm_tower_d1_tok_ids512_r4_56e98f'

def setup_inputs(seed: int=0):
    np.random.seed(seed)
    _w = jnp.asarray

    def _rec_inputs():
        import jax
        import jax.numpy as jnp
        _rk = jax.random.key(seed)
        x = jax.random.randint(jax.random.fold_in(_rk, 1), (128, 128), 0, 8000, jnp.int32)
        return x
    x = _rec_inputs()

    def _L0_tok_setup():
        import jax, jax.numpy as jnp
        import numpy as np
        VOCAB = 8000
        EMB = 128
        K = 3
        B, T = (8, 1024)
        key = jax.random.key(seed)
        k_ids, k_w = jax.random.split(key)
        token_ids = jax.random.randint(k_ids, (B, T), 0, VOCAB, dtype=jnp.int64)
        conv_w = jax.random.normal(k_w, (EMB, VOCAB, K), dtype=jnp.float32) * 0.02
        return {'token_ids': token_ids, 'conv_w': conv_w}
    _L0_tok_all = _L0_tok_setup()
    _L0_tok_in = {k: v for k, v in _L0_tok_all.items() if k in ('conv_w',)}
    del _L0_tok_all

    def _L0_attn_setup():
        import jax, jax.numpy as jnp
        import numpy as np
        B, S, D = (8, 512, 128)
        QK_DIM = 128
        HID = 2 * D
        EPS = 1e-05

        def _layernorm(x, g, b):
            mu = jnp.mean(x, axis=-1, keepdims=True)
            var = jnp.mean((x - mu) ** 2, axis=-1, keepdims=True)
            return (x - mu) * jax.lax.rsqrt(var + EPS) * g + b
        key = jax.random.key(seed)
        ks = jax.random.split(key, 8)
        std = 0.02
        return {'x': jax.random.normal(ks[0], (B, S, D), dtype=jnp.float32), 'ln_g': jnp.ones((D,), jnp.float32), 'ln_b': jnp.zeros((D,), jnp.float32), 'Wh': jax.random.normal(ks[1], (D, HID * 2), jnp.float32) * std, 'bh': jnp.zeros((HID * 2,), jnp.float32), 'Wqk': jax.random.normal(ks[2], (D, QK_DIM), jnp.float32) * std, 'bqk': jnp.zeros((QK_DIM,), jnp.float32), 'gamma': jax.random.normal(ks[3], (2, QK_DIM), jnp.float32) * std, 'beta': jnp.zeros((2, QK_DIM), jnp.float32), 'Wo': jax.random.normal(ks[4], (HID, D), jnp.float32) * std, 'bo': jnp.zeros((D,), jnp.float32)}
    _L0_attn_all = _L0_attn_setup()
    _L0_attn_in = {k: v for k, v in _L0_attn_all.items() if k in ('ln_g', 'ln_b', 'Wh', 'bh', 'Wqk', 'bqk', 'gamma', 'beta', 'Wo', 'bo')}
    del _L0_attn_all

    def _L0_ffn_setup():
        import jax, jax.numpy as jnp
        import numpy as np
        EPS = 1e-05
        NUM_HEADS = 8
        TOP_K = 2
        CAP_FACTOR = 2

        def layernorm(x, g, b):
            m = jnp.mean(x, axis=-1, keepdims=True)
            v = jnp.var(x, axis=-1, keepdims=True)
            return (x - m) * jax.lax.rsqrt(v + EPS) * g + b
        key = jax.random.key(seed)
        ks = jax.random.split(key, 16)
        B, S, H, E, F = (2, 512, 128, 64, 512)
        s = 0.02
        return {'x': jax.random.normal(ks[0], (B, S, H), jnp.float32), 'ln1_g': jnp.ones((H,), jnp.float32), 'ln1_b': jnp.zeros((H,), jnp.float32), 'wq': jax.random.normal(ks[1], (H, H), jnp.float32) * s, 'wk': jax.random.normal(ks[2], (H, H), jnp.float32) * s, 'wv': jax.random.normal(ks[3], (H, H), jnp.float32) * s, 'wo': jax.random.normal(ks[4], (H, H), jnp.float32) * s, 'ln2_g': jnp.ones((H,), jnp.float32), 'ln2_b': jnp.zeros((H,), jnp.float32), 'wr': jax.random.normal(ks[5], (H, E), jnp.float32) * s, 'w1': jax.random.normal(ks[6], (E, H, F), jnp.float32) * s, 'b1': jnp.zeros((E, F), jnp.float32), 'w2': jax.random.normal(ks[7], (E, F, H), jnp.float32) * s, 'b2': jnp.zeros((E, H), jnp.float32)}
    _L0_ffn_all = _L0_ffn_setup()
    _L0_ffn_in = {k: v for k, v in _L0_ffn_all.items() if k in ('ln1_g', 'ln1_b', 'wq', 'wk', 'wv', 'wo', 'ln2_g', 'ln2_b', 'wr', 'w1', 'b1', 'w2', 'b2')}
    del _L0_ffn_all
    return {'x': x, 'L0_tok_conv_w': _L0_tok_in['conv_w'], 'L0_attn_ln_g': _L0_attn_in['ln_g'], 'L0_attn_ln_b': _L0_attn_in['ln_b'], 'L0_attn_Wh': _L0_attn_in['Wh'], 'L0_attn_bh': _L0_attn_in['bh'], 'L0_attn_Wqk': _L0_attn_in['Wqk'], 'L0_attn_bqk': _L0_attn_in['bqk'], 'L0_attn_gamma': _L0_attn_in['gamma'], 'L0_attn_beta': _L0_attn_in['beta'], 'L0_attn_Wo': _L0_attn_in['Wo'], 'L0_attn_bo': _L0_attn_in['bo'], 'L0_ffn_ln1_g': _L0_ffn_in['ln1_g'], 'L0_ffn_ln1_b': _L0_ffn_in['ln1_b'], 'L0_ffn_wq': _L0_ffn_in['wq'], 'L0_ffn_wk': _L0_ffn_in['wk'], 'L0_ffn_wv': _L0_ffn_in['wv'], 'L0_ffn_wo': _L0_ffn_in['wo'], 'L0_ffn_ln2_g': _L0_ffn_in['ln2_g'], 'L0_ffn_ln2_b': _L0_ffn_in['ln2_b'], 'L0_ffn_wr': _L0_ffn_in['wr'], 'L0_ffn_w1': _L0_ffn_in['w1'], 'L0_ffn_b1': _L0_ffn_in['b1'], 'L0_ffn_w2': _L0_ffn_in['w2'], 'L0_ffn_b2': _L0_ffn_in['b2']}

def reference(x, L0_tok_conv_w, L0_attn_ln_g, L0_attn_ln_b, L0_attn_Wh, L0_attn_bh, L0_attn_Wqk, L0_attn_bqk, L0_attn_gamma, L0_attn_beta, L0_attn_Wo, L0_attn_bo, L0_ffn_ln1_g, L0_ffn_ln1_b, L0_ffn_wq, L0_ffn_wk, L0_ffn_wv, L0_ffn_wo, L0_ffn_ln2_g, L0_ffn_ln2_b, L0_ffn_wr, L0_ffn_w1, L0_ffn_b1, L0_ffn_w2, L0_ffn_b2):
    import jax
    import jax.numpy as jnp

    def _L0_tok_ref(token_ids, conv_w):
        import jax, jax.numpy as jnp
        import numpy as np
        VOCAB = 8000
        EMB = 128
        K = 3
        B, T = (8, 1024)
        'Equivalent to one_hot(token_ids) -> Conv1d(V->F, k=K, pad=K//2, no bias).\n\n            Because the conv input is one-hot over the vocab channel, the V-dim\n            contraction reduces to gathering one weight row per (position, tap):\n              out[b,t,f] = sum_k W[f, token[b, t+k-pad], k]   (zero outside [0,T)).\n            '
        Bn, Tn = token_ids.shape
        F_, V_, Kn = conv_w.shape
        pad = Kn // 2
        out = jnp.zeros((Bn, Tn, F_), dtype=conv_w.dtype)
        t = jnp.arange(Tn)
        for k in range(Kn):
            shift = k - pad
            src = t + shift
            valid = (src >= 0) & (src < Tn)
            src_c = jnp.clip(src, 0, Tn - 1)
            ids = token_ids[:, src_c]
            table_k = conv_w[:, :, k].T
            emb = table_k[ids]
            out = out + jnp.where(valid[None, :, None], emb, jnp.zeros((), conv_w.dtype))
        return out

    def _L0_attn_ref(x, ln_g, ln_b, Wh, bh, Wqk, bqk, gamma, beta, Wo, bo):
        import jax, jax.numpy as jnp
        import numpy as np
        B, S, D = (8, 512, 128)
        QK_DIM = 128
        HID = 2 * D
        EPS = 1e-05

        def _layernorm(x, g, b):
            mu = jnp.mean(x, axis=-1, keepdims=True)
            var = jnp.mean((x - mu) ** 2, axis=-1, keepdims=True)
            return (x - mu) * jax.lax.rsqrt(var + EPS) * g + b
        seq_len = x.shape[-2]
        normed = _layernorm(x, ln_g, ln_b)
        hid = jax.nn.silu(normed @ Wh + bh)
        v, gate = jnp.split(hid, 2, axis=-1)
        Z = jax.nn.silu(normed @ Wqk + bqk)
        QK = Z[..., None, :] * gamma + beta
        q, k = (QK[..., 0, :], QK[..., 1, :])
        sim = jnp.einsum('bid,bjd->bij', q, k) / seq_len
        A = jnp.square(jax.nn.relu(sim))
        V = jnp.einsum('bij,bjd->bid', A, v) * gate
        out = V @ Wo + bo
        return out + x

    def _L0_ffn_ref(x, ln1_g, ln1_b, wq, wk, wv, wo, ln2_g, ln2_b, wr, w1, b1, w2, b2):
        import jax, jax.numpy as jnp
        import numpy as np
        EPS = 1e-05
        NUM_HEADS = 8
        TOP_K = 2
        CAP_FACTOR = 2

        def layernorm(x, g, b):
            m = jnp.mean(x, axis=-1, keepdims=True)
            v = jnp.var(x, axis=-1, keepdims=True)
            return (x - m) * jax.lax.rsqrt(v + EPS) * g + b
        B, S, H = x.shape
        NH = NUM_HEADS
        dh = H // NH
        x1 = layernorm(x, ln1_g, ln1_b)
        q = (x1 @ wq).reshape(B, S, NH, dh)
        k = (x1 @ wk).reshape(B, S, NH, dh)
        v = (x1 @ wv).reshape(B, S, NH, dh)
        scores = jnp.einsum('bqhd,bkhd->bhqk', q, k) * dh ** (-0.5)
        p = jax.nn.softmax(scores, axis=-1)
        attn_out = jnp.einsum('bhqk,bkhd->bqhd', p, v).reshape(B, S, H) @ wo
        x = x + attn_out
        x2 = layernorm(x, ln2_g, ln2_b).reshape(B * S, H)
        T = B * S
        E = wr.shape[1]
        C = CAP_FACTOR * (T * TOP_K // E)
        probs = jax.nn.softmax(x2 @ wr, axis=-1)
        gate_v, gate_i = jax.lax.top_k(probs, TOP_K)
        gate_v = gate_v / jnp.sum(gate_v, axis=-1, keepdims=True)
        ef = gate_i.reshape(-1)
        gf = gate_v.reshape(-1)
        oh = jax.nn.one_hot(ef, E, dtype=x2.dtype)
        pos = jnp.sum((jnp.cumsum(oh, axis=0) - oh) * oh, axis=1).astype(jnp.int32)
        keep = (pos < C).astype(x2.dtype)
        posc = jnp.minimum(pos, C - 1)
        tok = jnp.repeat(x2, TOP_K, axis=0) * keep[:, None]
        buf = jnp.zeros((E, C, H), x2.dtype).at[ef, posc].add(tok)
        h = jax.nn.gelu(jnp.einsum('ech,ehf->ecf', buf, w1) + b1[:, None, :])
        y = jnp.einsum('ecf,efh->ech', h, w2) + b2[:, None, :]
        ys = y[ef, posc] * (gf * keep)[:, None]
        moe_out = ys.reshape(T, TOP_K, H).sum(axis=1).reshape(B, S, H)
        return x + moe_out
    h = _L0_tok_ref(x, L0_tok_conv_w)
    h = h + _L0_attn_ref(_layernorm(h, axis=-1), L0_attn_ln_g, L0_attn_ln_b, L0_attn_Wh, L0_attn_bh, L0_attn_Wqk, L0_attn_bqk, L0_attn_gamma, L0_attn_beta, L0_attn_Wo, L0_attn_bo)
    h = h + _L0_ffn_ref(_layernorm(h, axis=-1), L0_ffn_ln1_g, L0_ffn_ln1_b, L0_ffn_wq, L0_ffn_wk, L0_ffn_wv, L0_ffn_wo, L0_ffn_ln2_g, L0_ffn_ln2_b, L0_ffn_wr, L0_ffn_w1, L0_ffn_b1, L0_ffn_w2, L0_ffn_b2)
    return h

_drawn_inputs = setup_inputs


def setup_inputs(seed=0):
    import zlib

    import numpy as np

    out = dict(_drawn_inputs(seed))
    spreads = {'L0_attn_ln_g': (1.0, 0.6),
     'L0_attn_ln_b': (0.0, 0.8),
     'L0_attn_bh': (0.0, 0.8),
     'L0_attn_bqk': (0.0, 0.8),
     'L0_attn_beta': (0.0, 0.8),
     'L0_attn_bo': (0.0, 0.1),
     'L0_ffn_ln1_g': (1.0, 0.6),
     'L0_ffn_ln1_b': (0.0, 0.8),
     'L0_ffn_ln2_g': (1.0, 0.6),
     'L0_ffn_ln2_b': (0.0, 0.419),
     'L0_ffn_b1': (0.0, 0.8),
     'L0_ffn_b2': (0.0, 0.8)}
    factors = {'L0_attn_Wh': 8.0,
     'L0_attn_Wqk': 8.0,
     'L0_attn_gamma': 8.0,
     'L0_attn_Wo': 8.0,
     'L0_ffn_wq': 8.0,
     'L0_ffn_wk': 8.0,
     'L0_ffn_wv': 8.0,
     'L0_ffn_wo': 8.0,
     'L0_ffn_w1': 2.976,
     'L0_ffn_w2': 2.694}
    for name, (base, spread) in spreads.items():
        noise = np.random.default_rng([zlib.crc32(name.encode()), seed]).standard_normal(out[name].shape)
        drawn = base * np.exp(spread * noise) if base else spread * noise
        out[name] = jnp.asarray(drawn.astype(out[name].dtype))
    for name, factor in factors.items():
        out[name] = (out[name] * factor).astype(out[name].dtype)
    return out
```

```python
from contextlib import ExitStack

import numpy as np
import concourse.bass as bass
from concourse import mybir

F32 = mybir.dt.float32
BF16 = mybir.dt.bfloat16
I32 = mybir.dt.int32
U32 = mybir.dt.uint32
ALU = mybir.AluOpType
ACT = mybir.ActivationFunctionType
AX = mybir.AxisListType.X

P = 128
VOCAB = 8000
TAPS = 3
SEQS = 128
G = 4
GROUPS = SEQS // G
N = G * P
HEADS = 8
DH = P // HEADS
E = 64
FF = 512
FC = FF // P
TOKENS = SEQS * P
CAP = 2 * (TOKENS * 2 // E)
SLOTS = E * CAP
UNIT = 512
UNITS = CAP // UNIT
ROW = 132
EPS = 1e-5
BACK_PART = 2048
BACK_PARTS = TOKENS * 2 // BACK_PART
NOWHERE = 1 << 24
(C_LNG, C_LNB, C_BQK, C_GA0, C_GA1, C_BE0, C_BE1, C_BO, C_BG0, C_BG1,
 C_L1G, C_L1B, C_L2G, C_L2B) = range(14)
NVEC = 14


def after(eng, sem, value):
    if not isinstance(value, int) or value > 0:
        eng.wait_ge(sem, value)


def pipelined(eng, body, lag, pairs_from=2):
    for i in range(2 * pairs_from):
        body(i, i // 2, i % 2, lambda l, i=i: 0 <= i - l)
    with eng.Fori(pairs_from, GROUPS // 2) as pair:
        for parity in range(2):
            body(pair * 2 + parity, pair, parity, lambda l: True)
    for i in range(GROUPS, GROUPS + lag):
        body(i, i // 2, i % 2, lambda l, i=i: i - l < GROUPS)


def settle(eng, s):
    eng.sem_inc(s.settled, 1)


class Shared:
    pass


def constants(nc, ctx, s, ins):
    def sb(name, shape, dt=F32):
        return ctx.enter_context(nc.sbuf_tensor(name, shape, dt))
    s.vec = sb("vec", [P, NVEC])
    s.ident = sb("ident", [P, P])
    s.h = sb("h_all", [P, SEQS, P])
    s.gates = sb("gates", [P, SEQS, 2])
    s.expo = sb("expo", [P, 2 * G])
    const_ready = s.const_ready = ctx.enter_context(nc.semaphore("const_ready"))
    s.settled = ctx.enter_context(nc.semaphore("settled"))
    vec_loaded = ctx.enter_context(nc.semaphore("vec_loaded"))
    with nc.Block() as block:
        @block.sync
        def _(sp):
            sp.dma_start(s.vec[:], ins["vecs"]).then_inc(vec_loaded, 16)
            sp.wait_ge(vec_loaded, 16)

        @block.gpsimd
        def _(pool):
            nc.gpsimd.memset(s.ident[:], 1.0).then_inc(const_ready, 1)
            nc.gpsimd.memset(s.expo[:], -0.5).then_inc(const_ready, 1)
            pool.wait_ge(const_ready, 2)
            nc.gpsimd.affine_select(out=s.ident[:], in_=s.ident[:], compare_op=ALU.is_equal, fill=0.0,
                                    base=0, pattern=[[-1, P]], channel_multiplier=1).then_inc(const_ready, 1)
            pool.wait_ge(const_ready, 3)


def phase1(nc, s, ins):
    with ExitStack() as ctx:
        def sb(name, shape, dt=F32):
            return ctx.enter_context(nc.sbuf_tensor("a_" + name, shape, dt))

        def sem(name):
            return ctx.enter_context(nc.semaphore("a_" + name))

        ids = sb("ids", [P, SEQS], I32)
        idx = [sb(f"idx{i}", [P, G], I32) for i in range(2)]
        emb = [sb(f"emb{i}", [P, G, TAPS * P]) for i in range(2)]
        wh = sb("wh", [P, 512])
        wqk = sb("wqk", [P, P])
        wo = sb("wo", [P, 2, P])
        bv = sb("bv", [P, 2 * P])
        down = sb("down", [P, P])
        up = sb("up", [P, P])
        zrow = sb("zrow", [P, 8, ROW])
        zm = sb("zm", [P, BACK_PART])
        h0 = [sb(f"h0_{i}", [P, G, P]) for i in range(2)]
        bn = sb("bn", [P, G, 6])
        mv = [sb(f"mv{i}", [P, G, 2]) for i in range(2)]
        ve = sb("ve", [P, 2, G])
        rs = [sb(f"rs{i}", [P, 2, G]) for i in range(2)]
        u = sb("u", [P, G, P])
        n = [sb(f"n{i}", [P, G, P]) for i in range(2)]
        nt = [sb(f"nt{i}", [P, N]) for i in range(2)]
        z = [sb(f"z{i}", [P, N]) for i in range(2)]
        q = [sb(f"q{i}", [P, N]) for i in range(2)]
        k = [sb(f"k{i}", [P, N]) for i in range(2)]
        gate = [sb(f"gate{i}", [P, 2, N]) for i in range(2)]
        vpre = sb("vpre", [P, G, 2 * P])
        v = [sb(f"v{i}", [P, G, 2 * P]) for i in range(2)]
        r = sb("r", [P, N])
        at = sb("at", [P, N])
        vg = sb("vg", [P, 2, N])
        ot = sb("ot", [P, N])
        bank = [ctx.enter_context(nc.psum_tensor(f"a_bank{i}", [P, 512], F32)) for i in range(8)]
        b_conv, b_n, b_x, b_y, b_s, b_vt0, b_vt1, b_ot = bank

        loaded, shift_made, zero_made, zeroed = sem("loaded"), sem("shift_made"), sem("zero_made"), sem("zeroed")
        idx_ready = sem("idx_ready")
        emb_in = [sem(f"emb_in{i}") for i in range(2)]
        conv_done, h0_done, bn_done, mv_done = sem("conv"), sem("h0"), sem("bn"), sem("mv")
        ve_done, rs_done, u_done, hu_done = sem("ve"), sem("rs"), sem("u"), sem("hu")
        n_done, nt_ps, nt_done = sem("n"), sem("nt_ps"), sem("nt")
        z_ps, g_ps, v_ps = sem("z_ps"), sem("g_ps"), sem("v_ps")
        z_done, g_done, vb_done, v_done, qk_done = sem("z"), sem("g"), sem("vb"), sem("v"), sem("qk")
        sim_ps, r_done, at_done, vt_ps, vg_done = sem("sim_ps"), sem("r"), sem("at"), sem("vt_ps"), sem("vg")
        ot_ps, ot_done, o_ps, h1_done = sem("ot_ps"), sem("ot"), sem("o_ps"), sem("h1")
        LOADS = 6

        with nc.Block() as block:
            @block.sync
            def _(sp):
                for dst, src in ((ids[:], ins["ids"]), (wqk[:], ins["Wqk"]), (wh[:], ins["Wh"]),
                                 (wo[:], ins["Wo"].rearrange("(c p) n -> p c n", p=P)),
                                 (bv[:], ins["bh"][:, 0:2 * P].to_broadcast([P, 2 * P]))):
                    sp.dma_start(dst, src).then_inc(loaded, 16)
                sp.wait_ge(zero_made, 3)
                with sp.Fori(0, E) as e:
                    sp.dma_start(ins["slot_parts"][bass.ds(e * P, P)], zrow[:]).then_inc(zeroed, 16)
                with sp.Fori(0, BACK_PARTS) as e:
                    sp.dma_start(ins["back_parts"][bass.ds(e * P, P)], zm[:]).then_inc(zeroed, 16)
                sp.wait_ge(zeroed, 16 * (E + BACK_PARTS))

            @block.gpsimd
            def _(pool):
                for m in (down, up):
                    nc.gpsimd.memset(m[:], 1.0).then_inc(shift_made, 1)
                pool.wait_ge(shift_made, 2)
                for m, way in ((down, 1), (up, -1)):
                    nc.gpsimd.affine_select(out=m[:], in_=m[:], compare_op=ALU.is_equal, fill=0.0, base=way,
                                            pattern=[[-1, P]], channel_multiplier=1).then_inc(shift_made, 1)
                pool.wait_ge(loaded, 16 * (LOADS - 1))

                def body(i, pair, par, on):
                    if on(0):
                        after(pool, conv_done, i - 1)
                        after(pool, h0_done, i - 1)
                        settle(pool, s)
                        nc.gpsimd.tensor_copy(idx[par][:], ids[:, bass.ds(i * G, G)]).then_inc(idx_ready, 1)
                        pool.wait_ge(idx_ready, i + 1)
                        settle(pool, s)
                        for t in range(G):
                            nc.gpsimd.indirect_dma_start(
                                emb[par][:, t, :], None, ins["table"],
                                bass.IndirectOffsetOnAxis(ap=idx[par][:, t:t + 1], axis=0),
                                bounds_check=VOCAB - 1, oob_is_err=False).then_inc(emb_in[par], 16)
                    if on(1):
                        g, b = i - 1, 1 - par
                        pool.wait_ge(mv_done, G * g + G)
                        after(pool, n_done, g - 1)
                        settle(pool, s)
                        nc.gpsimd.tensor_scalar(ve[:, 0, :], mv[b][:, :, 1], EPS, None, ALU.add).then_inc(ve_done, 1)
                        nc.gpsimd.tensor_scalar(ve[:, 1, :], mv[b][:, :, 1], 1.0 + EPS, EPS * EPS,
                                                ALU.mult, ALU.add).then_inc(ve_done, 1)
                        pool.wait_ge(ve_done, 2 * g + 2)
                        settle(pool, s)
                        nc.gpsimd.tensor_tensor(rs[b][:].rearrange("p a t -> p (a t)"),
                                                ve[:].rearrange("p a t -> p (a t)"), s.expo[:],
                                                ALU.pow).then_inc(rs_done, 1)
                        pool.wait_ge(rs_done, g + 1)
                        after(pool, hu_done, g)
                        settle(pool, s)
                        for t in range(G):
                            last = nc.gpsimd.tensor_scalar(u[:, t, :], h0[b][:, t, :], mv[b][:, t, 0:1],
                                                           rs[b][:, 0, t:t + 1], ALU.subtract, ALU.mult)
                        last.then_inc(u_done, 1)
                        pool.wait_ge(u_done, g + 1)
                        settle(pool, s)
                        nc.gpsimd.tensor_tensor(s.h[:, bass.ds(g * G, G), :], u[:], h0[b][:],
                                                ALU.add).then_inc(hu_done, 1)

                pipelined(pool, body, 1)

            @block.tensor
            def _(pe):
                pe.wait_ge(loaded, 16 * (LOADS - 1))
                pe.wait_ge(shift_made, 4)

                def body(i, pair, par, on):
                    g, b = i - 2, par
                    w, c = i - 3, 1 - par
                    if on(2):
                        pe.wait_ge(n_done, g + 1)
                        after(pe, nt_done, g)
                        for t in range(G):
                            last = nc.tensor.transpose(b_n[:, t * P:(t + 1) * P], n[b][:, t, :], s.ident[:])
                        last.then_inc(nt_ps, 1)
                    if on(3):
                        pe.wait_ge(qk_done, 2 * w + 2)
                        after(pe, h1_done, w)
                        for t in range(G):
                            sl = slice(t * P, (t + 1) * P)
                            last = nc.tensor.matmul(b_s[:, sl], k[c][:, sl], q[c][:, sl], start=True, stop=True)
                        last.then_inc(sim_ps, 1)
                    if on(2):
                        pe.wait_ge(nt_done, g + 1)
                        after(pe, vb_done, 2 * g)
                        nc.tensor.matmul(b_x[:], wqk[:], nt[b][:], start=True, stop=True).then_inc(z_ps, 1)
                        nc.tensor.matmul(b_y[:], wh[:, 2 * P:3 * P], nt[b][:], start=True, stop=True).then_inc(g_ps, 1)
                    if on(3):
                        pe.wait_ge(at_done, w + 1)
                        pe.wait_ge(v_done, 2 * w + 2)
                        after(pe, vg_done, 2 * w)
                        for ch, bk in enumerate((b_vt0, b_vt1)):
                            for t in range(G):
                                sl = slice(t * P, (t + 1) * P)
                                last = nc.tensor.matmul(bk[:, sl], v[c][:, t, ch * P:(ch + 1) * P], at[:, sl],
                                                        start=True, stop=True)
                            last.then_inc(vt_ps, 1)
                    if on(2):
                        pe.wait_ge(z_done, g + 1)
                        nc.tensor.matmul(b_x[:], wh[:, 3 * P:4 * P], nt[b][:], start=True, stop=True).then_inc(g_ps, 1)
                        for half, bk in enumerate((b_y, b_x)):
                            pe.wait_ge(g_done, 2 * g + 1 + half)
                            for j in range(2):
                                t = 2 * half + j
                                last = nc.tensor.matmul(bk[:, j * 256:(j + 1) * 256], nt[b][:, t * P:(t + 1) * P],
                                                        wh[:, 0:2 * P], start=True, stop=True)
                            last.then_inc(v_ps, 1)
                    if on(3):
                        pe.wait_ge(vg_done, 2 * w + 2)
                        after(pe, ot_done, w)
                        for ch in range(2):
                            last = nc.tensor.matmul(b_ot[:], wo[:, ch, :], vg[:, ch, :], start=(ch == 0), stop=(ch == 1))
                        last.then_inc(ot_ps, 1)
                    if on(0):
                        pe.wait_ge(emb_in[par], pair * 16 * G + 16 * G)
                        after(pe, h0_done, i)
                        nc.tensor.matmul(b_conv[:], down[:], emb[par][:, :, 0:P], start=True, stop=False)
                        nc.tensor.matmul(b_conv[:], up[:], emb[par][:, :, 2 * P:3 * P], start=False,
                                         stop=True).then_inc(conv_done, 1)
                    if on(3):
                        pe.wait_ge(ot_done, w + 1)
                        pe.wait_ge(r_done, w + 1)
                        for t in range(G):
                            last = nc.tensor.transpose(b_s[:, t * P:(t + 1) * P], ot[:, t * P:(t + 1) * P], s.ident[:])
                        last.then_inc(o_ps, 1)

                pipelined(pe, body, 3)

            @block.scalar
            def _(act):
                def body(i, pair, par, on):
                    g, b = i - 2, par
                    w, c = i - 3, 1 - par
                    if on(2):
                        act.wait_ge(z_ps, g + 1)
                        after(act, qk_done, 2 * (g - 1))
                        nc.scalar.activation(z[b][:], b_x[:], ACT.Silu, bias=s.vec[:, C_BQK:C_BQK + 1]).then_inc(z_done, 1)
                    if on(3):
                        act.wait_ge(r_done, w + 1)
                        after(act, vt_ps, 2 * w)
                        nc.scalar.activation(at[:], r[:], ACT.Square).then_inc(at_done, 1)
                    if on(2):
                        after(act, vg_done, 2 * (g - 1))
                        for ch, bk in enumerate((b_y, b_x)):
                            act.wait_ge(g_ps, 2 * g + 1 + ch)
                            nc.scalar.activation(gate[b][:, ch, :], bk[:], ACT.Silu,
                                                 bias=s.vec[:, C_BG0 + ch:C_BG0 + ch + 1]).then_inc(g_done, 1)
                        after(act, vt_ps, 2 * (g - 1))
                        for half in range(2):
                            act.wait_ge(vb_done, 2 * g + 1 + half)
                            nc.scalar.activation(v[b][:, 2 * half:2 * half + 2, :], vpre[:, 2 * half:2 * half + 2, :],
                                                 ACT.Silu).then_inc(v_done, 1)
                    if on(3):
                        act.wait_ge(ot_ps, w + 1)
                        after(act, o_ps, w)
                        nc.scalar.activation(ot[:], b_ot[:], ACT.Identity, bias=s.vec[:, C_BO:C_BO + 1]).then_inc(ot_done, 1)

                pipelined(act, body, 3)

            @block.vector
            def _(dve):
                nc.vector.memset(zrow[:], 0.0).then_inc(zero_made, 1)
                nc.vector.memset(zm[:], 0.0).then_inc(zero_made, 1)
                dve.wait_ge(zero_made, 1)
                nc.vector.memset(zrow[:, :, P:P + 1].bitcast(I32), NOWHERE).then_inc(zero_made, 1)
                dve.wait_ge(loaded, 16 * (LOADS - 1))

                def body(i, pair, par, on):
                    g, b = i - 2, par
                    w, c = i - 3, 1 - par
                    if on(2):
                        dve.wait_ge(nt_ps, g + 1)
                        after(dve, v_ps, 2 * (g - 1))
                        nc.vector.tensor_scalar(nt[b][:], b_n[:], s.vec[:, C_LNG:C_LNG + 1], s.vec[:, C_LNB:C_LNB + 1],
                                                ALU.mult, ALU.add).then_inc(nt_done, 1)
                    if on(3):
                        dve.wait_ge(sim_ps, w + 1)
                        after(dve, at_done, w)
                        nc.vector.tensor_scalar(r[:], b_s[:], 0.0, 1.0 / P, ALU.max, ALU.mult).then_inc(r_done, 1)
                    if on(2):
                        dve.wait_ge(z_done, g + 1)
                        after(dve, sim_ps, g - 1)
                        for dst, ga, be in ((q, C_GA0, C_BE0), (k, C_GA1, C_BE1)):
                            nc.vector.tensor_scalar(dst[b][:], z[b][:], s.vec[:, ga:ga + 1], s.vec[:, be:be + 1],
                                                    ALU.mult, ALU.add).then_inc(qk_done, 1)
                    if on(3):
                        after(dve, ot_ps, w)
                        for ch, bk in enumerate((b_vt0, b_vt1)):
                            dve.wait_ge(vt_ps, 2 * w + 1 + ch)
                            nc.vector.tensor_tensor(vg[:, ch, :], bk[:], gate[c][:, ch, :], ALU.mult).then_inc(vg_done, 1)
                    if on(2):
                        for half, bk in enumerate((b_y, b_x)):
                            dve.wait_ge(v_ps, 2 * g + 1 + half)
                            after(dve, v_done, 2 * (g - 1) + 1 + half)
                            nc.vector.tensor_tensor(
                                vpre[:, 2 * half:2 * half + 2, :], bk[:].rearrange("p (j n) -> p j n", j=2),
                                bv[:].rearrange("p (j n) -> p j n", j=1).to_broadcast([P, 2, 2 * P]),
                                ALU.add).then_inc(vb_done, 1)
                    if on(0):
                        dve.wait_ge(conv_done, i + 1)
                        after(dve, hu_done, i - 1)
                        nc.vector.tensor_tensor(h0[par][:], b_conv[:].rearrange("p (t n) -> p t n", t=G),
                                                emb[par][:, :, P:2 * P], ALU.add).then_inc(h0_done, 1)
                        dve.wait_ge(h0_done, i + 1)
                        after(dve, mv_done, G * i)
                        settle(dve, s)
                        for t in range(G):
                            nc.vector.bn_stats(bn[:, t, :], h0[par][:, t, :]).then_inc(bn_done, 1)
                        for t in range(G):
                            dve.wait_ge(bn_done, G * i + t + 1)
                            settle(dve, s)
                            nc.vector.bn_aggr(mv[par][:, t, :], bn[:, t, :]).then_inc(mv_done, 1)
                    if on(1):
                        m, d = i - 1, 1 - par
                        dve.wait_ge(rs_done, m + 1)
                        after(dve, nt_ps, m - 1)
                        for t in range(G):
                            last = nc.vector.tensor_scalar(n[d][:, t, :], h0[d][:, t, :], mv[d][:, t, 0:1],
                                                           rs[d][:, 1, t:t + 1], ALU.subtract, ALU.mult)
                        last.then_inc(n_done, 1)
                    if on(3):
                        dve.wait_ge(o_ps, w + 1)
                        dve.wait_ge(hu_done, w + 1)
                        hs = s.h[:, bass.ds(w * G, G), :]
                        nc.vector.tensor_tensor(hs, b_s[:].rearrange("p (t n) -> p t n", t=G), hs,
                                                ALU.add).then_inc(h1_done, 1)

                pipelined(dve, body, 3)


def phase2(nc, s, ins):
    with ExitStack() as ctx:
        def sb(name, shape, dt=F32):
            return ctx.enter_context(nc.sbuf_tensor("b_" + name, shape, dt))

        def two(name, shape, dt=F32):
            return [sb(f"{name}{i}", shape, dt) for i in range(2)]

        def sem(name):
            return ctx.enter_context(nc.semaphore("b_" + name))

        wq, wk, wv, wo = (sb(x, [P, P]) for x in ("wq", "wk", "wv", "wo"))
        wr = sb("wr", [P, E])
        headmask = sb("headmask", [P, HEADS])
        hm_tmp = sb("hm_tmp", [P, HEADS])
        iota_e = sb("iota_e", [P, E], I32)
        iota_f = sb("iota_f", [P, E])
        payload = sb("payload", [P, SEQS, 2], I32)
        before_f = sb("before_f", [P, P])
        before = sb("before", [P, P], BF16)
        ones = sb("ones", [P, P], BF16)
        onespad = sb("onespad", [P, 2, 32])
        bn = sb("bn", [P, G, 6])
        mv = two("mv", [P, G, 2])
        ve = sb("ve", [P, 2, G])
        rs = two("rs", [P, 2, G])
        nn = two("nn", [P, G, P])
        xa = two("xa", [P, G, P])
        n = two("n", [P, G, P])
        xt = sb("xt", [P, N])
        q = two("q", [P, N])
        k = sb("k", [P, N])
        km = two("km", [P, HEADS, N])
        vpad = two("vpad", [P, G * 4, 2, 32])
        mx = two("mx", [P, HEADS])
        ex = two("ex", [P, HEADS, P])
        et = two("et", [P, HEADS, P])
        rden = sb("rden", [P, N])
        att = sb("att", [P, N])
        bn2 = sb("bn2", [P, G, 6])
        mv2 = sb("mv2", [P, G, 2])
        ve2 = sb("ve2", [P, G])
        rs2 = sb("rs2", [P, G])
        rows = two("rows", [P, G, 2, ROW])
        x2t = sb("x2t", [P, N])
        lg = sb("lg", [P, G, E])
        top = sb("top", [P, G, 8])
        topi = sb("topi", [P, G, 8], U32)
        ixf = sb("ixf", [P, G, 2])
        dl = sb("dl", [P, G])
        el = sb("el", [P, G])
        oh = sb("oh", [P, G * 2, E])
        ohs = sb("ohs", [P, G, E], BF16)
        base = sb("base", [P, E])
        cb = sb("cb", [P, G, E])
        pm = sb("pm", [P, G * 2, E])
        pos = sb("pos", [P, G * 2])
        keep = sb("keep", [P, G * 2])
        far = sb("far", [P, G * 2])
        slot = sb("slot", [P, G * 2])
        sidx = two("sidx", [P, G * 2], I32)
        gs = sb("gs", [P, G])
        gg = sb("gg", [P, G, 2])
        p_o = ctx.enter_context(nc.psum_tensor("b_o", [P, 512], F32))
        p_d = ctx.enter_context(nc.psum_tensor("b_d", [P, 512], F32))
        b_x = ctx.enter_context(nc.psum_tensor("b_x", [P, 512], F32))
        b_y = ctx.enter_context(nc.psum_tensor("b_y", [P, 512], F32))
        p_s = ctx.enter_context(nc.psum_tensor("b_s", [P, 1024], F32))
        p_t = ctx.enter_context(nc.psum_tensor("b_t", [P, 1024], F32))

        loaded, made, filled = sem("loaded"), sem("made"), sem("filled")
        bn_done, mv_done, ve_done, rs_done, n_done = sem("bn"), sem("mv"), sem("ve"), sem("rs"), sem("n")
        copy_done, nn_done, sum_done = sem("copy"), sem("nn"), sem("sum")
        nt_ps, xt_done, q_ps, q_done, k_ps, k_done = (sem(x) for x in ("nt_ps", "xt", "q_ps", "q", "k_ps", "k"))
        km_done, v_ps, v_done = sem("km"), sem("v_ps"), sem("v")
        s_ps, mx_done, ex_done, et_ps, eta_done, etb_done, pv_ps = (
            sem(x) for x in ("s_ps", "mx", "ex", "et_ps", "eta", "etb", "pv_ps"))
        rd_done, att_done, wo_ps, res_done = sem("rd"), sem("att"), sem("wo_ps"), sem("res")
        bn2_done, mv2_done, ve2_done, rs2_done, n2_done, rows_done = (
            sem(x) for x in ("bn2", "mv2", "ve2", "rs2", "n2", "rows"))
        x2_ps, x2_done, lg_ps, lg_done = sem("x2_ps"), sem("x2"), sem("lg_ps"), sem("lg")
        top_done, topi_done, step, el_done, ohs_done, cum_ps, cb_done, slot_done = (
            sem(x) for x in ("top", "topi", "step", "el", "ohs", "cum_ps", "cb", "slot"))
        scattered = [sem(f"scattered{i}") for i in range(2)]
        LOADS = 5
        PAIR0 = 3
        STEPS = 12

        with nc.Block() as block:
            @block.sync
            def _(sp):
                for dst, src in ((wq, "wq"), (wk, "wk"), (wv, "wv"), (wo, "wo"), (wr, "wr")):
                    sp.dma_start(dst[:], ins[src]).then_inc(loaded, 16)
                sp.wait_ge(loaded, 16 * LOADS)

            @block.gpsimd
            def _(pool):
                made_n = [0]

                def make(ins_):
                    ins_.then_inc(made, 1)
                    made_n[0] += 1

                nc_g = nc.gpsimd
                make(nc_g.memset(hm_tmp[:], 1.0))
                make(nc_g.memset(before_f[:], 1.0))
                make(nc_g.memset(ones[:], 1.0))
                make(nc_g.memset(onespad[:], 0.0))
                make(nc_g.iota(iota_e[:], pattern=[[1, E]], base=0, channel_multiplier=0))
                make(nc_g.iota(payload[:].rearrange("p s k -> p (s k)"), pattern=[[2 * P, SEQS], [1, 2]], base=0,
                               channel_multiplier=2))
                for b in range(2):
                    make(nc_g.memset(rows[b][:], 0.0))
                    make(nc_g.memset(vpad[b][:], 0.0))
                make(nc_g.memset(base[:], 0.0))
                pool.wait_ge(made, made_n[0])
                make(nc_g.affine_select(out=hm_tmp[:], in_=hm_tmp[:], compare_op=ALU.is_ge, fill=0.0, base=0,
                                        pattern=[[-DH, HEADS]], channel_multiplier=1))
                make(nc_g.affine_select(out=before_f[:], in_=before_f[:], compare_op=ALU.is_gt, fill=0.0, base=0,
                                        pattern=[[1, P]], channel_multiplier=-1))
                make(nc_g.tensor_copy(iota_f[:], iota_e[:]))
                make(nc_g.memset(onespad[:, 0, 0:16], 1.0))
                make(nc_g.memset(onespad[:, 1, 16:32], 1.0))
                pool.wait_ge(made, made_n[0])
                make(nc_g.affine_select(out=headmask[:], in_=hm_tmp[:], compare_op=ALU.is_ge, fill=0.0, base=DH - 1,
                                        pattern=[[DH, HEADS]], channel_multiplier=-1))
                make(nc_g.tensor_copy(before[:], before_f[:]))
                pool.wait_ge(made, made_n[0])
                s.made2 = made_n[0]

                def body(i, pair, par, on):
                    if on(4):
                        r, c = i - 4, par
                        pool.wait_ge(mv2_done, G * r + G)
                        after(pool, rs2_done, r)
                        settle(pool, s)
                        nc_g.tensor_scalar(ve2[:], mv2[:, :, 1], EPS, None, ALU.add).then_inc(ve2_done, 1)
                        pool.wait_ge(ve2_done, r + 1)
                        after(pool, n2_done, r)
                        settle(pool, s)
                        nc_g.tensor_tensor(rs2[:], ve2[:], s.expo[:, 0:G], ALU.pow).then_inc(rs2_done, 1)
                    if on(1):
                        m, d = i - 1, 1 - par
                        pool.wait_ge(mv_done, G * m + G)
                        after(pool, n_done, m - 1)
                        after(pool, rs_done, m)
                        settle(pool, s)
                        nc_g.tensor_scalar(ve[:, 0, :], mv[d][:, :, 1], EPS, None, ALU.add).then_inc(ve_done, 1)
                        nc_g.tensor_scalar(ve[:, 1, :], mv[d][:, :, 1], 1.0 + EPS, EPS * EPS,
                                           ALU.mult, ALU.add).then_inc(ve_done, 1)
                        pool.wait_ge(ve_done, 2 * m + 2)
                        settle(pool, s)
                        nc_g.tensor_tensor(rs[d][:].rearrange("p a t -> p (a t)"), ve[:].rearrange("p a t -> p (a t)"),
                                           s.expo[:], ALU.pow).then_inc(rs_done, 1)
                    if on(2):
                        g, b = i - 2, par
                        pool.wait_ge(rs_done, g + 1)
                        after(pool, res_done, g - 1)
                        settle(pool, s)
                        nc_g.tensor_copy(nn[b][:], s.h[:, bass.ds(g * G, G), :]).then_inc(copy_done, 1)
                        pool.wait_ge(copy_done, g + 1)
                        settle(pool, s)
                        for t in range(G):
                            last = nc_g.tensor_scalar(nn[b][:, t, :], nn[b][:, t, :],
                                                      mv[b][:, t, 0:1], rs[b][:, 0, t:t + 1], ALU.subtract, ALU.mult)
                        last.then_inc(nn_done, 1)
                    if on(4):
                        r, c = i - 4, par
                        pool.wait_ge(res_done, r + 1)
                        settle(pool, s)
                        hs = s.h[:, bass.ds(r * G, G), :]
                        nc_g.tensor_tensor(hs, xa[c][:], hs, ALU.add).then_inc(sum_done, 1)
                    if on(4):
                        r, c = i - 4, par
                        pool.wait_ge(n2_done, r + 1)
                        settle(pool, s)
                        nc_g.tensor_copy(rows[c][:, :, 1, 0:P], rows[c][:, :, 0, 0:P]).then_inc(rows_done, 1)
                        nc_g.tensor_copy(rows[c][:, :, :, P:P + 1].bitcast(I32).rearrange("p t k a -> p t (k a)"),
                                         payload[:, bass.ds(r * G, G), :]).then_inc(rows_done, 1)
                    if on(5):
                        r, d = i - 5, 1 - par
                        pool.wait_ge(slot_done, r + 1)
                        pool.wait_ge(rows_done, 2 * r + 2)
                        settle(pool, s)
                        for t in range(G):
                            for kk in range(2):
                                nc_g.indirect_dma_start(
                                    ins["slots"], bass.IndirectOffsetOnAxis(ap=sidx[d][:, 2 * t + kk:2 * t + kk + 1], axis=0),
                                    rows[d][:, t, kk, :], None, bounds_check=SLOTS - 1,
                                    oob_is_err=False).then_inc(scattered[d], 16)
                    if on(2):
                        g, b = i - 2, par
                        pool.wait_ge(k_done, g + 1)
                        after(pool, s_ps, G * (g - 1))
                        settle(pool, s)
                        for hd in range(HEADS):
                            last = nc_g.tensor_scalar(km[b][:, hd, :], k[:], headmask[:, hd:hd + 1], None, ALU.mult)
                        last.then_inc(km_done, 1)

                pipelined(pool, body, 5, PAIR0)
                for b in range(2):
                    pool.wait_ge(scattered[b], 16 * 2 * G * (GROUPS // 2))

            @block.tensor
            def _(pe):
                pe.wait_ge(loaded, 16 * LOADS)
                pe.wait_ge(made, s.made2)

                def body(i, pair, par, on):
                    g, b = i - 2, par
                    w, c = i - 3, 1 - par
                    r = i - 4

                    def scores(t):
                        pe.wait_ge(km_done, w + 1)
                        after(pe, ex_done, G * w + t)
                        for half in range(2):
                            last = nc.tensor.matmul(p_s[:, half * 512:(half + 1) * 512], q[c][:, t * P:(t + 1) * P],
                                                    km[c][:, 4 * half:4 * half + 4, t * P:(t + 1) * P],
                                                    start=True, stop=True)
                        last.then_inc(s_ps, 1)

                    def turn(t):
                        pe.wait_ge(ex_done, G * w + t + 1)
                        after(pe, eta_done, G * w + t)
                        after(pe, etb_done, G * w + t)
                        for hd in range(HEADS):
                            last = nc.tensor.transpose(p_t[:, hd * P:(hd + 1) * P], ex[t % 2][:, hd, :], s.ident[:])
                        last.then_inc(et_ps, 1)

                    def weigh(t):
                        pe.wait_ge(eta_done, G * w + t + 1)
                        pe.wait_ge(etb_done, G * w + t + 1)
                        if t == 0:
                            after(pe, att_done, w)
                        for dst, is_v in ((p_o, True), (p_d, False)):
                            for gr in range(4):
                                for hp in range(2):
                                    lhs = vpad[c][:, t * 4 + gr, hp, :] if is_v else onespad[:, hp, :]
                                    last = nc.tensor.matmul(dst[32 * gr:32 * gr + 32, t * P:(t + 1) * P], lhs,
                                                            et[t % 2][:, 2 * gr + hp, :], start=(hp == 0), stop=(hp == 1))
                        last.then_inc(pv_ps, 1)

                    if on(2):
                        pe.wait_ge(n_done, g + 1)
                        after(pe, res_done, g - 1)
                        for t in range(G):
                            last = nc.tensor.transpose(b_y[:, t * P:(t + 1) * P], n[b][:, t, :], s.ident[:])
                        last.then_inc(nt_ps, 1)
                    if on(3):
                        scores(0)
                    if on(4):
                        pe.wait_ge(n2_done, r + 1)
                        after(pe, cb_done, 2 * r)
                        for t in range(G):
                            last = nc.tensor.transpose(b_x[:, t * P:(t + 1) * P], rows[par][:, t, 0, 0:P], s.ident[:])
                        last.then_inc(x2_ps, 1)
                    if on(2):
                        pe.wait_ge(xt_done, g + 1)
                        nc.tensor.matmul(b_y[:], wq[:], xt[:], start=True, stop=True).then_inc(q_ps, 1)
                    if on(3):
                        scores(1)
                        turn(0)
                    if on(2):
                        if on(4):
                            pe.wait_ge(x2_done, r + 1)
                        nc.tensor.matmul(b_x[:], wk[:], xt[:], start=True, stop=True).then_inc(k_ps, 1)
                    if on(3):
                        weigh(0)
                        scores(2)
                        turn(1)
                    if on(4):
                        pe.wait_ge(x2_done, r + 1)
                        after(pe, res_done, w)
                        if on(2):
                            pe.wait_ge(q_done, g + 1)
                        for t in range(G):
                            last = nc.tensor.matmul(b_y[:, t * E:(t + 1) * E], x2t[:, t * P:(t + 1) * P], wr[:],
                                                    start=True, stop=True)
                        last.then_inc(lg_ps, 1)
                    if on(3):
                        weigh(1)
                        scores(3)
                    if on(2):
                        pe.wait_ge(k_done, g + 1)
                        for t in range(G):
                            last = nc.tensor.matmul(b_x[:, t * P:(t + 1) * P], xt[:, t * P:(t + 1) * P], wv[:],
                                                    start=True, stop=True)
                        last.then_inc(v_ps, 1)
                    if on(3):
                        turn(2)
                        weigh(2)
                    if on(4):
                        pe.wait_ge(ohs_done, r + 1)
                        if on(2):
                            pe.wait_ge(v_done, 2 * g + 2)
                        nc.tensor.matmul(b_x[:, 0:G * E], before[:], ohs[:], start=True, stop=False, skip_group_check=True)
                        for t in range(G):
                            last = nc.tensor.matmul(
                                b_x[:, (t + 1) * E:(G + 1) * E].rearrange("p (t e) -> p t e", e=E), ones[:],
                                ohs[:, t:t + 1, :].to_broadcast([P, G - t, E]), start=False, stop=(t == G - 1),
                                skip_group_check=True)
                        last.then_inc(cum_ps, 1)
                    if on(3):
                        turn(3)
                        weigh(3)
                        pe.wait_ge(att_done, w + 1)
                        if on(2):
                            pe.wait_ge(q_done, g + 1)
                        if on(4):
                            pe.wait_ge(lg_done, r + 1)
                        for t in range(G):
                            last = nc.tensor.matmul(b_y[:, t * P:(t + 1) * P], att[:, t * P:(t + 1) * P], wo[:],
                                                    start=True, stop=True)
                        last.then_inc(wo_ps, 1)

                pipelined(pe, body, 4, PAIR0)

            @block.scalar
            def _(act):
                def body(i, pair, par, on):
                    g, b = i - 2, par
                    w, c = i - 3, 1 - par
                    r = i - 4

                    def exps(t):
                        act.wait_ge(mx_done, G * w + t + 1)
                        after(act, et_ps, G * w + t - 1)
                        for hd in range(HEADS):
                            last = nc.scalar.activation(ex[t % 2][:, hd, :], p_s[:, hd * P:(hd + 1) * P], ACT.Exp,
                                                        bias=mx[t % 2][:, hd:hd + 1])
                        last.then_inc(ex_done, 1)

                    def eta(t):
                        act.wait_ge(et_ps, G * w + t + 1)
                        after(act, pv_ps, G * w + t - 1)
                        nc.scalar.copy(et[t % 2][:, 0:4, :], p_t[:, 0:512].rearrange("p (h n) -> p h n", h=4)).then_inc(eta_done, 1)

                    if on(2):
                        act.wait_ge(nt_ps, g + 1)
                        after(act, v_ps, g)
                        nc.scalar.activation(xt[:], b_y[:], ACT.Identity, bias=s.vec[:, C_L1B:C_L1B + 1],
                                             scale=s.vec[:, C_L1G:C_L1G + 1]).then_inc(xt_done, 1)
                    if on(3):
                        exps(0)
                    if on(4):
                        act.wait_ge(x2_ps, r + 1)
                        after(act, lg_ps, r)
                        nc.scalar.activation(x2t[:], b_x[:], ACT.Identity, bias=s.vec[:, C_L2B:C_L2B + 1],
                                             scale=s.vec[:, C_L2G:C_L2G + 1]).then_inc(x2_done, 1)
                    if on(2):
                        act.wait_ge(q_ps, g + 1)
                        after(act, s_ps, G * (g - 1))
                        nc.scalar.activation(q[b][:], b_y[:], ACT.Copy, scale=float(DH) ** -0.5).then_inc(q_done, 1)
                    if on(3):
                        exps(1)
                        eta(0)
                    if on(2):
                        act.wait_ge(k_ps, g + 1)
                        after(act, km_done, g)
                        nc.scalar.copy(k[:], b_x[:]).then_inc(k_done, 1)
                    if on(3):
                        exps(2)
                        eta(1)
                    if on(4):
                        act.wait_ge(step, STEPS * r + 2)
                        nc.scalar.activation(el[:], dl[:], ACT.Exp).then_inc(el_done, 1)
                    if on(3):
                        exps(3)
                        eta(2)
                        eta(3)

                pipelined(act, body, 4, PAIR0)

            @block.vector
            def _(dve):
                V = nc.vector
                dve.wait_ge(made, s.made2)

                def stats(src, bnb, mvb, bn_sem, mv_sem, k0):
                    after(dve, mv_sem, G * k0)
                    settle(dve, s)
                    for t in range(G):
                        V.bn_stats(bnb[:, t, :], src(t)).then_inc(bn_sem, 1)
                    for t in range(G):
                        dve.wait_ge(bn_sem, G * k0 + t + 1)
                        settle(dve, s)
                        V.bn_aggr(mvb[:, t, :], bnb[:, t, :]).then_inc(mv_sem, 1)

                def body(i, pair, par, on):
                    g, b = i - 2, par
                    w, c = i - 3, 1 - par
                    r = i - 4

                    def maxes(t):
                        dve.wait_ge(s_ps, G * w + t + 1)
                        after(dve, ex_done, G * w + t - 1)
                        V.tensor_reduce(mx[t % 2][:], p_s[:].rearrange("p (h n) -> p h n", h=HEADS), AX, ALU.max,
                                        negate=True).then_inc(mx_done, 1)

                    def etb(t):
                        dve.wait_ge(et_ps, G * w + t + 1)
                        after(dve, pv_ps, G * w + t - 1)
                        V.tensor_copy(et[t % 2][:, 4:8, :], p_t[:, 512:1024].rearrange("p (h n) -> p h n", h=4)).then_inc(etb_done, 1)

                    count = [0]

                    def stepped(ins_):
                        count[0] += 1
                        ins_.then_inc(step, 1)

                    def steps_done():
                        dve.wait_ge(step, STEPS * r + count[0])

                    if on(4):
                        dve.wait_ge(rs2_done, r + 1)
                        if on(6):
                            dve.wait_ge(scattered[par], (pair - 2) * (16 * 2 * G))
                        for t in range(G):
                            last = V.tensor_scalar(rows[par][:, t, 0, 0:P], xa[par][:, t, :],
                                                   mv2[:, t, 0:1], rs2[:, t:t + 1], ALU.subtract, ALU.mult)
                        last.then_inc(n2_done, 1)
                    if on(3):
                        maxes(0)
                        maxes(1)
                        etb(0)
                        maxes(2)
                    if on(4):
                        dve.wait_ge(lg_ps, r + 1)
                        after(dve, topi_done, G * r)
                        V.tensor_copy(lg[:], b_y[:, 0:G * E].rearrange("p (t e) -> p t e", e=E)).then_inc(lg_done, 1)
                        dve.wait_ge(lg_done, r + 1)
                        settle(dve, s)
                        for t in range(G):
                            V.max(top[:, t, :], lg[:, t, :]).then_inc(top_done, 1)
                        for t in range(G):
                            dve.wait_ge(top_done, G * r + t + 1)
                            settle(dve, s)
                            V.max_index(topi[:, t, :], top[:, t, :], lg[:, t, :]).then_inc(topi_done, 1)
                        dve.wait_ge(topi_done, G * r + G)
                        stepped(V.tensor_copy(ixf[:], topi[:, :, 0:2]))
                        after(dve, el_done, r)
                        stepped(V.tensor_tensor(dl[:], top[:, :, 1], top[:, :, 0], ALU.subtract))
                        steps_done()
                        stepped(V.tensor_tensor(
                            oh[:], iota_f[:].rearrange("p (a e) -> p a e", a=1).to_broadcast([P, G * 2, E]),
                            ixf[:].rearrange("p t (k a) -> p (t k) a", a=1).to_broadcast([P, G * 2, E]), ALU.is_equal))
                        steps_done()
                        o2 = oh[:].rearrange("p (t k) e -> p t k e", k=2)
                        after(dve, cum_ps, r)
                        V.tensor_tensor(ohs[:], o2[:, :, 0, :], o2[:, :, 1, :], ALU.add).then_inc(ohs_done, 1)
                    if on(3):
                        etb(1)
                        maxes(3)
                    if on(2):
                        dve.wait_ge(v_ps, g + 1)
                        after(dve, pv_ps, G * (g - 1))
                        for hp in range(2):
                            V.tensor_copy(vpad[b][:, :, hp, 16 * hp:16 * hp + 16],
                                          b_x[:].rearrange("p (a k d) -> p a k d", k=2, d=DH)[:, :, hp, :]).then_inc(v_done, 1)
                    if on(3):
                        etb(2)
                    if on(4):
                        dve.wait_ge(cum_ps, r + 1)
                        V.tensor_tensor(cb[:], b_x[:, 0:G * E].rearrange("p (t e) -> p t e", e=E),
                                        base[:].rearrange("p (a e) -> p a e", a=1).to_broadcast([P, G, E]),
                                        ALU.add).then_inc(cb_done, 1)
                        dve.wait_ge(cb_done, 2 * r + 1)
                        V.tensor_tensor(base[:], b_x[:, G * E:(G + 1) * E], base[:], ALU.add).then_inc(cb_done, 1)
                        dve.wait_ge(cb_done, 2 * r + 2)
                        stepped(V.tensor_tensor(
                            pm[:].rearrange("p (t k) e -> p t k e", k=2), o2,
                            cb[:].rearrange("p t (a e) -> p t a e", a=1).to_broadcast([P, G, 2, E]), ALU.mult))
                        steps_done()
                        stepped(V.tensor_reduce(pos[:], pm[:], AX, ALU.add))
                        steps_done()
                        stepped(V.tensor_scalar(keep[:], pos[:], float(CAP), None, ALU.is_lt))
                        stepped(V.scalar_tensor_tensor(slot[:], ixf[:].rearrange("p t k -> p (t k)"), float(CAP), pos[:],
                                                       ALU.mult, ALU.add))
                        steps_done()
                        stepped(V.tensor_scalar(far[:], keep[:], -float(NOWHERE), float(NOWHERE), ALU.mult, ALU.add))
                        steps_done()
                        V.tensor_tensor(sidx[par][:], slot[:], far[:], ALU.add).then_inc(slot_done, 1)
                        dve.wait_ge(el_done, r + 1)
                        stepped(V.tensor_scalar(gs[:], el[:], 1.0, None, ALU.add))
                        steps_done()
                        stepped(V.reciprocal(gg[:, :, 0], gs[:]))
                        steps_done()
                        stepped(V.tensor_tensor(gg[:, :, 1], gg[:, :, 0], el[:], ALU.mult))
                        steps_done()
                        stepped(V.tensor_tensor(s.gates[:, bass.ds(r * G, G), :], gg[:],
                                                keep[:].rearrange("p (t k) -> p t k", k=2), ALU.mult))
                    if on(3):
                        etb(3)
                        dve.wait_ge(pv_ps, G * w + G)
                        V.reciprocal(rden[:], p_d[:]).then_inc(rd_done, 1)
                        dve.wait_ge(rd_done, w + 1)
                        after(dve, wo_ps, w)
                        V.tensor_tensor(att[:], p_o[:], rden[:], ALU.mult).then_inc(att_done, 1)
                        dve.wait_ge(wo_ps, w + 1)
                        dve.wait_ge(nn_done, w + 1)
                        after(dve, n2_done, w - 1)
                        after(dve, sum_done, w - 1)
                        V.tensor_tensor(xa[c][:], b_y[:].rearrange("p (t n) -> p t n", t=G), nn[c][:], ALU.add).then_inc(res_done, 1)
                        dve.wait_ge(res_done, w + 1)
                        after(dve, ve2_done, w)
                        settle(dve, s)
                        stats(lambda t: xa[c][:, t, :], bn2, mv2,
                              bn2_done, mv2_done, w)
                    if on(0):
                        after(dve, nn_done, i - 1)
                        settle(dve, s)
                        stats(lambda t: s.h[:, bass.ds(i * G + t, 1), :].rearrange("p a n -> p (a n)"), bn, mv[par],
                              bn_done, mv_done, i)
                    if on(1):
                        m, d = i - 1, 1 - par
                        dve.wait_ge(rs_done, m + 1)
                        after(dve, nt_ps, m - 1)
                        for t in range(G):
                            last = V.tensor_scalar(n[d][:, t, :], s.h[:, bass.ds(m * G + t, 1), :].rearrange("p a n -> p (a n)"),
                                                   mv[d][:, t, 0:1], rs[d][:, 1, t:t + 1], ALU.subtract, ALU.mult)
                        last.then_inc(n_done, 1)

                pipelined(dve, body, 4, PAIR0)


def phase3(nc, s, ins):
    NU = E * UNITS
    with ExitStack() as ctx:
        def sb(name, shape, dt=F32):
            return ctx.enter_context(nc.sbuf_tensor("c_" + name, shape, dt))

        def sem(name):
            return ctx.enter_context(nc.semaphore("c_" + name))

        b1 = sb("b1", [P, E * FC])
        b2 = sb("b2", [P, E])
        w1 = [sb(f"w1_{i}", [P, FF]) for i in range(2)]
        w2 = [sb(f"w2_{i}", [P, FC, P]) for i in range(2)]
        xin = [sb(f"xin{i}", [P, G, ROW]) for i in range(4)]
        xt = [sb(f"xt{i}", [P, UNIT]) for i in range(2)]
        ht = [sb(f"ht{i}", [P, FC, UNIT]) for i in range(2)]
        yt = [sb(f"yt{i}", [P, UNIT]) for i in range(2)]
        y = [sb(f"y{i}", [P, G, P]) for i in range(2)]
        p_x, p_y, p_b = (ctx.enter_context(nc.psum_tensor(f"c_{x}", [P, 512], F32)) for x in ("px", "py", "pb"))
        p_h = [ctx.enter_context(nc.psum_tensor(f"c_ph{i}", [P, 512], F32)) for i in range(FC)]

        b_loaded = sem("b_loaded")
        w_loaded = [sem(f"w_loaded{i}") for i in range(2)]
        x_loaded = [sem(f"x_loaded{i}") for i in range(4)]
        x_ps, xt_done, h_ps, ht_done, y_ps, yt_done, b_ps, y_done = (
            sem(x) for x in ("x_ps", "xt", "h_ps", "ht", "y_ps", "yt", "b_ps", "y"))
        sent = [sem(f"sent{i}") for i in range(4)]

        def units(eng, body, lag, quads_from):
            for i in range(4 * quads_from):
                body(i, i // 4, i % 4, lambda l, i=i: 0 <= i - l)
            with eng.Fori(quads_from, NU // 4) as quad:
                for ph in range(4):
                    body(quad * 4 + ph, quad, ph, lambda l: True)
            for i in range(NU, NU + lag):
                body(i, i // 4, i % 4, lambda l, i=i: i - l < NU)

        QUAD0 = 2
        with nc.Block() as block:
            @block.sync
            def _(sp):
                sp.dma_start(b1[:], ins["b1"]).then_inc(b_loaded, 16)
                sp.dma_start(b2[:], ins["b2"]).then_inc(b_loaded, 16)

                def body(i, quad, ph, on):
                    if not on(0):
                        return
                    if ph % UNITS == 0:
                        e, ep = quad * 2 + ph // UNITS, ph // UNITS
                        after(sp, y_ps, i - 2)
                        sp.dma_start(w1[ep][:], ins["w1"][bass.ds(e, 1)].rearrange("a p f -> p (a f)")).then_inc(w_loaded[ep], 16)
                        sp.dma_start(w2[ep][:], ins["w2"][bass.ds(e, 1)].rearrange("a (p c) n -> p (a c) n", c=FC)
                                     ).then_inc(w_loaded[ep], 16)
                    after(sp, sent[ph], 16 * G * quad)
                    sp.dma_start(xin[ph][:], ins["slots"][bass.ds(i * UNIT, UNIT)].rearrange("(t p) n -> p t n", p=P)
                                 ).then_inc(x_loaded[ph], 16)

                units(sp, body, 0, QUAD0)

            @block.tensor
            def _(pe):
                def body(i, quad, ph, on):
                    if on(2):
                        j, b = i - 2, (ph - 2) % 4
                        pe.wait_ge(x_loaded[b], 16 * (quad + (ph - 2) // 4) + 16)
                        after(pe, xt_done, j)
                        for t in range(G):
                            last = nc.tensor.transpose(p_x[:, t * P:(t + 1) * P], xin[b][:, t, 0:P], s.ident[:])
                        last.then_inc(x_ps, 1)
                    if on(3):
                        j, b, ep = i - 3, (ph - 3) % 2, (ph - 3) // 2 % 2
                        pe.wait_ge(w_loaded[ep], 32 * ((quad * 2 + (ph - 3) // 2 - ep) // 2 + 1)
                                   if isinstance(quad, int) else 32 * (quad + ((ph - 3) // 2 - ep) // 2) + 32)
                        pe.wait_ge(xt_done, j + 1)
                        for ch in range(FC):
                            after(pe, ht_done, FC * (j - 1) + ch + 1)
                            nc.tensor.matmul(p_h[ch][:], w1[ep][:].rearrange("p (f c) -> p c f", c=FC)[:, ch, :],
                                             xt[b][:], start=True, stop=True).then_inc(h_ps, 1)
                    if on(5):
                        j, b = i - 5, (ph - 5) % 2
                        pe.wait_ge(yt_done, j + 1)
                        after(pe, y_done, j)
                        for t in range(G):
                            last = nc.tensor.transpose(p_b[:, t * P:(t + 1) * P], yt[b][:, t * P:(t + 1) * P], s.ident[:])
                        last.then_inc(b_ps, 1)
                    if on(4):
                        j, b, ep = i - 4, (ph - 4) % 2, (ph - 4) // 2 % 2
                        after(pe, yt_done, j)
                        for ch in range(FC):
                            pe.wait_ge(ht_done, FC * j + ch + 1)
                            last = nc.tensor.matmul(p_y[:], w2[ep][:, ch, :], ht[b][:, ch, :], start=(ch == 0),
                                                    stop=(ch == FC - 1))
                        last.then_inc(y_ps, 1)

                units(pe, body, 5, QUAD0)

            @block.scalar
            def _(act):
                act.wait_ge(b_loaded, 32)

                def body(i, quad, ph, on):
                    if on(3):
                        j, b, e = i - 3, (ph - 3) % 2, quad * 2 + (ph - 3) // 2
                        after(act, y_ps, j - 1)
                        for ch in range(FC):
                            act.wait_ge(h_ps, FC * j + ch + 1)
                            settle(act, s)
                            nc.scalar.activation(ht[b][:, ch, :], p_h[ch][:], ACT.Gelu_apprx_tanh,
                                                 bias=b1[:, bass.ds(e * FC + ch, 1)]).then_inc(ht_done, 1)

                units(act, body, 3, QUAD0)

            @block.vector
            def _(dve):
                dve.wait_ge(b_loaded, 32)

                def body(i, quad, ph, on):
                    if on(2):
                        j, b = i - 2, (ph - 2) % 2
                        dve.wait_ge(x_ps, j + 1)
                        after(dve, h_ps, FC * (j - 1))
                        nc.vector.tensor_scalar(xt[b][:], p_x[:], s.vec[:, C_L2G:C_L2G + 1], s.vec[:, C_L2B:C_L2B + 1],
                                                ALU.mult, ALU.add).then_inc(xt_done, 1)
                    if on(4):
                        j, b, e = i - 4, (ph - 4) % 2, quad * 2 + (ph - 4) // 2
                        dve.wait_ge(y_ps, j + 1)
                        after(dve, b_ps, j - 1)
                        nc.vector.tensor_scalar(yt[b][:], p_y[:], b2[:, bass.ds(e, 1)], None, ALU.add).then_inc(yt_done, 1)
                    if on(5):
                        j, b = i - 5, (ph - 5) % 2
                        dve.wait_ge(b_ps, j + 1)
                        if on(7):
                            back = (ph - 7) % 4
                            after(dve, sent[back], 16 * G * (quad + (ph - 7) // 4 + 1))
                        nc.vector.tensor_copy(y[b][:], p_b[:].rearrange("p (t n) -> p t n", t=G)).then_inc(y_done, 1)

                units(dve, body, 5, QUAD0)

            @block.gpsimd
            def _(pool):
                def body(i, quad, ph, on):
                    if on(5):
                        j, b, x = i - 5, (ph - 5) % 2, (ph - 5) % 4
                        pool.wait_ge(y_done, j + 1)
                        settle(pool, s)
                        for t in range(G):
                            nc.gpsimd.indirect_dma_start(
                                ins["back"], bass.IndirectOffsetOnAxis(ap=xin[x][:, t, P:P + 1].bitcast(I32), axis=0),
                                y[b][:, t, :], None, bounds_check=2 * TOKENS - 1, oob_is_err=False).then_inc(sent[x], 16)

                units(pool, body, 5, QUAD0)
                for x in range(4):
                    pool.wait_ge(sent[x], 16 * G * (NU // 4))


def phase4(nc, s, ins, out):
    with ExitStack() as ctx:
        def sb(name, shape, dt=F32):
            return ctx.enter_context(nc.sbuf_tensor("d_" + name, shape, dt))

        def sem(name):
            return ctx.enter_context(nc.semaphore("d_" + name))

        got = [sb(f"got{i}", [P, G, 2, P]) for i in range(2)]
        part = [sb(f"part{i}", [P, G, P]) for i in range(2)]
        res = [sb(f"res{i}", [P, G, P]) for i in range(2)]
        got_in = [sem(f"got_in{i}") for i in range(2)]
        part_done, res_done = sem("part"), sem("res")
        stored = [sem(f"stored{i}") for i in range(2)]
        with nc.Block() as block:
            @block.sync
            def _(sp):
                def body(i, pair, par, on):
                    after(sp, res_done, i - 1)
                    sp.dma_start(got[par][:], ins["back_tokens"][:, bass.ds(i * G, G)]).then_inc(got_in[par], 16)
                pipelined(sp, body, 0)

            @block.vector
            def _(dve):
                def body(i, pair, par, on):
                    dve.wait_ge(got_in[par], 16 * pair + 16)
                    after(dve, stored[par], 16 * pair)
                    for t in range(G):
                        last = nc.vector.scalar_tensor_tensor(
                            part[par][:, t, :], got[par][:, t, 0, :], s.gates[:, bass.ds(i * G + t, 1), 0],
                            s.h[:, bass.ds(i * G + t, 1), :].rearrange("p a n -> p (a n)"), ALU.mult, ALU.add)
                    last.then_inc(part_done, 1)
                    dve.wait_ge(part_done, i + 1)
                    for t in range(G):
                        last = nc.vector.scalar_tensor_tensor(
                            res[par][:, t, :], got[par][:, t, 1, :], s.gates[:, bass.ds(i * G + t, 1), 1],
                            part[par][:, t, :], ALU.mult, ALU.add)
                    last.then_inc(res_done, 1)
                pipelined(dve, body, 0)

            @block.scalar
            def _(act):
                def body(i, pair, par, on):
                    act.wait_ge(res_done, i + 1)
                    act.dma_start(out[:, bass.ds(i * G, G)], res[par][:]).then_inc(stored[par], 16)
                pipelined(act, body, 0)
                for b in range(2):
                    act.wait_ge(stored[b], 16 * (GROUPS // 2))


_DRAM = ["table", "ids", "vecs", "Wh", "bh", "Wqk", "Wo", "wq", "wk", "wv", "wo", "wr", "w1", "w2", "b1", "b2"]


def build(nc, ins, out):
    slots = nc.dram_tensor("slots", [SLOTS, ROW], F32).ap()
    back = nc.dram_tensor("back", [2 * TOKENS, P], F32).ap()
    ins["slots"] = slots
    ins["slot_parts"] = slots.rearrange("(a r) n -> a r n", r=8)
    ins["back"] = back
    ins["back_parts"] = back.rearrange("(a r) n -> a (r n)", r=BACK_PART // P)
    ins["back_tokens"] = back.rearrange("(s p k) n -> p s k n", p=P, k=2)
    s = Shared()
    with ExitStack() as ctx:
        constants(nc, ctx, s, ins)
        phase1(nc, s, ins)
        phase2(nc, s, ins)
        phase3(nc, s, ins)
        phase4(nc, s, ins, out.rearrange("s p n -> p s n"))


def kernel(**inputs):
    import concourse.bacc as bacc
    from concourse.bass_utils import run_bass_kernel_spmd

    a = {k: np.asarray(v) for k, v in inputs.items()}
    c = np.ascontiguousarray
    gamma, beta, bh = a["L0_attn_gamma"], a["L0_attn_beta"], a["L0_attn_bh"]
    arrays = {
        "table": c(a["L0_tok_conv_w"].transpose(1, 2, 0).reshape(VOCAB, TAPS * P)),
        "ids": c(a["x"].T),
        "vecs": c(np.stack([a["L0_attn_ln_g"], a["L0_attn_ln_b"], a["L0_attn_bqk"], gamma[0], gamma[1], beta[0],
                            beta[1], a["L0_attn_bo"], bh[2 * P:3 * P], bh[3 * P:4 * P], a["L0_ffn_ln1_g"],
                            a["L0_ffn_ln1_b"], a["L0_ffn_ln2_g"], a["L0_ffn_ln2_b"]], axis=1)),
        "Wh": c(a["L0_attn_Wh"]), "bh": c(bh.reshape(1, -1)), "Wqk": c(a["L0_attn_Wqk"]), "Wo": c(a["L0_attn_Wo"]),
        "wq": c(a["L0_ffn_wq"]), "wk": c(a["L0_ffn_wk"]), "wv": c(a["L0_ffn_wv"]), "wo": c(a["L0_ffn_wo"]),
        "wr": c(a["L0_ffn_wr"]), "w1": c(a["L0_ffn_w1"]), "w2": c(a["L0_ffn_w2"]),
        "b1": c(a["L0_ffn_b1"].reshape(E, P, FC).transpose(1, 0, 2).reshape(P, E * FC)),
        "b2": c(a["L0_ffn_b2"].T),
    }
    nc = bacc.Bacc("TRN2", target_bir_lowering=False, num_devices=1)
    ins = {k: nc.dram_tensor("in_" + k, arrays[k].shape, mybir.dt.from_np(arrays[k].dtype), kind="ExternalInput").ap()
           for k in _DRAM}
    out = nc.dram_tensor("out", [SEQS, P, P], F32, kind="ExternalOutput").ap()
    build(nc, ins, out)
    got = run_bass_kernel_spmd(nc, [{"in_" + k: arrays[k] for k in _DRAM}], core_ids=[0])
    return got.results[0]["out"]
```

```python
from contextlib import ExitStack

import numpy as np
import concourse.bass as bass
from concourse import mybir

F32 = mybir.dt.float32
BF16 = mybir.dt.bfloat16
I32 = mybir.dt.int32
U32 = mybir.dt.uint32
ALU = mybir.AluOpType
ACT = mybir.ActivationFunctionType
AX = mybir.AxisListType.X

P = 128
VOCAB = 8000
TAPS = 3
SEQS = 128
G = 4
GROUPS = SEQS // G
N = G * P
HEADS = 8
DH = P // HEADS
E = 64
FF = 512
FC = FF // P
TOKENS = SEQS * P
CAP = 2 * (TOKENS * 2 // E)
SLOTS = E * CAP
ROW = 132
EPS = 1e-5
BACK_PART = 2048
BACK_PARTS = TOKENS * 2 // BACK_PART
NOWHERE = 1 << 24
(C_LNG, C_LNB, C_BQK, C_GA0, C_GA1, C_BE0, C_BE1, C_BO, C_BG0, C_BG1,
 C_L1G, C_L1B, C_L2G, C_L2B) = range(14)
NVEC = 14


def after(eng, sem, value):
    if not isinstance(value, int) or value > 0:
        eng.wait_ge(sem, value)


def pipelined(eng, body, lag, pairs_from=2):
    for i in range(2 * pairs_from):
        body(i, i // 2, i % 2, lambda l, i=i: 0 <= i - l)
    with eng.Fori(pairs_from, GROUPS // 2) as pair:
        for parity in range(2):
            body(pair * 2 + parity, pair, parity, lambda l: True)
    for i in range(GROUPS, GROUPS + lag):
        body(i, i // 2, i % 2, lambda l, i=i: i - l < GROUPS)


def settle(eng, s):
    eng.sem_inc(s.settled, 1)


class Shared:
    pass


def constants(nc, ctx, s, ins):
    def sb(name, shape, dt=F32):
        return ctx.enter_context(nc.sbuf_tensor(name, shape, dt))
    s.vec = sb("vec", [P, NVEC])
    s.ident = sb("ident", [P, P])
    s.h = sb("h_all", [P, SEQS, P])
    s.gates = sb("gates", [P, SEQS, 2])
    s.counts = sb("counts", [1, E], I32)
    s.expo = sb("expo", [P, 2 * G])
    const_ready = s.const_ready = ctx.enter_context(nc.semaphore("const_ready"))
    s.settled = ctx.enter_context(nc.semaphore("settled"))
    vec_loaded = ctx.enter_context(nc.semaphore("vec_loaded"))
    with nc.Block() as block:
        @block.sync
        def _(sp):
            sp.dma_start(s.vec[:], ins["vecs"]).then_inc(vec_loaded, 16)
            sp.wait_ge(vec_loaded, 16)

        @block.gpsimd
        def _(pool):
            nc.gpsimd.memset(s.ident[:], 1.0).then_inc(const_ready, 1)
            nc.gpsimd.memset(s.expo[:], -0.5).then_inc(const_ready, 1)
            pool.wait_ge(const_ready, 2)
            nc.gpsimd.affine_select(out=s.ident[:], in_=s.ident[:], compare_op=ALU.is_equal, fill=0.0,
                                    base=0, pattern=[[-1, P]], channel_multiplier=1).then_inc(const_ready, 1)
            pool.wait_ge(const_ready, 3)


def phase1(nc, s, ins):
    with ExitStack() as ctx:
        def sb(name, shape, dt=F32):
            return ctx.enter_context(nc.sbuf_tensor("a_" + name, shape, dt))

        def sem(name):
            return ctx.enter_context(nc.semaphore("a_" + name))

        ids = sb("ids", [P, SEQS], I32)
        idx = [sb(f"idx{i}", [P, G], I32) for i in range(2)]
        emb = [sb(f"emb{i}", [P, G, TAPS * P]) for i in range(2)]
        wh = sb("wh", [P, 512])
        wqk = sb("wqk", [P, P])
        wo = sb("wo", [P, 2, P])
        bv = sb("bv", [P, 2 * P])
        down = sb("down", [P, P])
        up = sb("up", [P, P])
        zrow = sb("zrow", [P, 8, ROW])
        zm = sb("zm", [P, BACK_PART])
        h0 = [sb(f"h0_{i}", [P, G, P]) for i in range(2)]
        bn = sb("bn", [P, G, 6])
        mv = [sb(f"mv{i}", [P, G, 2]) for i in range(2)]
        ve = sb("ve", [P, 2, G])
        rs = [sb(f"rs{i}", [P, 2, G]) for i in range(2)]
        u = sb("u", [P, G, P])
        n = [sb(f"n{i}", [P, G, P]) for i in range(2)]
        nt = [sb(f"nt{i}", [P, N]) for i in range(2)]
        z = [sb(f"z{i}", [P, N]) for i in range(2)]
        q = [sb(f"q{i}", [P, N]) for i in range(2)]
        k = [sb(f"k{i}", [P, N]) for i in range(2)]
        gate = [sb(f"gate{i}", [P, 2, N]) for i in range(2)]
        vpre = sb("vpre", [P, G, 2 * P])
        v = [sb(f"v{i}", [P, G, 2 * P]) for i in range(2)]
        r = sb("r", [P, N])
        at = sb("at", [P, N])
        vg = sb("vg", [P, 2, N])
        ot = sb("ot", [P, N])
        bank = [ctx.enter_context(nc.psum_tensor(f"a_bank{i}", [P, 512], F32)) for i in range(8)]
        b_conv, b_n, b_x, b_y, b_s, b_vt0, b_vt1, b_ot = bank

        loaded, shift_made, zero_made, zeroed = sem("loaded"), sem("shift_made"), sem("zero_made"), sem("zeroed")
        idx_ready = sem("idx_ready")
        emb_in = [sem(f"emb_in{i}") for i in range(2)]
        conv_done, h0_done, bn_done, mv_done = sem("conv"), sem("h0"), sem("bn"), sem("mv")
        ve_done, rs_done, u_done, hu_done = sem("ve"), sem("rs"), sem("u"), sem("hu")
        n_done, nt_ps, nt_done = sem("n"), sem("nt_ps"), sem("nt")
        z_ps, g_ps, v_ps = sem("z_ps"), sem("g_ps"), sem("v_ps")
        z_done, g_done, vb_done, v_done, qk_done = sem("z"), sem("g"), sem("vb"), sem("v"), sem("qk")
        sim_ps, r_done, at_done, vt_ps, vg_done = sem("sim_ps"), sem("r"), sem("at"), sem("vt_ps"), sem("vg")
        ot_ps, ot_done, o_ps, h1_done = sem("ot_ps"), sem("ot"), sem("o_ps"), sem("h1")
        LOADS = 6

        with nc.Block() as block:
            @block.sync
            def _(sp):
                for dst, src in ((ids[:], ins["ids"]), (wqk[:], ins["Wqk"]), (wh[:], ins["Wh"]),
                                 (wo[:], ins["Wo"].rearrange("(c p) n -> p c n", p=P)),
                                 (bv[:], ins["bh"][:, 0:2 * P].to_broadcast([P, 2 * P]))):
                    sp.dma_start(dst, src).then_inc(loaded, 16)
                sp.wait_ge(zero_made, 3)
                with sp.Fori(0, E) as e:
                    sp.dma_start(ins["slot_parts"][bass.ds(e * P, P)], zrow[:]).then_inc(zeroed, 16)
                with sp.Fori(0, BACK_PARTS) as e:
                    sp.dma_start(ins["back_parts"][bass.ds(e * P, P)], zm[:]).then_inc(zeroed, 16)
                sp.wait_ge(zeroed, 16 * (E + BACK_PARTS))

            @block.gpsimd
            def _(pool):
                for m in (down, up):
                    nc.gpsimd.memset(m[:], 1.0).then_inc(shift_made, 1)
                pool.wait_ge(shift_made, 2)
                for m, way in ((down, 1), (up, -1)):
                    nc.gpsimd.affine_select(out=m[:], in_=m[:], compare_op=ALU.is_equal, fill=0.0, base=way,
                                            pattern=[[-1, P]], channel_multiplier=1).then_inc(shift_made, 1)
                pool.wait_ge(loaded, 16 * (LOADS - 1))

                def body(i, pair, par, on):
                    if on(0):
                        after(pool, conv_done, i - 1)
                        after(pool, h0_done, i - 1)
                        settle(pool, s)
                        nc.gpsimd.tensor_copy(idx[par][:], ids[:, bass.ds(i * G, G)]).then_inc(idx_ready, 1)
                        pool.wait_ge(idx_ready, i + 1)
                        settle(pool, s)
                        for t in range(G):
                            nc.gpsimd.indirect_dma_start(
                                emb[par][:, t, :], None, ins["table"],
                                bass.IndirectOffsetOnAxis(ap=idx[par][:, t:t + 1], axis=0),
                                bounds_check=VOCAB - 1, oob_is_err=False).then_inc(emb_in[par], 16)
                    if on(1):
                        g, b = i - 1, 1 - par
                        pool.wait_ge(mv_done, G * g + G)
                        after(pool, n_done, g - 1)
                        settle(pool, s)
                        nc.gpsimd.tensor_scalar(ve[:, 0, :], mv[b][:, :, 1], EPS, None, ALU.add).then_inc(ve_done, 1)
                        nc.gpsimd.tensor_scalar(ve[:, 1, :], mv[b][:, :, 1], 1.0 + EPS, EPS * EPS,
                                                ALU.mult, ALU.add).then_inc(ve_done, 1)
                        pool.wait_ge(ve_done, 2 * g + 2)
                        settle(pool, s)
                        nc.gpsimd.tensor_tensor(rs[b][:].rearrange("p a t -> p (a t)"),
                                                ve[:].rearrange("p a t -> p (a t)"), s.expo[:],
                                                ALU.pow).then_inc(rs_done, 1)
                        pool.wait_ge(rs_done, g + 1)
                        after(pool, hu_done, g)
                        settle(pool, s)
                        for t in range(G):
                            last = nc.gpsimd.tensor_scalar(u[:, t, :], h0[b][:, t, :], mv[b][:, t, 0:1],
                                                           rs[b][:, 0, t:t + 1], ALU.subtract, ALU.mult)
                        last.then_inc(u_done, 1)
                        pool.wait_ge(u_done, g + 1)
                        settle(pool, s)
                        nc.gpsimd.tensor_tensor(s.h[:, bass.ds(g * G, G), :], u[:], h0[b][:],
                                                ALU.add).then_inc(hu_done, 1)

                pipelined(pool, body, 1)

            @block.tensor
            def _(pe):
                pe.wait_ge(loaded, 16 * (LOADS - 1))
                pe.wait_ge(shift_made, 4)

                def body(i, pair, par, on):
                    g, b = i - 2, par
                    w, c = i - 3, 1 - par
                    if on(2):
                        pe.wait_ge(n_done, g + 1)
                        after(pe, nt_done, g)
                        for t in range(G):
                            last = nc.tensor.transpose(b_n[:, t * P:(t + 1) * P], n[b][:, t, :], s.ident[:])
                        last.then_inc(nt_ps, 1)
                    if on(3):
                        pe.wait_ge(qk_done, 2 * w + 2)
                        after(pe, h1_done, w)
                        for t in range(G):
                            sl = slice(t * P, (t + 1) * P)
                            last = nc.tensor.matmul(b_s[:, sl], k[c][:, sl], q[c][:, sl], start=True, stop=True)
                        last.then_inc(sim_ps, 1)
                    if on(2):
                        pe.wait_ge(nt_done, g + 1)
                        after(pe, vb_done, 2 * g)
                        nc.tensor.matmul(b_x[:], wqk[:], nt[b][:], start=True, stop=True).then_inc(z_ps, 1)
                        nc.tensor.matmul(b_y[:], wh[:, 2 * P:3 * P], nt[b][:], start=True, stop=True).then_inc(g_ps, 1)
                    if on(3):
                        pe.wait_ge(at_done, w + 1)
                        pe.wait_ge(v_done, 2 * w + 2)
                        after(pe, vg_done, 2 * w)
                        for ch, bk in enumerate((b_vt0, b_vt1)):
                            for t in range(G):
                                sl = slice(t * P, (t + 1) * P)
                                last = nc.tensor.matmul(bk[:, sl], v[c][:, t, ch * P:(ch + 1) * P], at[:, sl],
                                                        start=True, stop=True)
                            last.then_inc(vt_ps, 1)
                    if on(2):
                        pe.wait_ge(z_done, g + 1)
                        nc.tensor.matmul(b_x[:], wh[:, 3 * P:4 * P], nt[b][:], start=True, stop=True).then_inc(g_ps, 1)
                        for half, bk in enumerate((b_y, b_x)):
                            pe.wait_ge(g_done, 2 * g + 1 + half)
                            for j in range(2):
                                t = 2 * half + j
                                last = nc.tensor.matmul(bk[:, j * 256:(j + 1) * 256], nt[b][:, t * P:(t + 1) * P],
                                                        wh[:, 0:2 * P], start=True, stop=True)
                            last.then_inc(v_ps, 1)
                    if on(3):
                        pe.wait_ge(vg_done, 2 * w + 2)
                        after(pe, ot_done, w)
                        for ch in range(2):
                            last = nc.tensor.matmul(b_ot[:], wo[:, ch, :], vg[:, ch, :], start=(ch == 0), stop=(ch == 1))
                        last.then_inc(ot_ps, 1)
                    if on(0):
                        pe.wait_ge(emb_in[par], pair * 16 * G + 16 * G)
                        after(pe, h0_done, i)
                        nc.tensor.matmul(b_conv[:], down[:], emb[par][:, :, 0:P], start=True, stop=False)
                        nc.tensor.matmul(b_conv[:], up[:], emb[par][:, :, 2 * P:3 * P], start=False,
                                         stop=True).then_inc(conv_done, 1)
                    if on(3):
                        pe.wait_ge(ot_done, w + 1)
                        pe.wait_ge(r_done, w + 1)
                        for t in range(G):
                            last = nc.tensor.transpose(b_s[:, t * P:(t + 1) * P], ot[:, t * P:(t + 1) * P], s.ident[:])
                        last.then_inc(o_ps, 1)

                pipelined(pe, body, 3)

            @block.scalar
            def _(act):
                def body(i, pair, par, on):
                    g, b = i - 2, par
                    w, c = i - 3, 1 - par
                    if on(2):
                        act.wait_ge(z_ps, g + 1)
                        after(act, qk_done, 2 * (g - 1))
                        nc.scalar.activation(z[b][:], b_x[:], ACT.Silu, bias=s.vec[:, C_BQK:C_BQK + 1]).then_inc(z_done, 1)
                    if on(3):
                        act.wait_ge(r_done, w + 1)
                        after(act, vt_ps, 2 * w)
                        nc.scalar.activation(at[:], r[:], ACT.Square).then_inc(at_done, 1)
                    if on(2):
                        after(act, vg_done, 2 * (g - 1))
                        for ch, bk in enumerate((b_y, b_x)):
                            act.wait_ge(g_ps, 2 * g + 1 + ch)
                            nc.scalar.activation(gate[b][:, ch, :], bk[:], ACT.Silu,
                                                 bias=s.vec[:, C_BG0 + ch:C_BG0 + ch + 1]).then_inc(g_done, 1)
                        after(act, vt_ps, 2 * (g - 1))
                        for half in range(2):
                            act.wait_ge(vb_done, 2 * g + 1 + half)
                            nc.scalar.activation(v[b][:, 2 * half:2 * half + 2, :], vpre[:, 2 * half:2 * half + 2, :],
                                                 ACT.Silu).then_inc(v_done, 1)
                    if on(3):
                        act.wait_ge(ot_ps, w + 1)
                        after(act, o_ps, w)
                        nc.scalar.activation(ot[:], b_ot[:], ACT.Identity, bias=s.vec[:, C_BO:C_BO + 1]).then_inc(ot_done, 1)

                pipelined(act, body, 3)

            @block.vector
            def _(dve):
                nc.vector.memset(zrow[:], 0.0).then_inc(zero_made, 1)
                nc.vector.memset(zm[:], 0.0).then_inc(zero_made, 1)
                dve.wait_ge(zero_made, 1)
                nc.vector.memset(zrow[:, :, P:P + 1].bitcast(I32), NOWHERE).then_inc(zero_made, 1)
                dve.wait_ge(loaded, 16 * (LOADS - 1))

                def body(i, pair, par, on):
                    g, b = i - 2, par
                    w, c = i - 3, 1 - par
                    if on(2):
                        dve.wait_ge(nt_ps, g + 1)
                        after(dve, v_ps, 2 * (g - 1))
                        nc.vector.tensor_scalar(nt[b][:], b_n[:], s.vec[:, C_LNG:C_LNG + 1], s.vec[:, C_LNB:C_LNB + 1],
                                                ALU.mult, ALU.add).then_inc(nt_done, 1)
                    if on(3):
                        dve.wait_ge(sim_ps, w + 1)
                        after(dve, at_done, w)
                        nc.vector.tensor_scalar(r[:], b_s[:], 0.0, 1.0 / P, ALU.max, ALU.mult).then_inc(r_done, 1)
                    if on(2):
                        dve.wait_ge(z_done, g + 1)
                        after(dve, sim_ps, g - 1)
                        for dst, ga, be in ((q, C_GA0, C_BE0), (k, C_GA1, C_BE1)):
                            nc.vector.tensor_scalar(dst[b][:], z[b][:], s.vec[:, ga:ga + 1], s.vec[:, be:be + 1],
                                                    ALU.mult, ALU.add).then_inc(qk_done, 1)
                    if on(3):
                        after(dve, ot_ps, w)
                        for ch, bk in enumerate((b_vt0, b_vt1)):
                            dve.wait_ge(vt_ps, 2 * w + 1 + ch)
                            nc.vector.tensor_tensor(vg[:, ch, :], bk[:], gate[c][:, ch, :], ALU.mult).then_inc(vg_done, 1)
                    if on(2):
                        for half, bk in enumerate((b_y, b_x)):
                            dve.wait_ge(v_ps, 2 * g + 1 + half)
                            after(dve, v_done, 2 * (g - 1) + 1 + half)
                            nc.vector.tensor_tensor(
                                vpre[:, 2 * half:2 * half + 2, :], bk[:].rearrange("p (j n) -> p j n", j=2),
                                bv[:].rearrange("p (j n) -> p j n", j=1).to_broadcast([P, 2, 2 * P]),
                                ALU.add).then_inc(vb_done, 1)
                    if on(0):
                        dve.wait_ge(conv_done, i + 1)
                        after(dve, hu_done, i - 1)
                        nc.vector.tensor_tensor(h0[par][:], b_conv[:].rearrange("p (t n) -> p t n", t=G),
                                                emb[par][:, :, P:2 * P], ALU.add).then_inc(h0_done, 1)
                        dve.wait_ge(h0_done, i + 1)
                        after(dve, mv_done, G * i)
                        settle(dve, s)
                        for t in range(G):
                            nc.vector.bn_stats(bn[:, t, :], h0[par][:, t, :]).then_inc(bn_done, 1)
                        for t in range(G):
                            dve.wait_ge(bn_done, G * i + t + 1)
                            settle(dve, s)
                            nc.vector.bn_aggr(mv[par][:, t, :], bn[:, t, :]).then_inc(mv_done, 1)
                    if on(1):
                        m, d = i - 1, 1 - par
                        dve.wait_ge(rs_done, m + 1)
                        after(dve, nt_ps, m - 1)
                        for t in range(G):
                            last = nc.vector.tensor_scalar(n[d][:, t, :], h0[d][:, t, :], mv[d][:, t, 0:1],
                                                           rs[d][:, 1, t:t + 1], ALU.subtract, ALU.mult)
                        last.then_inc(n_done, 1)
                    if on(3):
                        dve.wait_ge(o_ps, w + 1)
                        dve.wait_ge(hu_done, w + 1)
                        hs = s.h[:, bass.ds(w * G, G), :]
                        nc.vector.tensor_tensor(hs, b_s[:].rearrange("p (t n) -> p t n", t=G), hs,
                                                ALU.add).then_inc(h1_done, 1)

                pipelined(dve, body, 3)


def phase2(nc, s, ins):
    with ExitStack() as ctx:
        def sb(name, shape, dt=F32):
            return ctx.enter_context(nc.sbuf_tensor("b_" + name, shape, dt))

        def two(name, shape, dt=F32):
            return [sb(f"{name}{i}", shape, dt) for i in range(2)]

        def sem(name):
            return ctx.enter_context(nc.semaphore("b_" + name))

        wq, wk, wv, wo = (sb(x, [P, P]) for x in ("wq", "wk", "wv", "wo"))
        wr = sb("wr", [P, E])
        headmask = sb("headmask", [P, HEADS])
        hm_tmp = sb("hm_tmp", [P, HEADS])
        iota_e = sb("iota_e", [P, E], I32)
        iota_f = sb("iota_f", [P, E])
        payload = sb("payload", [P, SEQS, 2], I32)
        before_f = sb("before_f", [P, P])
        before = sb("before", [P, P], BF16)
        ones = sb("ones", [P, P], BF16)
        onespad = sb("onespad", [P, 2, 32])
        bn = sb("bn", [P, G, 6])
        mv = two("mv", [P, G, 2])
        ve = sb("ve", [P, 2, G])
        rs = two("rs", [P, 2, G])
        nn = two("nn", [P, G, P])
        xa = two("xa", [P, G, P])
        n = two("n", [P, G, P])
        xt = sb("xt", [P, N])
        q = two("q", [P, N])
        k = sb("k", [P, N])
        km = two("km", [P, HEADS, N])
        vpad = two("vpad", [P, G * 4, 2, 32])
        mx = two("mx", [P, HEADS])
        ex = two("ex", [P, HEADS, P])
        et = two("et", [P, HEADS, P])
        rden = sb("rden", [P, N])
        att = sb("att", [P, N])
        bn2 = sb("bn2", [P, G, 6])
        mv2 = sb("mv2", [P, G, 2])
        ve2 = sb("ve2", [P, G])
        rs2 = sb("rs2", [P, G])
        rows = two("rows", [P, G, 2, ROW])
        x2t = sb("x2t", [P, N])
        lg = sb("lg", [P, G, E])
        top = sb("top", [P, G, 8])
        topi = sb("topi", [P, G, 8], U32)
        ixf = sb("ixf", [P, G, 2])
        dl = sb("dl", [P, G])
        el = sb("el", [P, G])
        oh = sb("oh", [P, G * 2, E])
        ohs = sb("ohs", [P, G, E], BF16)
        base = sb("base", [P, E])
        cb = sb("cb", [P, G, E])
        pm = sb("pm", [P, G * 2, E])
        pos = sb("pos", [P, G * 2])
        keep = sb("keep", [P, G * 2])
        far = sb("far", [P, G * 2])
        slot = sb("slot", [P, G * 2])
        sidx = two("sidx", [P, G * 2], I32)
        gs = sb("gs", [P, G])
        gg = sb("gg", [P, G, 2])
        p_o = ctx.enter_context(nc.psum_tensor("b_o", [P, 512], F32))
        p_d = ctx.enter_context(nc.psum_tensor("b_d", [P, 512], F32))
        b_x = ctx.enter_context(nc.psum_tensor("b_x", [P, 512], F32))
        b_y = ctx.enter_context(nc.psum_tensor("b_y", [P, 512], F32))
        p_s = ctx.enter_context(nc.psum_tensor("b_s", [P, 1024], F32))
        p_t = ctx.enter_context(nc.psum_tensor("b_t", [P, 1024], F32))

        loaded, made, filled = sem("loaded"), sem("made"), sem("filled")
        bn_done, mv_done, ve_done, rs_done, n_done = sem("bn"), sem("mv"), sem("ve"), sem("rs"), sem("n")
        copy_done, nn_done, sum_done = sem("copy"), sem("nn"), sem("sum")
        nt_ps, xt_done, q_ps, q_done, k_ps, k_done = (sem(x) for x in ("nt_ps", "xt", "q_ps", "q", "k_ps", "k"))
        km_done, v_ps, v_done = sem("km"), sem("v_ps"), sem("v")
        s_ps, mx_done, ex_done, et_ps, eta_done, etb_done, pv_ps = (
            sem(x) for x in ("s_ps", "mx", "ex", "et_ps", "eta", "etb", "pv_ps"))
        rd_done, att_done, wo_ps, res_done = sem("rd"), sem("att"), sem("wo_ps"), sem("res")
        bn2_done, mv2_done, ve2_done, rs2_done, n2_done, rows_done = (
            sem(x) for x in ("bn2", "mv2", "ve2", "rs2", "n2", "rows"))
        x2_ps, x2_done, lg_ps, lg_done = sem("x2_ps"), sem("x2"), sem("lg_ps"), sem("lg")
        top_done, topi_done, step, el_done, ohs_done, cum_ps, cb_done, slot_done = (
            sem(x) for x in ("top", "topi", "step", "el", "ohs", "cum_ps", "cb", "slot"))
        counted = sem("counted")
        scattered = [sem(f"scattered{i}") for i in range(2)]
        LOADS = 5
        PAIR0 = 3
        STEPS = 12

        with nc.Block() as block:
            @block.sync
            def _(sp):
                for dst, src in ((wq, "wq"), (wk, "wk"), (wv, "wv"), (wo, "wo"), (wr, "wr")):
                    sp.dma_start(dst[:], ins[src]).then_inc(loaded, 16)
                sp.wait_ge(loaded, 16 * LOADS)

            @block.gpsimd
            def _(pool):
                made_n = [0]

                def make(ins_):
                    ins_.then_inc(made, 1)
                    made_n[0] += 1

                nc_g = nc.gpsimd
                make(nc_g.memset(hm_tmp[:], 1.0))
                make(nc_g.memset(before_f[:], 1.0))
                make(nc_g.memset(ones[:], 1.0))
                make(nc_g.memset(onespad[:], 0.0))
                make(nc_g.iota(iota_e[:], pattern=[[1, E]], base=0, channel_multiplier=0))
                make(nc_g.iota(payload[:].rearrange("p s k -> p (s k)"), pattern=[[2 * P, SEQS], [1, 2]], base=0,
                               channel_multiplier=2))
                for b in range(2):
                    make(nc_g.memset(rows[b][:], 0.0))
                    make(nc_g.memset(vpad[b][:], 0.0))
                make(nc_g.memset(base[:], 0.0))
                pool.wait_ge(made, made_n[0])
                make(nc_g.affine_select(out=hm_tmp[:], in_=hm_tmp[:], compare_op=ALU.is_ge, fill=0.0, base=0,
                                        pattern=[[-DH, HEADS]], channel_multiplier=1))
                make(nc_g.affine_select(out=before_f[:], in_=before_f[:], compare_op=ALU.is_gt, fill=0.0, base=0,
                                        pattern=[[1, P]], channel_multiplier=-1))
                make(nc_g.tensor_copy(iota_f[:], iota_e[:]))
                make(nc_g.memset(onespad[:, 0, 0:16], 1.0))
                make(nc_g.memset(onespad[:, 1, 16:32], 1.0))
                pool.wait_ge(made, made_n[0])
                make(nc_g.affine_select(out=headmask[:], in_=hm_tmp[:], compare_op=ALU.is_ge, fill=0.0, base=DH - 1,
                                        pattern=[[DH, HEADS]], channel_multiplier=-1))
                make(nc_g.tensor_copy(before[:], before_f[:]))
                pool.wait_ge(made, made_n[0])
                s.made2 = made_n[0]

                def body(i, pair, par, on):
                    if on(4):
                        r, c = i - 4, par
                        pool.wait_ge(mv2_done, G * r + G)
                        after(pool, rs2_done, r)
                        settle(pool, s)
                        nc_g.tensor_scalar(ve2[:], mv2[:, :, 1], EPS, None, ALU.add).then_inc(ve2_done, 1)
                        pool.wait_ge(ve2_done, r + 1)
                        after(pool, n2_done, r)
                        settle(pool, s)
                        nc_g.tensor_tensor(rs2[:], ve2[:], s.expo[:, 0:G], ALU.pow).then_inc(rs2_done, 1)
                    if on(1):
                        m, d = i - 1, 1 - par
                        pool.wait_ge(mv_done, G * m + G)
                        after(pool, n_done, m - 1)
                        after(pool, rs_done, m)
                        settle(pool, s)
                        nc_g.tensor_scalar(ve[:, 0, :], mv[d][:, :, 1], EPS, None, ALU.add).then_inc(ve_done, 1)
                        nc_g.tensor_scalar(ve[:, 1, :], mv[d][:, :, 1], 1.0 + EPS, EPS * EPS,
                                           ALU.mult, ALU.add).then_inc(ve_done, 1)
                        pool.wait_ge(ve_done, 2 * m + 2)
                        settle(pool, s)
                        nc_g.tensor_tensor(rs[d][:].rearrange("p a t -> p (a t)"), ve[:].rearrange("p a t -> p (a t)"),
                                           s.expo[:], ALU.pow).then_inc(rs_done, 1)
                    if on(2):
                        g, b = i - 2, par
                        pool.wait_ge(rs_done, g + 1)
                        after(pool, res_done, g - 1)
                        settle(pool, s)
                        nc_g.tensor_copy(nn[b][:], s.h[:, bass.ds(g * G, G), :]).then_inc(copy_done, 1)
                        pool.wait_ge(copy_done, g + 1)
                        settle(pool, s)
                        for t in range(G):
                            last = nc_g.tensor_scalar(nn[b][:, t, :], nn[b][:, t, :],
                                                      mv[b][:, t, 0:1], rs[b][:, 0, t:t + 1], ALU.subtract, ALU.mult)
                        last.then_inc(nn_done, 1)
                    if on(4):
                        r, c = i - 4, par
                        pool.wait_ge(res_done, r + 1)
                        settle(pool, s)
                        hs = s.h[:, bass.ds(r * G, G), :]
                        nc_g.tensor_tensor(hs, xa[c][:], hs, ALU.add).then_inc(sum_done, 1)
                    if on(4):
                        r, c = i - 4, par
                        pool.wait_ge(n2_done, r + 1)
                        settle(pool, s)
                        nc_g.tensor_copy(rows[c][:, :, 1, 0:P], rows[c][:, :, 0, 0:P]).then_inc(rows_done, 1)
                        nc_g.tensor_copy(rows[c][:, :, :, P:P + 1].bitcast(I32).rearrange("p t k a -> p t (k a)"),
                                         payload[:, bass.ds(r * G, G), :]).then_inc(rows_done, 1)
                    if on(5):
                        r, d = i - 5, 1 - par
                        pool.wait_ge(slot_done, r + 1)
                        pool.wait_ge(rows_done, 2 * r + 2)
                        settle(pool, s)
                        for t in range(G):
                            for kk in range(2):
                                nc_g.indirect_dma_start(
                                    ins["slots"], bass.IndirectOffsetOnAxis(ap=sidx[d][:, 2 * t + kk:2 * t + kk + 1], axis=0),
                                    rows[d][:, t, kk, :], None, bounds_check=SLOTS - 1,
                                    oob_is_err=False).then_inc(scattered[d], 16)
                    if on(2):
                        g, b = i - 2, par
                        pool.wait_ge(k_done, g + 1)
                        after(pool, s_ps, G * (g - 1))
                        settle(pool, s)
                        for hd in range(HEADS):
                            last = nc_g.tensor_scalar(km[b][:, hd, :], k[:], headmask[:, hd:hd + 1], None, ALU.mult)
                        last.then_inc(km_done, 1)

                pipelined(pool, body, 5, PAIR0)
                for b in range(2):
                    pool.wait_ge(scattered[b], 16 * 2 * G * (GROUPS // 2))

            @block.tensor
            def _(pe):
                pe.wait_ge(loaded, 16 * LOADS)
                pe.wait_ge(made, s.made2)

                def body(i, pair, par, on):
                    g, b = i - 2, par
                    w, c = i - 3, 1 - par
                    r = i - 4

                    def scores(t):
                        pe.wait_ge(km_done, w + 1)
                        after(pe, ex_done, G * w + t)
                        for half in range(2):
                            last = nc.tensor.matmul(p_s[:, half * 512:(half + 1) * 512], q[c][:, t * P:(t + 1) * P],
                                                    km[c][:, 4 * half:4 * half + 4, t * P:(t + 1) * P],
                                                    start=True, stop=True)
                        last.then_inc(s_ps, 1)

                    def turn(t):
                        pe.wait_ge(ex_done, G * w + t + 1)
                        after(pe, eta_done, G * w + t)
                        after(pe, etb_done, G * w + t)
                        for hd in range(HEADS):
                            last = nc.tensor.transpose(p_t[:, hd * P:(hd + 1) * P], ex[t % 2][:, hd, :], s.ident[:])
                        last.then_inc(et_ps, 1)

                    def weigh(t):
                        pe.wait_ge(eta_done, G * w + t + 1)
                        pe.wait_ge(etb_done, G * w + t + 1)
                        if t == 0:
                            after(pe, att_done, w)
                        for dst, is_v in ((p_o, True), (p_d, False)):
                            for gr in range(4):
                                for hp in range(2):
                                    lhs = vpad[c][:, t * 4 + gr, hp, :] if is_v else onespad[:, hp, :]
                                    last = nc.tensor.matmul(dst[32 * gr:32 * gr + 32, t * P:(t + 1) * P], lhs,
                                                            et[t % 2][:, 2 * gr + hp, :], start=(hp == 0), stop=(hp == 1))
                        last.then_inc(pv_ps, 1)

                    if on(2):
                        pe.wait_ge(n_done, g + 1)
                        after(pe, res_done, g - 1)
                        for t in range(G):
                            last = nc.tensor.transpose(b_y[:, t * P:(t + 1) * P], n[b][:, t, :], s.ident[:])
                        last.then_inc(nt_ps, 1)
                    if on(3):
                        scores(0)
                    if on(4):
                        pe.wait_ge(n2_done, r + 1)
                        after(pe, cb_done, 2 * r)
                        for t in range(G):
                            last = nc.tensor.transpose(b_x[:, t * P:(t + 1) * P], rows[par][:, t, 0, 0:P], s.ident[:])
                        last.then_inc(x2_ps, 1)
                    if on(2):
                        pe.wait_ge(xt_done, g + 1)
                        nc.tensor.matmul(b_y[:], wq[:], xt[:], start=True, stop=True).then_inc(q_ps, 1)
                    if on(3):
                        scores(1)
                        turn(0)
                    if on(2):
                        if on(4):
                            pe.wait_ge(x2_done, r + 1)
                        nc.tensor.matmul(b_x[:], wk[:], xt[:], start=True, stop=True).then_inc(k_ps, 1)
                    if on(3):
                        weigh(0)
                        scores(2)
                        turn(1)
                    if on(4):
                        pe.wait_ge(x2_done, r + 1)
                        after(pe, res_done, w)
                        if on(2):
                            pe.wait_ge(q_done, g + 1)
                        for t in range(G):
                            last = nc.tensor.matmul(b_y[:, t * E:(t + 1) * E], x2t[:, t * P:(t + 1) * P], wr[:],
                                                    start=True, stop=True)
                        last.then_inc(lg_ps, 1)
                    if on(3):
                        weigh(1)
                        scores(3)
                    if on(2):
                        pe.wait_ge(k_done, g + 1)
                        for t in range(G):
                            last = nc.tensor.matmul(b_x[:, t * P:(t + 1) * P], xt[:, t * P:(t + 1) * P], wv[:],
                                                    start=True, stop=True)
                        last.then_inc(v_ps, 1)
                    if on(3):
                        turn(2)
                        weigh(2)
                    if on(4):
                        pe.wait_ge(ohs_done, r + 1)
                        if on(2):
                            pe.wait_ge(v_done, 2 * g + 2)
                        nc.tensor.matmul(b_x[:, 0:G * E], before[:], ohs[:], start=True, stop=False, skip_group_check=True)
                        for t in range(G):
                            last = nc.tensor.matmul(
                                b_x[:, (t + 1) * E:(G + 1) * E].rearrange("p (t e) -> p t e", e=E), ones[:],
                                ohs[:, t:t + 1, :].to_broadcast([P, G - t, E]), start=False, stop=(t == G - 1),
                                skip_group_check=True)
                        last.then_inc(cum_ps, 1)
                    if on(3):
                        turn(3)
                        weigh(3)
                        pe.wait_ge(att_done, w + 1)
                        if on(2):
                            pe.wait_ge(q_done, g + 1)
                        if on(4):
                            pe.wait_ge(lg_done, r + 1)
                        for t in range(G):
                            last = nc.tensor.matmul(b_y[:, t * P:(t + 1) * P], att[:, t * P:(t + 1) * P], wo[:],
                                                    start=True, stop=True)
                        last.then_inc(wo_ps, 1)

                pipelined(pe, body, 4, PAIR0)

            @block.scalar
            def _(act):
                def body(i, pair, par, on):
                    g, b = i - 2, par
                    w, c = i - 3, 1 - par
                    r = i - 4

                    def exps(t):
                        act.wait_ge(mx_done, G * w + t + 1)
                        after(act, et_ps, G * w + t - 1)
                        for hd in range(HEADS):
                            last = nc.scalar.activation(ex[t % 2][:, hd, :], p_s[:, hd * P:(hd + 1) * P], ACT.Exp,
                                                        bias=mx[t % 2][:, hd:hd + 1])
                        last.then_inc(ex_done, 1)

                    def eta(t):
                        act.wait_ge(et_ps, G * w + t + 1)
                        after(act, pv_ps, G * w + t - 1)
                        nc.scalar.copy(et[t % 2][:, 0:4, :], p_t[:, 0:512].rearrange("p (h n) -> p h n", h=4)).then_inc(eta_done, 1)

                    if on(2):
                        act.wait_ge(nt_ps, g + 1)
                        after(act, v_ps, g)
                        nc.scalar.activation(xt[:], b_y[:], ACT.Identity, bias=s.vec[:, C_L1B:C_L1B + 1],
                                             scale=s.vec[:, C_L1G:C_L1G + 1]).then_inc(xt_done, 1)
                    if on(3):
                        exps(0)
                    if on(4):
                        act.wait_ge(x2_ps, r + 1)
                        after(act, lg_ps, r)
                        nc.scalar.activation(x2t[:], b_x[:], ACT.Identity, bias=s.vec[:, C_L2B:C_L2B + 1],
                                             scale=s.vec[:, C_L2G:C_L2G + 1]).then_inc(x2_done, 1)
                    if on(2):
                        act.wait_ge(q_ps, g + 1)
                        after(act, s_ps, G * (g - 1))
                        nc.scalar.activation(q[b][:], b_y[:], ACT.Copy, scale=float(DH) ** -0.5).then_inc(q_done, 1)
                    if on(3):
                        exps(1)
                        eta(0)
                    if on(2):
                        act.wait_ge(k_ps, g + 1)
                        after(act, km_done, g)
                        nc.scalar.copy(k[:], b_x[:]).then_inc(k_done, 1)
                    if on(3):
                        exps(2)
                        eta(1)
                    if on(4):
                        act.wait_ge(step, STEPS * r + 2)
                        nc.scalar.activation(el[:], dl[:], ACT.Exp).then_inc(el_done, 1)
                    if on(3):
                        exps(3)
                        eta(2)
                        eta(3)

                pipelined(act, body, 4, PAIR0)

            @block.vector
            def _(dve):
                V = nc.vector
                dve.wait_ge(made, s.made2)

                def stats(src, bnb, mvb, bn_sem, mv_sem, k0):
                    after(dve, mv_sem, G * k0)
                    settle(dve, s)
                    for t in range(G):
                        V.bn_stats(bnb[:, t, :], src(t)).then_inc(bn_sem, 1)
                    for t in range(G):
                        dve.wait_ge(bn_sem, G * k0 + t + 1)
                        settle(dve, s)
                        V.bn_aggr(mvb[:, t, :], bnb[:, t, :]).then_inc(mv_sem, 1)

                def body(i, pair, par, on):
                    g, b = i - 2, par
                    w, c = i - 3, 1 - par
                    r = i - 4

                    def maxes(t):
                        dve.wait_ge(s_ps, G * w + t + 1)
                        after(dve, ex_done, G * w + t - 1)
                        V.tensor_reduce(mx[t % 2][:], p_s[:].rearrange("p (h n) -> p h n", h=HEADS), AX, ALU.max,
                                        negate=True).then_inc(mx_done, 1)

                    def etb(t):
                        dve.wait_ge(et_ps, G * w + t + 1)
                        after(dve, pv_ps, G * w + t - 1)
                        V.tensor_copy(et[t % 2][:, 4:8, :], p_t[:, 512:1024].rearrange("p (h n) -> p h n", h=4)).then_inc(etb_done, 1)

                    count = [0]

                    def stepped(ins_):
                        count[0] += 1
                        ins_.then_inc(step, 1)

                    def steps_done():
                        dve.wait_ge(step, STEPS * r + count[0])

                    if on(4):
                        dve.wait_ge(rs2_done, r + 1)
                        if on(6):
                            dve.wait_ge(scattered[par], (pair - 2) * (16 * 2 * G))
                        for t in range(G):
                            last = V.tensor_scalar(rows[par][:, t, 0, 0:P], xa[par][:, t, :],
                                                   mv2[:, t, 0:1], rs2[:, t:t + 1], ALU.subtract, ALU.mult)
                        last.then_inc(n2_done, 1)
                    if on(3):
                        maxes(0)
                        maxes(1)
                        etb(0)
                        maxes(2)
                    if on(4):
                        dve.wait_ge(lg_ps, r + 1)
                        after(dve, topi_done, G * r)
                        V.tensor_copy(lg[:], b_y[:, 0:G * E].rearrange("p (t e) -> p t e", e=E)).then_inc(lg_done, 1)
                        dve.wait_ge(lg_done, r + 1)
                        settle(dve, s)
                        for t in range(G):
                            V.max(top[:, t, :], lg[:, t, :]).then_inc(top_done, 1)
                        for t in range(G):
                            dve.wait_ge(top_done, G * r + t + 1)
                            settle(dve, s)
                            V.max_index(topi[:, t, :], top[:, t, :], lg[:, t, :]).then_inc(topi_done, 1)
                        dve.wait_ge(topi_done, G * r + G)
                        stepped(V.tensor_copy(ixf[:], topi[:, :, 0:2]))
                        after(dve, el_done, r)
                        stepped(V.tensor_tensor(dl[:], top[:, :, 1], top[:, :, 0], ALU.subtract))
                        steps_done()
                        stepped(V.tensor_tensor(
                            oh[:], iota_f[:].rearrange("p (a e) -> p a e", a=1).to_broadcast([P, G * 2, E]),
                            ixf[:].rearrange("p t (k a) -> p (t k) a", a=1).to_broadcast([P, G * 2, E]), ALU.is_equal))
                        steps_done()
                        o2 = oh[:].rearrange("p (t k) e -> p t k e", k=2)
                        after(dve, cum_ps, r)
                        V.tensor_tensor(ohs[:], o2[:, :, 0, :], o2[:, :, 1, :], ALU.add).then_inc(ohs_done, 1)
                    if on(3):
                        etb(1)
                        maxes(3)
                    if on(2):
                        dve.wait_ge(v_ps, g + 1)
                        after(dve, pv_ps, G * (g - 1))
                        for hp in range(2):
                            V.tensor_copy(vpad[b][:, :, hp, 16 * hp:16 * hp + 16],
                                          b_x[:].rearrange("p (a k d) -> p a k d", k=2, d=DH)[:, :, hp, :]).then_inc(v_done, 1)
                    if on(3):
                        etb(2)
                    if on(4):
                        dve.wait_ge(cum_ps, r + 1)
                        V.tensor_tensor(cb[:], b_x[:, 0:G * E].rearrange("p (t e) -> p t e", e=E),
                                        base[:].rearrange("p (a e) -> p a e", a=1).to_broadcast([P, G, E]),
                                        ALU.add).then_inc(cb_done, 1)
                        dve.wait_ge(cb_done, 2 * r + 1)
                        V.tensor_tensor(base[:], b_x[:, G * E:(G + 1) * E], base[:], ALU.add).then_inc(cb_done, 1)
                        dve.wait_ge(cb_done, 2 * r + 2)
                        stepped(V.tensor_tensor(
                            pm[:].rearrange("p (t k) e -> p t k e", k=2), o2,
                            cb[:].rearrange("p t (a e) -> p t a e", a=1).to_broadcast([P, G, 2, E]), ALU.mult))
                        steps_done()
                        stepped(V.tensor_reduce(pos[:], pm[:], AX, ALU.add))
                        steps_done()
                        stepped(V.tensor_scalar(keep[:], pos[:], float(CAP), None, ALU.is_lt))
                        stepped(V.scalar_tensor_tensor(slot[:], ixf[:].rearrange("p t k -> p (t k)"), float(CAP), pos[:],
                                                       ALU.mult, ALU.add))
                        steps_done()
                        stepped(V.tensor_scalar(far[:], keep[:], -float(NOWHERE), float(NOWHERE), ALU.mult, ALU.add))
                        steps_done()
                        V.tensor_tensor(sidx[par][:], slot[:], far[:], ALU.add).then_inc(slot_done, 1)
                        dve.wait_ge(el_done, r + 1)
                        stepped(V.tensor_scalar(gs[:], el[:], 1.0, None, ALU.add))
                        steps_done()
                        stepped(V.reciprocal(gg[:, :, 0], gs[:]))
                        steps_done()
                        stepped(V.tensor_tensor(gg[:, :, 1], gg[:, :, 0], el[:], ALU.mult))
                        steps_done()
                        stepped(V.tensor_tensor(s.gates[:, bass.ds(r * G, G), :], gg[:],
                                                keep[:].rearrange("p (t k) -> p t k", k=2), ALU.mult))
                    if on(3):
                        etb(3)
                        dve.wait_ge(pv_ps, G * w + G)
                        V.reciprocal(rden[:], p_d[:]).then_inc(rd_done, 1)
                        dve.wait_ge(rd_done, w + 1)
                        after(dve, wo_ps, w)
                        V.tensor_tensor(att[:], p_o[:], rden[:], ALU.mult).then_inc(att_done, 1)
                        dve.wait_ge(wo_ps, w + 1)
                        dve.wait_ge(nn_done, w + 1)
                        after(dve, n2_done, w - 1)
                        after(dve, sum_done, w - 1)
                        V.tensor_tensor(xa[c][:], b_y[:].rearrange("p (t n) -> p t n", t=G), nn[c][:], ALU.add).then_inc(res_done, 1)
                        dve.wait_ge(res_done, w + 1)
                        after(dve, ve2_done, w)
                        settle(dve, s)
                        stats(lambda t: xa[c][:, t, :], bn2, mv2,
                              bn2_done, mv2_done, w)
                    if on(0):
                        after(dve, nn_done, i - 1)
                        settle(dve, s)
                        stats(lambda t: s.h[:, bass.ds(i * G + t, 1), :].rearrange("p a n -> p (a n)"), bn, mv[par],
                              bn_done, mv_done, i)
                    if on(1):
                        m, d = i - 1, 1 - par
                        dve.wait_ge(rs_done, m + 1)
                        after(dve, nt_ps, m - 1)
                        for t in range(G):
                            last = V.tensor_scalar(n[d][:, t, :], s.h[:, bass.ds(m * G + t, 1), :].rearrange("p a n -> p (a n)"),
                                                   mv[d][:, t, 0:1], rs[d][:, 1, t:t + 1], ALU.subtract, ALU.mult)
                        last.then_inc(n_done, 1)

                pipelined(dve, body, 4, PAIR0)
                dve.wait_ge(cb_done, 2 * GROUPS)
                V.tensor_copy(s.counts[:], base[0:1, :]).then_inc(counted, 1)
                dve.wait_ge(counted, 1)


def phase3(nc, s, ins):
    UNIT = ((0, 1), (1, 1), (2, 2), (4, 4))
    NU = len(UNIT)
    BUFS = 4
    assert sum(n for _, n in UNIT) * P == CAP
    with ExitStack() as ctx:
        def sb(name, shape, dt=F32):
            return ctx.enter_context(nc.sbuf_tensor("c_" + name, shape, dt))

        def sem(name):
            return ctx.enter_context(nc.semaphore("c_" + name))

        b1 = sb("b1", [P, E * FC])
        b2 = [sb(f"b2_{i}", [P, P]) for i in range(BUFS)]
        w1 = [sb(f"w1_{i}", [P, FF]) for i in range(BUFS)]
        w2 = [sb(f"w2_{i}", [P, FC, P]) for i in range(BUFS)]
        xin = [sb(f"xin{i}", [P, CAP // P, ROW]) for i in range(BUFS)]
        dest = [sb(f"dest{i}", [P, CAP // P], I32) for i in range(BUFS)]
        xt = [sb(f"xt{i}", [P, CAP]) for i in range(2)]
        ht = [sb(f"ht{i}", [P, FC, CAP]) for i in range(2)]
        y = [sb(f"y{i}", [P, CAP // P, P]) for i in range(2)]
        p_x, p_y = ([ctx.enter_context(nc.psum_tensor(f"c_{x}{i}", [P, 512], F32)) for i in range(2)] for x in ("px", "py"))
        p_h = [ctx.enter_context(nc.psum_tensor(f"c_ph{i}", [P, 512], F32)) for i in range(FC)]

        b_loaded = sem("b_loaded")
        w_loaded = [sem(f"w_loaded{i}") for i in range(BUFS)]
        x_loaded = [[sem(f"x_loaded{i}_{u}") for u in range(NU)] for i in range(BUFS)]
        sent = [sem(f"sent{u}") for u in range(NU)]
        buffers_sent = sem("buffers_sent")
        x_ps, xt_done, dest_done, h_ps, ht_done, y_ps, y_done = (
            sem(x) for x in ("x_ps", "xt", "dest", "h_ps", "ht", "y_ps", "y"))

        def experts(body, eng, lag):
            regs = [eng.alloc_register(f"rows{r}") for r in range(4)]

            def step(i, quad, ph, on):
                if on(0):
                    eng.load(regs[ph], s.counts[0:1, bass.ds(i, 1)])
                body(i, quad, ph, on, lambda l: regs[(ph - l) % 4])
            for i in range(4):
                step(i, i // 4, i % 4, lambda l, i=i: 0 <= i - l)
            with eng.Fori(1, E // 4) as quad:
                for ph in range(4):
                    step(quad * 4 + ph, quad, ph, lambda l: True)
            for i in range(E, E + lag):
                step(i, i // 4, i % 4, lambda l, i=i: i - l < E)

        def later_units(eng, count, work, skipped):
            with eng.If_cmp(count, UNIT[1][0] * P, "IS_GT"):
                work(1)
                with eng.If_cmp(count, UNIT[2][0] * P, "IS_GT"):
                    work(2)
                    with eng.If_cmp(count, UNIT[3][0] * P, "IS_GT"):
                        work(3)
                    with eng.Else():
                        skipped(3)
                with eng.Else():
                    skipped(2)
            with eng.Else():
                skipped(1)

        def counting(eng, done, e, steps=1):
            def skipped(u):
                eng.wait_ge(done, (e * NU + u) * steps)
                eng.sem_inc(done, (NU - u) * steps)
            return skipped

        with nc.Block() as block:
            @block.sync
            def _(sp):
                sp.dma_start(b1[:], ins["b1"]).then_inc(b_loaded, 16)

                def body(e, quad, ph, on, count):
                    after(sp, x_ps, NU * (e - BUFS) + NU)
                    after(sp, dest_done, NU * (e - BUFS) + NU)

                    def load(u):
                        first, n = UNIT[u]
                        sp.dma_start(xin[ph][:, first:first + n, :],
                                     ins["slots"][bass.ds(e * CAP + first * P, n * P)].rearrange("(p t) n -> p t n", t=n)
                                     ).then_inc(x_loaded[ph][u], 16)

                    def skipped(u):
                        for v in range(u, NU):
                            sp.sem_inc(x_loaded[ph][v], 16)
                    load(0)
                    after(sp, y_done, NU * (e - BUFS) + NU)
                    for dst, src in ((w1[ph][:], ins["w1"][bass.ds(e, 1)].rearrange("a p f -> p (a f)")),
                                     (w2[ph][:], ins["w2"][bass.ds(e, 1)].rearrange("a (p c) n -> p (a c) n", c=FC)),
                                     (b2[ph][:], ins["b2"][bass.ds(e, 1), :].to_broadcast([P, P]))):
                        sp.dma_start(dst, src).then_inc(w_loaded[ph], 16)
                    later_units(sp, count(0), load, skipped)

                experts(body, sp, 0)

            @block.tensor
            def _(pe):
                def body(i, quad, ph, on, count):
                    def turn(u):
                        e, b = i, ph
                        first, n = UNIT[u]
                        pe.wait_ge(x_loaded[b][u], 16 * quad + 16)
                        after(pe, xt_done, NU * e + u - 1)
                        for t in range(n):
                            last = nc.tensor.transpose(p_x[u % 2][:, t * P:(t + 1) * P], xin[b][:, first + t, 0:P], s.ident[:])
                        last.then_inc(x_ps, 1)

                    def layer1(u):
                        e, b = i - 1, (ph - 1) % 4
                        first, n = UNIT[u]
                        cols = slice(first * P, (first + n) * P)
                        pe.wait_ge(xt_done, NU * e + u + 1)
                        if u == 0:
                            pe.wait_ge(w_loaded[b], 48 * (quad + (ph - 1) // 4) + 48)
                        for ch in range(FC):
                            after(pe, ht_done, FC * (NU * e + u - 1) + ch + 1)
                            nc.tensor.matmul(p_h[ch][:, 0:n * P], w1[b][:].rearrange("p (f c) -> p c f", c=FC)[:, ch, :],
                                             xt[b % 2][:, cols], start=True, stop=True).then_inc(h_ps, 1)

                    def layer2(u):
                        e, b = i - 2, (ph - 2) % 4
                        first, n = UNIT[u]
                        pe.wait_ge(ht_done, FC * (NU * e + u) + FC)
                        after(pe, y_done, NU * e + u - 1)
                        for t in range(n):
                            for ch in range(FC):
                                last = nc.tensor.matmul(p_y[u % 2][:, t * P:(t + 1) * P],
                                                        ht[b % 2][:, ch, (first + t) * P:(first + t + 1) * P],
                                                        w2[b][:, ch, :], start=(ch == 0), stop=(ch == FC - 1))
                        last.then_inc(y_ps, 1)

                    if on(1):
                        layer1(0)
                    if on(0):
                        turn(0)
                    if on(2):
                        layer2(0)
                    if on(1):
                        later_units(pe, count(1), layer1, counting(pe, h_ps, i - 1, FC))
                    if on(0):
                        later_units(pe, count(0), turn, counting(pe, x_ps, i))
                    if on(2):
                        later_units(pe, count(2), layer2, counting(pe, y_ps, i - 2))

                experts(body, pe, 2)

            @block.scalar
            def _(act):
                act.wait_ge(b_loaded, 16)

                def body(i, quad, ph, on, count):
                    def gelu(u):
                        e, b = i - 1, (ph - 1) % 2
                        first, n = UNIT[u]
                        if u == 0:
                            after(act, y_ps, NU * (e - 2) + NU)
                        for ch in range(FC):
                            act.wait_ge(h_ps, FC * (NU * e + u) + ch + 1)
                            settle(act, s)
                            nc.scalar.activation(ht[b][:, ch, first * P:(first + n) * P], p_h[ch][:, 0:n * P],
                                                 ACT.Gelu_apprx_tanh, bias=b1[:, bass.ds(e * FC + ch, 1)]).then_inc(ht_done, 1)
                    if on(1):
                        gelu(0)
                        later_units(act, count(1), gelu, counting(act, ht_done, i - 1, FC))

                experts(body, act, 1)

            @block.vector
            def _(dve):
                def body(i, quad, ph, on, count):
                    def affine(u):
                        e, b = i, ph % 2
                        first, n = UNIT[u]
                        if u == 0:
                            after(dve, h_ps, FC * (NU * (e - 2) + NU))
                        dve.wait_ge(x_ps, NU * e + u + 1)
                        nc.vector.tensor_scalar(xt[b][:, first * P:(first + n) * P], p_x[u % 2][:, 0:n * P],
                                                s.vec[:, C_L2G:C_L2G + 1], s.vec[:, C_L2B:C_L2B + 1],
                                                ALU.mult, ALU.add).then_inc(xt_done, 1)

                    def result(u):
                        e, b = i - 2, (ph - 2) % 4
                        first, n = UNIT[u]
                        dve.wait_ge(y_ps, NU * e + u + 1)
                        if u == 0:
                            after(dve, buffers_sent, e - 1)
                        nc.vector.tensor_tensor(y[b % 2][:, first:first + n, :],
                                                p_y[u % 2][:, 0:n * P].rearrange("p (t n) -> p t n", t=n),
                                                b2[b][:].rearrange("p (t n) -> p t n", t=1).to_broadcast([P, n, P]),
                                                ALU.add).then_inc(y_done, 1)
                    if on(0):
                        affine(0)
                    if on(2):
                        result(0)
                    if on(0):
                        later_units(dve, count(0), affine, counting(dve, xt_done, i))
                    if on(2):
                        later_units(dve, count(2), result, counting(dve, y_done, i - 2))

                experts(body, dve, 2)

            @block.gpsimd
            def _(pool):
                issued = [pool.alloc_register(f"issued{u}") for u in range(NU)]
                for reg in issued:
                    pool.reg_mov(reg, 0)

                def body(i, quad, ph, on, count):
                    def keep_dest(u):
                        e, b = i, ph
                        first, n = UNIT[u]
                        pool.wait_ge(x_loaded[b][u], 16 * quad + 16)
                        settle(pool, s)
                        nc.gpsimd.tensor_copy(dest[b][:, first:first + n],
                                              xin[b][:, first:first + n, P:P + 1].bitcast(I32).rearrange("p t a -> p (t a)")
                                              ).then_inc(dest_done, 1)

                    def send(u):
                        e, b = i - 2, (ph - 2) % 4
                        first, n = UNIT[u]
                        pool.wait_ge(y_done, NU * e + u + 1)
                        pool.wait_ge(dest_done, NU * e + u + 1)
                        settle(pool, s)
                        for t in range(first, first + n):
                            nc.gpsimd.indirect_dma_start(
                                ins["back"], bass.IndirectOffsetOnAxis(ap=dest[b][:, t:t + 1], axis=0),
                                y[b % 2][:, t, :], None, bounds_check=2 * TOKENS - 1, oob_is_err=False).then_inc(sent[u], 16)
                        pool.reg_add(issued[u], issued[u], 16 * n)

                    def landed(u):
                        pool.wait_ge(sent[u], issued[u])
                        settle(pool, s)
                    if on(3):
                        landed(0)
                        later_units(pool, count(3), landed, lambda u: None)
                        pool.sem_inc(buffers_sent, 1)
                    if on(0):
                        keep_dest(0)
                        later_units(pool, count(0), keep_dest, counting(pool, dest_done, i))
                    if on(2):
                        send(0)
                        later_units(pool, count(2), send, lambda u: None)

                experts(body, pool, 3)


def phase4(nc, s, ins, out):
    with ExitStack() as ctx:
        def sb(name, shape, dt=F32):
            return ctx.enter_context(nc.sbuf_tensor("d_" + name, shape, dt))

        def sem(name):
            return ctx.enter_context(nc.semaphore("d_" + name))

        got = [sb(f"got{i}", [P, G, 2, P]) for i in range(2)]
        part = [sb(f"part{i}", [P, G, P]) for i in range(2)]
        res = [sb(f"res{i}", [P, G, P]) for i in range(2)]
        got_in = [sem(f"got_in{i}") for i in range(2)]
        part_done, res_done = sem("part"), sem("res")
        stored = [sem(f"stored{i}") for i in range(2)]
        with nc.Block() as block:
            @block.sync
            def _(sp):
                def body(i, pair, par, on):
                    after(sp, res_done, i - 1)
                    sp.dma_start(got[par][:], ins["back_tokens"][:, bass.ds(i * G, G)]).then_inc(got_in[par], 16)
                pipelined(sp, body, 0)

            @block.vector
            def _(dve):
                def body(i, pair, par, on):
                    dve.wait_ge(got_in[par], 16 * pair + 16)
                    after(dve, stored[par], 16 * pair)
                    for t in range(G):
                        last = nc.vector.scalar_tensor_tensor(
                            part[par][:, t, :], got[par][:, t, 0, :], s.gates[:, bass.ds(i * G + t, 1), 0],
                            s.h[:, bass.ds(i * G + t, 1), :].rearrange("p a n -> p (a n)"), ALU.mult, ALU.add)
                    last.then_inc(part_done, 1)
                    dve.wait_ge(part_done, i + 1)
                    for t in range(G):
                        last = nc.vector.scalar_tensor_tensor(
                            res[par][:, t, :], got[par][:, t, 1, :], s.gates[:, bass.ds(i * G + t, 1), 1],
                            part[par][:, t, :], ALU.mult, ALU.add)
                    last.then_inc(res_done, 1)
                pipelined(dve, body, 0)

            @block.scalar
            def _(act):
                def body(i, pair, par, on):
                    act.wait_ge(res_done, i + 1)
                    act.dma_start(out[:, bass.ds(i * G, G)], res[par][:]).then_inc(stored[par], 16)
                pipelined(act, body, 0)
                for b in range(2):
                    act.wait_ge(stored[b], 16 * (GROUPS // 2))


_DRAM = ["table", "ids", "vecs", "Wh", "bh", "Wqk", "Wo", "wq", "wk", "wv", "wo", "wr", "w1", "w2", "b1", "b2"]


def build(nc, ins, out):
    slots = nc.dram_tensor("slots", [SLOTS, ROW], F32).ap()
    back = nc.dram_tensor("back", [2 * TOKENS, P], F32).ap()
    ins["slots"] = slots
    ins["slot_parts"] = slots.rearrange("(a r) n -> a r n", r=8)
    ins["back"] = back
    ins["back_parts"] = back.rearrange("(a r) n -> a (r n)", r=BACK_PART // P)
    ins["back_tokens"] = back.rearrange("(s p k) n -> p s k n", p=P, k=2)
    s = Shared()
    with ExitStack() as ctx:
        constants(nc, ctx, s, ins)
        phase1(nc, s, ins)
        phase2(nc, s, ins)
        phase3(nc, s, ins)
        phase4(nc, s, ins, out.rearrange("s p n -> p s n"))


def kernel(**inputs):
    import concourse.bacc as bacc
    from concourse.bass_utils import run_bass_kernel_spmd

    a = {k: np.asarray(v) for k, v in inputs.items()}
    c = np.ascontiguousarray
    gamma, beta, bh = a["L0_attn_gamma"], a["L0_attn_beta"], a["L0_attn_bh"]
    arrays = {
        "table": c(a["L0_tok_conv_w"].transpose(1, 2, 0).reshape(VOCAB, TAPS * P)),
        "ids": c(a["x"].T),
        "vecs": c(np.stack([a["L0_attn_ln_g"], a["L0_attn_ln_b"], a["L0_attn_bqk"], gamma[0], gamma[1], beta[0],
                            beta[1], a["L0_attn_bo"], bh[2 * P:3 * P], bh[3 * P:4 * P], a["L0_ffn_ln1_g"],
                            a["L0_ffn_ln1_b"], a["L0_ffn_ln2_g"], a["L0_ffn_ln2_b"]], axis=1)),
        "Wh": c(a["L0_attn_Wh"]), "bh": c(bh.reshape(1, -1)), "Wqk": c(a["L0_attn_Wqk"]), "Wo": c(a["L0_attn_Wo"]),
        "wq": c(a["L0_ffn_wq"]), "wk": c(a["L0_ffn_wk"]), "wv": c(a["L0_ffn_wv"]), "wo": c(a["L0_ffn_wo"]),
        "wr": c(a["L0_ffn_wr"]), "w1": c(a["L0_ffn_w1"]), "w2": c(a["L0_ffn_w2"]),
        "b1": c(a["L0_ffn_b1"].reshape(E, P, FC).transpose(1, 0, 2).reshape(P, E * FC)),
        "b2": c(a["L0_ffn_b2"]),
    }
    nc = bacc.Bacc("TRN2", target_bir_lowering=False, num_devices=1)
    ins = {k: nc.dram_tensor("in_" + k, arrays[k].shape, mybir.dt.from_np(arrays[k].dtype), kind="ExternalInput").ap()
           for k in _DRAM}
    out = nc.dram_tensor("out", [SEQS, P, P], F32, kind="ExternalOutput").ap()
    build(nc, ins, out)
    got = run_bass_kernel_spmd(nc, [{"in_" + k: arrays[k] for k in _DRAM}], core_ids=[0])
    return got.results[0]["out"]
```

```python
from contextlib import ExitStack

import numpy as np
import concourse.bass as bass
from concourse import mybir

F32 = mybir.dt.float32
BF16 = mybir.dt.bfloat16
I32 = mybir.dt.int32
U32 = mybir.dt.uint32
ALU = mybir.AluOpType
ACT = mybir.ActivationFunctionType
AX = mybir.AxisListType.X

P = 128
VOCAB = 8000
TAPS = 3
SEQS = 128
G = 4
GROUPS = SEQS // G
N = G * P
HEADS = 8
DH = P // HEADS
E = 64
FF = 512
FC = FF // P
TOKENS = SEQS * P
CAP = 2 * (TOKENS * 2 // E)
SLOTS = E * CAP
ROW = 132
EPS = 1e-5
BACK_PART = 2048
BACK_PARTS = TOKENS * 2 // BACK_PART
NOWHERE = 1 << 24
(C_LNG, C_LNB, C_BQK, C_GA0, C_GA1, C_BE0, C_BE1, C_BG0, C_BG1,
 C_L1G, C_L1B, C_L2G, C_L2B) = range(13)
NVEC = 13


def after(eng, sem, value):
    if not isinstance(value, int) or value > 0:
        eng.wait_ge(sem, value)


def pipelined(eng, body, lag, pairs_from=2):
    for i in range(2 * pairs_from):
        body(i, i // 2, i % 2, lambda l, i=i: 0 <= i - l)
    with eng.Fori(pairs_from, GROUPS // 2) as pair:
        for parity in range(2):
            body(pair * 2 + parity, pair, parity, lambda l: True)
    for i in range(GROUPS, GROUPS + lag):
        body(i, i // 2, i % 2, lambda l, i=i: i - l < GROUPS)


def settle(eng, s):
    eng.sem_inc(s.settled, 1)


class Shared:
    pass


def constants(nc, ctx, s, ins):
    def sb(name, shape, dt=F32):
        return ctx.enter_context(nc.sbuf_tensor(name, shape, dt))
    s.vec = sb("vec", [P, NVEC])
    s.ident = sb("ident", [P, P])
    s.h = sb("h_all", [P, SEQS, P])
    s.gates = sb("gates", [P, SEQS, 2])
    s.counts = sb("counts", [1, E], I32)
    s.expo = sb("expo", [P, 2 * G])
    const_ready = s.const_ready = ctx.enter_context(nc.semaphore("const_ready"))
    s.settled = ctx.enter_context(nc.semaphore("settled"))
    vec_loaded = ctx.enter_context(nc.semaphore("vec_loaded"))
    with nc.Block() as block:
        @block.sync
        def _(sp):
            sp.dma_start(s.vec[:], ins["vecs"]).then_inc(vec_loaded, 16)
            sp.wait_ge(vec_loaded, 16)

        @block.gpsimd
        def _(pool):
            nc.gpsimd.memset(s.ident[:], 1.0).then_inc(const_ready, 1)
            nc.gpsimd.memset(s.expo[:], -0.5).then_inc(const_ready, 1)
            pool.wait_ge(const_ready, 2)
            nc.gpsimd.affine_select(out=s.ident[:], in_=s.ident[:], compare_op=ALU.is_equal, fill=0.0,
                                    base=0, pattern=[[-1, P]], channel_multiplier=1).then_inc(const_ready, 1)
            pool.wait_ge(const_ready, 3)


def phase1(nc, s, ins):
    with ExitStack() as ctx:
        def sb(name, shape, dt=F32):
            return ctx.enter_context(nc.sbuf_tensor("a_" + name, shape, dt))

        def sem(name):
            return ctx.enter_context(nc.semaphore("a_" + name))

        ids = sb("ids", [P, SEQS], I32)
        idx = [sb(f"idx{i}", [P, G], I32) for i in range(2)]
        emb = [sb(f"emb{i}", [P, G, TAPS * P]) for i in range(2)]
        wh = sb("wh", [P, 512])
        wqk = sb("wqk", [P, P])
        wo = sb("wo", [P, 2, P])
        bv = sb("bv", [P, 2 * P])
        bo = sb("bo", [P, P])
        down = sb("down", [P, P])
        up = sb("up", [P, P])
        zrow = sb("zrow", [P, 8, ROW])
        h0 = [sb(f"h0_{i}", [P, G, P]) for i in range(2)]
        bn = sb("bn", [P, G, 6])
        mv = [sb(f"mv{i}", [P, G, 2]) for i in range(2)]
        ve = sb("ve", [P, 2, G])
        rs = [sb(f"rs{i}", [P, 2, G]) for i in range(2)]
        u = sb("u", [P, G, P])
        hb = sb("hb", [P, G, P])
        n = [sb(f"n{i}", [P, G, P]) for i in range(2)]
        nt = [sb(f"nt{i}", [P, N]) for i in range(2)]
        z = [sb(f"z{i}", [P, N]) for i in range(2)]
        q = [sb(f"q{i}", [P, N]) for i in range(2)]
        k = [sb(f"k{i}", [P, N]) for i in range(2)]
        gate = [sb(f"gate{i}", [P, 2, N]) for i in range(2)]
        vpre = sb("vpre", [P, G, 2 * P])
        v = [sb(f"v{i}", [P, G, 2 * P]) for i in range(2)]
        r = sb("r", [P, N])
        at = sb("at", [P, N])
        vg = sb("vg", [P, 2, N])
        bank = [ctx.enter_context(nc.psum_tensor(f"a_bank{i}", [P, 512], F32)) for i in range(8)]
        b_conv, b_n, b_x, b_y, b_s, b_vt0, b_vt1, b_o = bank

        loaded, shift_made, zero_made, zeroed = sem("loaded"), sem("shift_made"), sem("zero_made"), sem("zeroed")
        idx_ready = sem("idx_ready")
        emb_in = [sem(f"emb_in{i}") for i in range(2)]
        conv_done, h0_done, bn_done, mv_done = sem("conv"), sem("h0"), sem("bn"), sem("mv")
        ve_done, rs_done, u_done, hb_done, hu_done = sem("ve"), sem("rs"), sem("u"), sem("hb"), sem("hu")
        n_done, nt_ps, nt_done = sem("n"), sem("nt_ps"), sem("nt")
        z_ps, g_ps, v_ps = sem("z_ps"), sem("g_ps"), sem("v_ps")
        z_done, g_done, vb_done, v_done, qk_done = sem("z"), sem("g"), sem("vb"), sem("v"), sem("qk")
        sim_ps, r_done, at_done, vt_ps, vg_done = sem("sim_ps"), sem("r"), sem("at"), sem("vt_ps"), sem("vg")
        o_ps, h1_done = sem("o_ps"), sem("h1")
        LOADS = 6
        PAIR0 = 3

        with nc.Block() as block:
            @block.sync
            def _(sp):
                for dst, src in ((ids[:], ins["ids"]), (wqk[:], ins["Wqk"]), (wh[:], ins["Wh"]),
                                 (wo[:], ins["Wo"].rearrange("(c p) n -> p c n", p=P)),
                                 (bv[:], ins["bh"][:, 0:2 * P].to_broadcast([P, 2 * P])),
                                 (bo[:], ins["bo"].to_broadcast([P, P]))):
                    sp.dma_start(dst, src).then_inc(loaded, 16)
                sp.wait_ge(zero_made, 2)
                with sp.Fori(0, GROUPS) as i:
                    sp.wait_ge(conv_done, i + 1)
                    for part in range(E // GROUPS):
                        sp.dma_start(ins["slot_parts"][bass.ds((i * (E // GROUPS) + part) * P, P)],
                                     zrow[:]).then_inc(zeroed, 16)
                sp.wait_ge(zeroed, 16 * E)

            @block.gpsimd
            def _(pool):
                for m in (down, up):
                    nc.gpsimd.memset(m[:], 1.0).then_inc(shift_made, 1)
                pool.wait_ge(shift_made, 2)
                for m, way in ((down, 1), (up, -1)):
                    nc.gpsimd.affine_select(out=m[:], in_=m[:], compare_op=ALU.is_equal, fill=0.0, base=way,
                                            pattern=[[-1, P]], channel_multiplier=1).then_inc(shift_made, 1)
                pool.wait_ge(loaded, 16 * LOADS)

                def body(i, pair, par, on):
                    if on(0):
                        after(pool, conv_done, i - 1)
                        after(pool, h0_done, i - 1)
                        settle(pool, s)
                        nc.gpsimd.tensor_copy(idx[par][:], ids[:, bass.ds(i * G, G)]).then_inc(idx_ready, 1)
                        pool.wait_ge(idx_ready, i + 1)
                        settle(pool, s)
                        for t in range(G):
                            nc.gpsimd.indirect_dma_start(
                                emb[par][:, t, :], None, ins["table"],
                                bass.IndirectOffsetOnAxis(ap=idx[par][:, t:t + 1], axis=0),
                                bounds_check=VOCAB - 1, oob_is_err=False).then_inc(emb_in[par], 16)
                    if on(1):
                        g, b = i - 1, 1 - par
                        pool.wait_ge(mv_done, G * g + G)
                        after(pool, n_done, g - 1)
                        settle(pool, s)
                        nc.gpsimd.tensor_scalar(ve[:, 0, :], mv[b][:, :, 1], EPS, None, ALU.add).then_inc(ve_done, 1)
                        nc.gpsimd.tensor_scalar(ve[:, 1, :], mv[b][:, :, 1], 1.0 + EPS, EPS * EPS,
                                                ALU.mult, ALU.add).then_inc(ve_done, 1)
                        pool.wait_ge(ve_done, 2 * g + 2)
                        settle(pool, s)
                        nc.gpsimd.tensor_tensor(rs[b][:].rearrange("p a t -> p (a t)"),
                                                ve[:].rearrange("p a t -> p (a t)"), s.expo[:],
                                                ALU.pow).then_inc(rs_done, 1)
                        pool.wait_ge(rs_done, g + 1)
                        pool.wait_ge(u_done, g + 1)
                        pool.wait_ge(hb_done, g + 1)
                        settle(pool, s)
                        nc.gpsimd.tensor_tensor(s.h[:, bass.ds(g * G, G), :], u[:], hb[:],
                                                ALU.add).then_inc(hu_done, 1)

                pipelined(pool, body, 1)

            @block.tensor
            def _(pe):
                pe.wait_ge(loaded, 16 * LOADS)
                pe.wait_ge(shift_made, 4)

                def body(i, pair, par, on):
                    g, b = i - 2, par
                    w, c = i - 3, 1 - par
                    x, d = i - 4, par
                    if on(2):
                        pe.wait_ge(n_done, g + 1)
                        after(pe, nt_done, g)
                        for t in range(G):
                            last = nc.tensor.transpose(b_n[:, t * P:(t + 1) * P], n[b][:, t, :], s.ident[:])
                        last.then_inc(nt_ps, 1)
                    if on(4):
                        pe.wait_ge(at_done, x + 1)
                        pe.wait_ge(v_done, 2 * x + 2)
                        after(pe, vg_done, 2 * x)
                        for ch, bk in enumerate((b_vt0, b_vt1)):
                            for t in range(G):
                                sl = slice(t * P, (t + 1) * P)
                                last = nc.tensor.matmul(bk[:, sl], v[d][:, t, ch * P:(ch + 1) * P], at[:, sl],
                                                        start=True, stop=True)
                            last.then_inc(vt_ps, 1)
                    if on(2):
                        pe.wait_ge(nt_done, g + 1)
                        after(pe, vb_done, 2 * g)
                        nc.tensor.matmul(b_x[:], wqk[:], nt[b][:], start=True, stop=True).then_inc(z_ps, 1)
                        nc.tensor.matmul(b_y[:], wh[:, 2 * P:3 * P], nt[b][:], start=True, stop=True).then_inc(g_ps, 1)
                    if on(3):
                        pe.wait_ge(qk_done, 2 * w + 2)
                        after(pe, r_done, w)
                        for t in range(G):
                            sl = slice(t * P, (t + 1) * P)
                            last = nc.tensor.matmul(b_s[:, sl], k[c][:, sl], q[c][:, sl], start=True, stop=True)
                        last.then_inc(sim_ps, 1)
                    if on(2):
                        pe.wait_ge(z_done, g + 1)
                        nc.tensor.matmul(b_x[:], wh[:, 3 * P:4 * P], nt[b][:], start=True, stop=True).then_inc(g_ps, 1)
                    if on(4):
                        pe.wait_ge(vg_done, 2 * x + 2)
                        after(pe, h1_done, x)
                        for t in range(G):
                            for ch in range(2):
                                last = nc.tensor.matmul(b_o[:, t * P:(t + 1) * P], vg[:, ch, t * P:(t + 1) * P],
                                                        wo[:, ch, :], start=(ch == 0), stop=(ch == 1))
                        last.then_inc(o_ps, 1)
                    if on(2):
                        for half, bk in enumerate((b_y, b_x)):
                            pe.wait_ge(g_done, 2 * g + 1 + half)
                            for j in range(2):
                                t = 2 * half + j
                                last = nc.tensor.matmul(bk[:, j * 256:(j + 1) * 256], nt[b][:, t * P:(t + 1) * P],
                                                        wh[:, 0:2 * P], start=True, stop=True)
                            last.then_inc(v_ps, 1)
                    if on(0):
                        pe.wait_ge(emb_in[par], pair * 16 * G + 16 * G)
                        after(pe, h0_done, i)
                        nc.tensor.matmul(b_conv[:], down[:], emb[par][:, :, 0:P], start=True, stop=False)
                        nc.tensor.matmul(b_conv[:], up[:], emb[par][:, :, 2 * P:3 * P], start=False,
                                         stop=True).then_inc(conv_done, 1)

                pipelined(pe, body, 4, PAIR0)

            @block.scalar
            def _(act):
                def body(i, pair, par, on):
                    g, b = i - 2, par
                    w = i - 3
                    if on(2):
                        act.wait_ge(z_ps, g + 1)
                        after(act, qk_done, 2 * (g - 1))
                        nc.scalar.activation(z[b][:], b_x[:], ACT.Silu, bias=s.vec[:, C_BQK:C_BQK + 1]).then_inc(z_done, 1)
                        after(act, vg_done, 2 * (g - 1))
                        act.wait_ge(g_ps, 2 * g + 1)
                        nc.scalar.activation(gate[b][:, 0, :], b_y[:], ACT.Silu, bias=s.vec[:, C_BG0:C_BG0 + 1]).then_inc(g_done, 1)
                    if on(3):
                        act.wait_ge(r_done, w + 1)
                        after(act, vt_ps, 2 * w)
                        nc.scalar.activation(at[:], r[:], ACT.Square).then_inc(at_done, 1)
                    if on(2):
                        act.wait_ge(g_ps, 2 * g + 2)
                        nc.scalar.activation(gate[b][:, 1, :], b_x[:], ACT.Silu, bias=s.vec[:, C_BG1:C_BG1 + 1]).then_inc(g_done, 1)
                        after(act, vt_ps, 2 * (g - 1))
                        for half in range(2):
                            act.wait_ge(vb_done, 2 * g + 1 + half)
                            nc.scalar.activation(v[b][:, 2 * half:2 * half + 2, :], vpre[:, 2 * half:2 * half + 2, :],
                                                 ACT.Silu).then_inc(v_done, 1)

                pipelined(act, body, 3, PAIR0)

            @block.vector
            def _(dve):
                nc.vector.memset(zrow[:], 0.0).then_inc(zero_made, 1)
                dve.wait_ge(zero_made, 1)
                nc.vector.memset(zrow[:, :, P:P + 1].bitcast(I32), NOWHERE).then_inc(zero_made, 1)
                dve.wait_ge(loaded, 16 * LOADS)

                def body(i, pair, par, on):
                    g, b = i - 2, par
                    w, c = i - 3, 1 - par
                    x, y = i - 4, par
                    if on(2):
                        dve.wait_ge(nt_ps, g + 1)
                        after(dve, v_ps, 2 * (g - 1))
                        nc.vector.tensor_scalar(nt[b][:], b_n[:], s.vec[:, C_LNG:C_LNG + 1], s.vec[:, C_LNB:C_LNB + 1],
                                                ALU.mult, ALU.add).then_inc(nt_done, 1)
                    if on(4):
                        after(dve, o_ps, x)
                        for ch, bk in enumerate((b_vt0, b_vt1)):
                            dve.wait_ge(vt_ps, 2 * x + 1 + ch)
                            nc.vector.tensor_tensor(vg[:, ch, :], bk[:], gate[y][:, ch, :], ALU.mult).then_inc(vg_done, 1)
                    if on(2):
                        dve.wait_ge(z_done, g + 1)
                        after(dve, sim_ps, g - 1)
                        for dst, ga, be in ((q, C_GA0, C_BE0), (k, C_GA1, C_BE1)):
                            nc.vector.tensor_scalar(dst[b][:], z[b][:], s.vec[:, ga:ga + 1], s.vec[:, be:be + 1],
                                                    ALU.mult, ALU.add).then_inc(qk_done, 1)
                    if on(3):
                        dve.wait_ge(sim_ps, w + 1)
                        after(dve, at_done, w)
                        nc.vector.tensor_scalar(r[:], b_s[:], 0.0, 1.0 / P, ALU.max, ALU.mult).then_inc(r_done, 1)
                    if on(1):
                        m, d = i - 1, 1 - par
                        dve.wait_ge(rs_done, m + 1)
                        after(dve, nt_ps, m - 1)
                        for t in range(G):
                            last = nc.vector.tensor_scalar(n[d][:, t, :], h0[d][:, t, :], mv[d][:, t, 0:1],
                                                           rs[d][:, 1, t:t + 1], ALU.subtract, ALU.mult)
                        last.then_inc(n_done, 1)
                        after(dve, hu_done, m)
                        for t in range(G):
                            last = nc.vector.tensor_scalar(u[:, t, :], h0[d][:, t, :], mv[d][:, t, 0:1],
                                                           rs[d][:, 0, t:t + 1], ALU.subtract, ALU.mult)
                        last.then_inc(u_done, 1)
                        nc.vector.tensor_tensor(hb[:], h0[d][:], bo[:].rearrange("p (t n) -> p t n", t=1).to_broadcast([P, G, P]),
                                                ALU.add).then_inc(hb_done, 1)
                    if on(4):
                        dve.wait_ge(o_ps, x + 1)
                        dve.wait_ge(hu_done, x + 1)
                        hs = s.h[:, bass.ds(x * G, G), :]
                        nc.vector.tensor_tensor(hs, b_o[:].rearrange("p (t n) -> p t n", t=G), hs,
                                                ALU.add).then_inc(h1_done, 1)
                    if on(2):
                        for half, bk in enumerate((b_y, b_x)):
                            dve.wait_ge(v_ps, 2 * g + 1 + half)
                            after(dve, v_done, 2 * (g - 1) + 1 + half)
                            nc.vector.tensor_tensor(
                                vpre[:, 2 * half:2 * half + 2, :], bk[:].rearrange("p (j n) -> p j n", j=2),
                                bv[:].rearrange("p (j n) -> p j n", j=1).to_broadcast([P, 2, 2 * P]),
                                ALU.add).then_inc(vb_done, 1)
                    if on(0):
                        dve.wait_ge(conv_done, i + 1)
                        after(dve, n_done, i - 1)
                        after(dve, hb_done, i - 1)
                        nc.vector.tensor_tensor(h0[par][:], b_conv[:].rearrange("p (t n) -> p t n", t=G),
                                                emb[par][:, :, P:2 * P], ALU.add).then_inc(h0_done, 1)
                        dve.wait_ge(h0_done, i + 1)
                        after(dve, mv_done, G * i)
                        settle(dve, s)
                        for t in range(G):
                            nc.vector.bn_stats(bn[:, t, :], h0[par][:, t, :]).then_inc(bn_done, 1)
                        for t in range(G):
                            dve.wait_ge(bn_done, G * i + t + 1)
                            settle(dve, s)
                            nc.vector.bn_aggr(mv[par][:, t, :], bn[:, t, :]).then_inc(mv_done, 1)

                pipelined(dve, body, 4, PAIR0)


def phase2(nc, s, ins):
    with ExitStack() as ctx:
        def sb(name, shape, dt=F32):
            return ctx.enter_context(nc.sbuf_tensor("b_" + name, shape, dt))

        def two(name, shape, dt=F32):
            return [sb(f"{name}{i}", shape, dt) for i in range(2)]

        def sem(name):
            return ctx.enter_context(nc.semaphore("b_" + name))

        wq, wk, wv, wo = (sb(x, [P, P]) for x in ("wq", "wk", "wv", "wo"))
        wr = sb("wr", [P, E])
        zeros = sb("zeros", [P, BACK_PART])
        headmask = sb("headmask", [P, HEADS])
        hm_tmp = sb("hm_tmp", [P, HEADS])
        iota_e = sb("iota_e", [P, E], I32)
        iota_f = sb("iota_f", [P, E])
        payload = sb("payload", [P, SEQS, 2], I32)
        before_f = sb("before_f", [P, P])
        before = sb("before", [P, P], BF16)
        ones = sb("ones", [P, P], BF16)
        bn = sb("bn", [P, G, 6])
        mv = two("mv", [P, G, 2])
        ve = sb("ve", [P, 2, G])
        rs = two("rs", [P, 3, G])
        nn = two("nn", [P, G, P])
        xa = two("xa", [P, G, P])
        n = two("n", [P, G, P])
        xt = sb("xt", [P, N])
        q = two("q", [P, N])
        k = sb("k", [P, N])
        km = two("km", [P, HEADS, N])
        vpad = two("vpad", [P, G * 4, 2, 32])
        mx = two("mx", [P, HEADS])
        ex = two("ex", [P, HEADS, P])
        et = two("et", [P, HEADS, P])
        sums = two("sums", [P, G * HEADS])
        rsum = sb("rsum", [P, G * HEADS])
        rwide = sb("rwide", [P, N])
        rden = sb("rden", [P, N])
        att = sb("att", [P, N])
        bn2 = sb("bn2", [P, G, 6])
        mv2 = two("mv2", [P, G, 2])
        ve2 = sb("ve2", [P, G])
        rs2 = two("rs2", [P, G])
        rows = two("rows", [P, G, 2, ROW])
        x2t = sb("x2t", [P, N])
        lg = sb("lg", [P, G, E])
        top = sb("top", [P, G, 8])
        topi = sb("topi", [P, G, 8], U32)
        ixf = sb("ixf", [P, G, 2])
        dl = sb("dl", [P, G])
        el = sb("el", [P, G])
        oh = sb("oh", [P, G * 2, E])
        ohs = sb("ohs", [P, G, E], BF16)
        base = sb("base", [P, E])
        cb = sb("cb", [P, G, E])
        pm = sb("pm", [P, G * 2, E])
        pos = sb("pos", [P, G * 2])
        keep = sb("keep", [P, G * 2])
        far = sb("far", [P, G * 2])
        slot = sb("slot", [P, G * 2])
        sidx = two("sidx", [P, G * 2], I32)
        gs = sb("gs", [P, G])
        gg = sb("gg", [P, G, 2])
        p_o = ctx.enter_context(nc.psum_tensor("b_o", [P, 512], F32))
        p_r = ctx.enter_context(nc.psum_tensor("b_r", [P, 512], F32))
        b_x = ctx.enter_context(nc.psum_tensor("b_x", [P, 512], F32))
        b_y = ctx.enter_context(nc.psum_tensor("b_y", [P, 512], F32))
        p_s = ctx.enter_context(nc.psum_tensor("b_s", [P, 1024], F32))
        p_t = ctx.enter_context(nc.psum_tensor("b_t", [P, 1024], F32))

        loaded, made, filled = sem("loaded"), sem("made"), sem("filled")
        bn_done, mv_done, ve_done, rs_done, n_done = sem("bn"), sem("mv"), sem("ve"), sem("rs"), sem("n")
        copy_done, nn_done, sum_done = sem("copy"), sem("nn"), sem("sum")
        nt_ps, xt_done, q_ps, q_done, k_ps, k_done = (sem(x) for x in ("nt_ps", "xt", "q_ps", "q", "k_ps", "k"))
        kma_done, kmb_done, v_ps, v_done = sem("kma"), sem("kmb"), sem("v_ps"), sem("v")
        s_ps, mx_done, ex_done, et_ps, eta_done, etb_done, pv_ps = (
            sem(x) for x in ("s_ps", "mx", "ex", "et_ps", "eta", "etb", "pv_ps"))
        rsum_done, rwide_done, r_ps, rden_done = sem("rsum"), sem("rwide"), sem("r_ps"), sem("rden")
        att_done, wo_ps, res_done = sem("att"), sem("wo_ps"), sem("res")
        bn2_done, mv2_done, ve2_done, rs2_done, n2_done, rows_done = (
            sem(x) for x in ("bn2", "mv2", "ve2", "rs2", "n2", "rows"))
        x2_ps, x2_done, lg_ps, lg_done = sem("x2_ps"), sem("x2"), sem("lg_ps"), sem("lg")
        top_done, topi_done, step, el_done, ohs_done, cum_ps, cb_done, slot_done = (
            sem(x) for x in ("top", "topi", "step", "el", "ohs", "cum_ps", "cb", "slot"))
        counted, zeros_made, zeroed = sem("counted"), sem("zeros_made"), sem("zeroed")
        scattered = [sem(f"scattered{i}") for i in range(2)]
        LOADS = 5
        PAIR0 = 4
        HALF = HEADS // 2
        KEYS_ACT = 3
        STEPS = 12

        with nc.Block() as block:
            @block.sync
            def _(sp):
                for dst, src in ((wq, "wq"), (wk, "wk"), (wv, "wv"), (wo, "wo"), (wr, "wr")):
                    sp.dma_start(dst[:], ins[src]).then_inc(loaded, 16)
                sp.wait_ge(loaded, 16 * LOADS)
                sp.wait_ge(zeros_made, 1)
                with sp.Fori(0, BACK_PARTS) as part:
                    sp.wait_ge(wo_ps, (part + 1) * (GROUPS // BACK_PARTS))
                    sp.dma_start(ins["back_parts"][bass.ds(part * P, P)], zeros[:]).then_inc(zeroed, 16)
                sp.wait_ge(zeroed, 16 * BACK_PARTS)

            @block.gpsimd
            def _(pool):
                made_n = [0]

                def make(ins_):
                    ins_.then_inc(made, 1)
                    made_n[0] += 1

                nc_g = nc.gpsimd
                make(nc_g.memset(hm_tmp[:], 1.0))
                make(nc_g.memset(before_f[:], 1.0))
                make(nc_g.memset(ones[:], 1.0))
                make(nc_g.iota(iota_e[:], pattern=[[1, E]], base=0, channel_multiplier=0))
                make(nc_g.iota(payload[:].rearrange("p s k -> p (s k)"), pattern=[[2 * P, SEQS], [1, 2]], base=0,
                               channel_multiplier=2))
                for b in range(2):
                    make(nc_g.memset(rows[b][:], 0.0))
                    make(nc_g.memset(vpad[b][:], 0.0))
                make(nc_g.memset(base[:], 0.0))
                pool.wait_ge(made, made_n[0])
                make(nc_g.affine_select(out=hm_tmp[:], in_=hm_tmp[:], compare_op=ALU.is_ge, fill=0.0, base=0,
                                        pattern=[[-DH, HEADS]], channel_multiplier=1))
                make(nc_g.affine_select(out=before_f[:], in_=before_f[:], compare_op=ALU.is_gt, fill=0.0, base=0,
                                        pattern=[[1, P]], channel_multiplier=-1))
                make(nc_g.tensor_copy(iota_f[:], iota_e[:]))
                pool.wait_ge(made, made_n[0])
                make(nc_g.affine_select(out=headmask[:], in_=hm_tmp[:], compare_op=ALU.is_ge, fill=0.0, base=DH - 1,
                                        pattern=[[DH, HEADS]], channel_multiplier=-1))
                make(nc_g.tensor_copy(before[:], before_f[:]))
                pool.wait_ge(made, made_n[0])
                s.made2 = made_n[0]

                def body(i, pair, par, on):
                    if on(7):
                        q, d = i - 7, 1 - par
                        pool.wait_ge(slot_done, q + 1)
                        pool.wait_ge(rows_done, 2 * q + 2)
                        settle(pool, s)
                        for t in range(G):
                            for kk in range(2):
                                nc_g.indirect_dma_start(
                                    ins["slots"], bass.IndirectOffsetOnAxis(ap=sidx[d][:, 2 * t + kk:2 * t + kk + 1], axis=0),
                                    rows[d][:, t, kk, :], None, bounds_check=SLOTS - 1,
                                    oob_is_err=False).then_inc(scattered[d], 16)
                    if on(1):
                        m, d = i - 1, 1 - par
                        pool.wait_ge(mv_done, G * m + G)
                        after(pool, n_done, m - 1)
                        after(pool, rs_done, 2 * m)
                        after(pool, nn_done, m - 1)
                        settle(pool, s)
                        nc_g.tensor_scalar(ve[:, 0, :], mv[d][:, :, 1], EPS, None, ALU.add).then_inc(ve_done, 1)
                        nc_g.tensor_scalar(ve[:, 1, :], mv[d][:, :, 1], 1.0 + EPS, EPS * EPS,
                                           ALU.mult, ALU.add).then_inc(ve_done, 1)
                        pool.wait_ge(ve_done, 2 * m + 2)
                        settle(pool, s)
                        nc_g.tensor_copy(rs[d][:, 2, :], mv[d][:, :, 0]).then_inc(rs_done, 1)
                        nc_g.tensor_tensor(rs[d][:, 0:2, :].rearrange("p a t -> p (a t)"), ve[:].rearrange("p a t -> p (a t)"),
                                           s.expo[:], ALU.pow).then_inc(rs_done, 1)
                    if on(2):
                        g, b = i - 2, par
                        pool.wait_ge(rs_done, 2 * g + 2)
                        after(pool, res_done, g - 1)
                        settle(pool, s)
                        nc_g.tensor_copy(nn[b][:], s.h[:, bass.ds(g * G, G), :]).then_inc(copy_done, 1)
                        pool.wait_ge(copy_done, g + 1)
                        settle(pool, s)
                        for t in range(G):
                            last = nc_g.tensor_scalar(nn[b][:, t, :], nn[b][:, t, :],
                                                      rs[b][:, 2, t:t + 1], rs[b][:, 0, t:t + 1], ALU.subtract, ALU.mult)
                        last.then_inc(nn_done, 1)
                    if on(4):
                        f, c = i - 4, par
                        pool.wait_ge(mv2_done, G * f + G)
                        after(pool, rs2_done, f)
                        after(pool, n2_done, f - 1)
                        settle(pool, s)
                        nc_g.tensor_scalar(ve2[:], mv2[c][:, :, 1], EPS, None, ALU.add).then_inc(ve2_done, 1)
                        pool.wait_ge(ve2_done, f + 1)
                        settle(pool, s)
                        nc_g.tensor_tensor(rs2[c][:], ve2[:], s.expo[:, 0:G], ALU.pow).then_inc(rs2_done, 1)
                        pool.wait_ge(res_done, f + 1)
                        settle(pool, s)
                        hs = s.h[:, bass.ds(f * G, G), :]
                        nc_g.tensor_tensor(hs, xa[c][:], hs, ALU.add).then_inc(sum_done, 1)
                    if on(5):
                        r, c = i - 5, 1 - par
                        pool.wait_ge(n2_done, r + 1)
                        settle(pool, s)
                        nc_g.tensor_copy(rows[c][:, :, 1, 0:P], rows[c][:, :, 0, 0:P]).then_inc(rows_done, 1)
                        nc_g.tensor_copy(rows[c][:, :, :, P:P + 1].bitcast(I32).rearrange("p t k a -> p t (k a)"),
                                         payload[:, bass.ds(r * G, G), :]).then_inc(rows_done, 1)

                pipelined(pool, body, 7, PAIR0)
                for b in range(2):
                    pool.wait_ge(scattered[b], 16 * 2 * G * (GROUPS // 2))

            @block.tensor
            def _(pe):
                pe.wait_ge(loaded, 16 * LOADS)
                pe.wait_ge(made, s.made2)

                def body(i, pair, par, on):
                    g, b = i - 2, par
                    w, c = i - 3, 1 - par
                    f, r, o = i - 4, i - 5, i - 6

                    def scores(w, c, t, half):
                        pe.wait_ge(kma_done, 2 * w + half + 1)
                        pe.wait_ge(kmb_done, 2 * w + half + 1)
                        after(pe, ex_done, 2 * (G * w + t) + half - 1)
                        nc.tensor.matmul(p_s[:, half * 512:(half + 1) * 512], q[c][:, t * P:(t + 1) * P],
                                         km[c][:, HALF * half:HALF * half + HALF, t * P:(t + 1) * P],
                                         start=True, stop=True).then_inc(s_ps, 1)

                    def turn(t, half):
                        pe.wait_ge(ex_done, 2 * (G * w + t) + half + 1)
                        after(pe, etb_done if half else eta_done, G * w + t)
                        for hd in range(HALF * half, HALF * half + HALF):
                            last = nc.tensor.transpose(p_t[:, hd * P:(hd + 1) * P], ex[t % 2][:, hd, :], s.ident[:])
                        last.then_inc(et_ps, 1)

                    def weigh(t):
                        pe.wait_ge(eta_done, G * w + t + 1)
                        pe.wait_ge(etb_done, G * w + t + 1)
                        if t == 0:
                            pe.wait_ge(v_done, 2 * w + 2)
                            after(pe, att_done, w)
                        for gr in range(4):
                            for hp in range(2):
                                last = nc.tensor.matmul(p_o[32 * gr:32 * gr + 32, t * P:(t + 1) * P],
                                                        vpad[c][:, t * 4 + gr, hp, :], et[t % 2][:, 2 * gr + hp, :],
                                                        start=(hp == 0), stop=(hp == 1))
                        last.then_inc(pv_ps, 1)

                    if on(3):
                        scores(w, c, 1, 0)
                        turn(0, 0)
                    if on(2):
                        pe.wait_ge(n_done, g + 1)
                        after(pe, lg_done, r)
                        for t in range(G):
                            last = nc.tensor.transpose(b_y[:, t * P:(t + 1) * P], n[b][:, t, :], s.ident[:])
                        last.then_inc(nt_ps, 1)
                    if on(3):
                        scores(w, c, 1, 1)
                        turn(0, 1)
                    if on(4):
                        pe.wait_ge(att_done, f + 1)
                        pe.wait_ge(rden_done, f + 1)
                        for t in range(G):
                            last = nc.tensor.matmul(p_r[:, t * P:(t + 1) * P], att[:, t * P:(t + 1) * P], wo[:],
                                                    start=True, stop=True)
                        last.then_inc(wo_ps, 1)
                    if on(2):
                        pe.wait_ge(xt_done, g + 1)
                        nc.tensor.matmul(b_y[:], wq[:], xt[:], start=True, stop=True).then_inc(q_ps, 1)
                    if on(3):
                        scores(w, c, 2, 0)
                        turn(1, 0)
                        weigh(0)
                    if on(2):
                        after(pe, v_done, 2 * g)
                        after(pe, x2_done, r)
                        nc.tensor.matmul(b_x[:], wk[:], xt[:], start=True, stop=True).then_inc(k_ps, 1)
                    if on(3):
                        scores(w, c, 2, 1)
                        turn(1, 1)
                    if on(3):
                        scores(w, c, 3, 0)
                        turn(2, 0)
                        weigh(1)
                        scores(w, c, 3, 1)
                        turn(2, 1)
                    if on(2):
                        pe.wait_ge(k_done, g + 1)
                        for t in range(G):
                            last = nc.tensor.matmul(b_x[:, t * P:(t + 1) * P], xt[:, t * P:(t + 1) * P], wv[:],
                                                    start=True, stop=True)
                        last.then_inc(v_ps, 1)
                    if on(6):
                        pe.wait_ge(ohs_done, o + 1)
                        if on(4):
                            pe.wait_ge(res_done, f + 1)
                        after(pe, cb_done, 2 * o)
                        nc.tensor.matmul(p_r[:, 0:G * E], before[:], ohs[:], start=True, stop=False, skip_group_check=True)
                        for t in range(G):
                            last = nc.tensor.matmul(
                                p_r[:, (t + 1) * E:(G + 1) * E].rearrange("p (t e) -> p t e", e=E), ones[:],
                                ohs[:, t:t + 1, :].to_broadcast([P, G - t, E]), start=False, stop=(t == G - 1),
                                skip_group_check=True)
                        last.then_inc(cum_ps, 1)
                    if on(2):
                        pe.wait_ge(q_done, g + 1)
                        scores(g, b, 0, 0)
                    if on(3):
                        turn(3, 0)
                        weigh(2)
                    if on(5):
                        pe.wait_ge(n2_done, r + 1)
                        after(pe, x2_done, r)
                        if on(2):
                            pe.wait_ge(v_done, 2 * g + 2)
                        for t in range(G):
                            last = nc.tensor.transpose(b_x[:, t * P:(t + 1) * P], rows[1 - par][:, t, 0, 0:P], s.ident[:])
                        last.then_inc(x2_ps, 1)
                    if on(2):
                        scores(g, b, 0, 1)
                    if on(3):
                        turn(3, 1)
                        pe.wait_ge(rwide_done, w + 1)
                        after(pe, res_done, w)
                        if on(6):
                            pe.wait_ge(cb_done, 2 * o + 2)
                        for t in range(G):
                            last = nc.tensor.transpose(p_r[:, t * P:(t + 1) * P], rwide[:, t * P:(t + 1) * P], s.ident[:])
                        last.then_inc(r_ps, 1)
                        weigh(3)
                    if on(5):
                        pe.wait_ge(x2_done, r + 1)
                        if on(2):
                            pe.wait_ge(q_done, g + 1)
                        after(pe, lg_done, r)
                        for t in range(G):
                            last = nc.tensor.matmul(b_y[:, t * E:(t + 1) * E], x2t[:, t * P:(t + 1) * P], wr[:],
                                                    start=True, stop=True)
                        last.then_inc(lg_ps, 1)

                pipelined(pe, body, 6, PAIR0)

            @block.scalar
            def _(act):
                act.wait_ge(made, s.made2)

                def body(i, pair, par, on):
                    g, b = i - 2, par
                    w, c = i - 3, 1 - par
                    r, o = i - 5, i - 6

                    def exps(w, c, t, half):
                        act.wait_ge(mx_done, 2 * (G * w + t) + half + 1)
                        after(act, et_ps, 2 * (G * w + t) + half - 3)
                        if t == 0:
                            after(act, rsum_done, w - 1)
                        for hd in range(HALF * half, HALF * half + HALF):
                            last = nc.scalar.activation(ex[t % 2][:, hd, :], p_s[:, hd * P:(hd + 1) * P], ACT.Exp,
                                                        bias=mx[t % 2][:, hd:hd + 1],
                                                        accum_out=sums[c][:, t * HEADS + hd:t * HEADS + hd + 1])
                        last.then_inc(ex_done, 1)

                    def one_head_keys(half):
                        for hd in range(HALF * half, HALF * half + KEYS_ACT):
                            last = nc.scalar.activation(km[b][:, hd, :], k[:], ACT.Copy, scale=headmask[:, hd:hd + 1])
                        last.then_inc(kma_done, 1)

                    def eta(t):
                        act.wait_ge(et_ps, 2 * (G * w + t) + 1)
                        after(act, pv_ps, G * w + t - 1)
                        nc.scalar.copy(et[t % 2][:, 0:4, :], p_t[:, 0:512].rearrange("p (h n) -> p h n", h=4)).then_inc(eta_done, 1)

                    if on(2):
                        act.wait_ge(nt_ps, g + 1)
                        after(act, v_ps, g)
                        nc.scalar.activation(xt[:], b_y[:], ACT.Identity, bias=s.vec[:, C_L1B:C_L1B + 1],
                                             scale=s.vec[:, C_L1G:C_L1G + 1]).then_inc(xt_done, 1)
                    if on(3):
                        exps(w, c, 1, 0)
                        eta(0)
                        exps(w, c, 1, 1)
                    if on(2):
                        act.wait_ge(q_ps, g + 1)
                        after(act, s_ps, 2 * G * (g - 1))
                        nc.scalar.activation(q[b][:], b_y[:], ACT.Copy, scale=float(DH) ** -0.5).then_inc(q_done, 1)
                    if on(3):
                        exps(w, c, 2, 0)
                        eta(1)
                    if on(2):
                        act.wait_ge(k_ps, g + 1)
                        after(act, kma_done, 2 * g)
                        after(act, kmb_done, 2 * g)
                        nc.scalar.copy(k[:], b_x[:]).then_inc(k_done, 1)
                    if on(3):
                        exps(w, c, 2, 1)
                    if on(2):
                        act.wait_ge(k_done, g + 1)
                        one_head_keys(0)
                    if on(3):
                        exps(w, c, 3, 0)
                        eta(2)
                    if on(2):
                        one_head_keys(1)
                    if on(3):
                        exps(w, c, 3, 1)
                    if on(6):
                        act.wait_ge(step, STEPS * o + 2)
                        nc.scalar.activation(el[:], dl[:], ACT.Exp).then_inc(el_done, 1)
                    if on(2):
                        exps(g, b, 0, 0)
                    if on(3):
                        eta(3)
                    if on(5):
                        act.wait_ge(x2_ps, r + 1)
                        after(act, lg_ps, r)
                        nc.scalar.activation(x2t[:], b_x[:], ACT.Identity, bias=s.vec[:, C_L2B:C_L2B + 1],
                                             scale=s.vec[:, C_L2G:C_L2G + 1]).then_inc(x2_done, 1)
                    if on(2):
                        exps(g, b, 0, 1)
                    if on(3):
                        act.wait_ge(r_ps, w + 1)
                        after(act, att_done, w)
                        nc.scalar.copy(rden[:], p_r[:]).then_inc(rden_done, 1)
                    if on(5):
                        act.wait_ge(lg_ps, r + 1)
                        after(act, topi_done, G * r)
                        nc.scalar.copy(lg[:], b_y[:, 0:G * E].rearrange("p (t e) -> p t e", e=E)).then_inc(lg_done, 1)

                pipelined(act, body, 6, PAIR0)

            @block.vector
            def _(dve):
                V = nc.vector
                V.memset(zeros[:], 0.0).then_inc(zeros_made, 1)
                dve.wait_ge(made, s.made2)

                def stats(src, bnb, mvb, bn_sem, mv_sem, k0):
                    after(dve, mv_sem, G * k0)
                    settle(dve, s)
                    for t in range(G):
                        V.bn_stats(bnb[:, t, :], src(t)).then_inc(bn_sem, 1)
                    for t in range(G):
                        dve.wait_ge(bn_sem, G * k0 + t + 1)
                        settle(dve, s)
                        V.bn_aggr(mvb[:, t, :], bnb[:, t, :]).then_inc(mv_sem, 1)

                def body(i, pair, par, on):
                    g, b = i - 2, par
                    w, c = i - 3, 1 - par
                    f, r, o = i - 4, i - 5, i - 6

                    def maxes(w, t, half):
                        dve.wait_ge(s_ps, 2 * (G * w + t) + half + 1)
                        after(dve, ex_done, 2 * (G * w + t) + half - 3)
                        V.tensor_reduce(mx[t % 2][:, HALF * half:HALF * half + HALF],
                                        p_s[:, half * 512:(half + 1) * 512].rearrange("p (h n) -> p h n", h=HALF), AX,
                                        ALU.max, negate=True).then_inc(mx_done, 1)

                    def one_head_keys(half):
                        for hd in range(HALF * half + KEYS_ACT, HALF * half + HALF):
                            last = V.tensor_scalar(km[b][:, hd, :], k[:], headmask[:, hd:hd + 1], None, ALU.mult)
                        last.then_inc(kmb_done, 1)

                    def etb(t):
                        dve.wait_ge(et_ps, 2 * (G * w + t) + 2)
                        after(dve, pv_ps, G * w + t - 1)
                        V.tensor_copy(et[t % 2][:, 4:8, :], p_t[:, 512:1024].rearrange("p (h n) -> p h n", h=4)).then_inc(etb_done, 1)

                    count = [0]

                    def stepped(ins_):
                        count[0] += 1
                        ins_.then_inc(step, 1)

                    def steps_done(group=o):
                        dve.wait_ge(step, STEPS * group + count[0])

                    if on(3):
                        maxes(w, 1, 0)
                        maxes(w, 1, 1)
                        etb(0)
                    if on(0):
                        after(dve, rs_done, 2 * (i - 1))
                        after(dve, n_done, i - 1)
                        settle(dve, s)
                        stats(lambda t: s.h[:, bass.ds(i * G + t, 1), :].rearrange("p a n -> p (a n)"), bn, mv[par],
                              bn_done, mv_done, i)
                    if on(7):
                        z, count[0] = i - 7, STEPS - 4
                        dve.wait_ge(el_done, z + 1)
                        stepped(V.tensor_scalar(gs[:], el[:], 1.0, None, ALU.add))
                        steps_done(z)
                        stepped(V.reciprocal(gg[:, :, 0], gs[:]))
                        steps_done(z)
                        stepped(V.tensor_tensor(gg[:, :, 1], gg[:, :, 0], el[:], ALU.mult))
                        steps_done(z)
                        stepped(V.tensor_tensor(s.gates[:, bass.ds(z * G, G), :], gg[:],
                                                keep[:].rearrange("p (t k) -> p t k", k=2), ALU.mult))
                        count[0] = 0
                    if on(6):
                        dve.wait_ge(lg_done, o + 1)
                        settle(dve, s)
                        for t in range(G):
                            V.max(top[:, t, :], lg[:, t, :]).then_inc(top_done, 1)
                        for t in range(G):
                            dve.wait_ge(top_done, G * o + t + 1)
                            settle(dve, s)
                            V.max_index(topi[:, t, :], top[:, t, :], lg[:, t, :]).then_inc(topi_done, 1)
                    if on(3):
                        maxes(w, 2, 0)
                        maxes(w, 2, 1)
                        etb(1)
                    if on(4):
                        dve.wait_ge(wo_ps, f + 1)
                        dve.wait_ge(nn_done, f + 1)
                        after(dve, n2_done, f - 1)
                        after(dve, sum_done, f - 1)
                        V.tensor_tensor(xa[par][:], p_r[:].rearrange("p (t n) -> p t n", t=G), nn[par][:], ALU.add).then_inc(res_done, 1)
                        dve.wait_ge(res_done, f + 1)
                        after(dve, rs2_done, f - 1)
                        settle(dve, s)
                        stats(lambda t: xa[par][:, t, :], bn2, mv2[par], bn2_done, mv2_done, f)
                    if on(6):
                        dve.wait_ge(topi_done, G * o + G)
                        stepped(V.tensor_copy(ixf[:], topi[:, :, 0:2]))
                        after(dve, el_done, o)
                        stepped(V.tensor_tensor(dl[:], top[:, :, 1], top[:, :, 0], ALU.subtract))
                        steps_done()
                        stepped(V.tensor_tensor(
                            oh[:], iota_f[:].rearrange("p (a e) -> p a e", a=1).to_broadcast([P, G * 2, E]),
                            ixf[:].rearrange("p t (k a) -> p (t k) a", a=1).to_broadcast([P, G * 2, E]), ALU.is_equal))
                        steps_done()
                        o2 = oh[:].rearrange("p (t k) e -> p t k e", k=2)
                        after(dve, cum_ps, o)
                        V.tensor_tensor(ohs[:], o2[:, :, 0, :], o2[:, :, 1, :], ALU.add).then_inc(ohs_done, 1)
                    if on(3):
                        maxes(w, 3, 0)
                        maxes(w, 3, 1)
                    if on(2):
                        dve.wait_ge(k_done, g + 1)
                        after(dve, s_ps, 2 * G * (g - 1))
                        one_head_keys(0)
                    if on(3):
                        etb(2)
                    if on(2):
                        one_head_keys(1)
                    if on(5):
                        dve.wait_ge(rs2_done, r + 1)
                        if on(7):
                            dve.wait_ge(scattered[1 - par], (pair - 3 + par) * (16 * 2 * G))
                        for t in range(G):
                            last = V.tensor_scalar(rows[1 - par][:, t, 0, 0:P], xa[1 - par][:, t, :],
                                                   mv2[1 - par][:, t, 0:1], rs2[1 - par][:, t:t + 1], ALU.subtract, ALU.mult)
                        last.then_inc(n2_done, 1)
                    if on(2):
                        dve.wait_ge(v_ps, g + 1)
                        after(dve, pv_ps, G * (g - 1))
                        for hp in range(2):
                            V.tensor_copy(vpad[b][:, :, hp, 16 * hp:16 * hp + 16],
                                          b_x[:].rearrange("p (a k d) -> p a k d", k=2, d=DH)[:, :, hp, :]).then_inc(v_done, 1)
                    if on(1):
                        m, d = i - 1, 1 - par
                        dve.wait_ge(rs_done, 2 * m + 2)
                        after(dve, nt_ps, m - 1)
                        for t in range(G):
                            last = V.tensor_scalar(n[d][:, t, :], s.h[:, bass.ds(m * G + t, 1), :].rearrange("p a n -> p (a n)"),
                                                   mv[d][:, t, 0:1], rs[d][:, 1, t:t + 1], ALU.subtract, ALU.mult)
                        last.then_inc(n_done, 1)
                    if on(2):
                        maxes(g, 0, 0)
                    if on(6):
                        dve.wait_ge(cum_ps, o + 1)
                        V.tensor_tensor(cb[:], p_r[:, 0:G * E].rearrange("p (t e) -> p t e", e=E),
                                        base[:].rearrange("p (a e) -> p a e", a=1).to_broadcast([P, G, E]),
                                        ALU.add).then_inc(cb_done, 1)
                        dve.wait_ge(cb_done, 2 * o + 1)
                        V.tensor_tensor(base[:], p_r[:, G * E:(G + 1) * E], base[:], ALU.add).then_inc(cb_done, 1)
                        dve.wait_ge(cb_done, 2 * o + 2)
                    if on(3):
                        dve.wait_ge(ex_done, 2 * G * (w + 1))
                        V.reciprocal(rsum[:], sums[c][:]).then_inc(rsum_done, 1)
                        dve.wait_ge(rsum_done, w + 1)
                        after(dve, r_ps, w)
                        V.tensor_copy(rwide[:].rearrange("p (a d) -> p a d", d=DH),
                                      rsum[:].rearrange("p (a d) -> p a d", d=1).to_broadcast([P, G * HEADS, DH])
                                      ).then_inc(rwide_done, 1)
                    if on(2):
                        maxes(g, 0, 1)
                    if on(3):
                        etb(3)
                    if on(6):
                        stepped(V.tensor_tensor(
                            pm[:].rearrange("p (t k) e -> p t k e", k=2), oh[:].rearrange("p (t k) e -> p t k e", k=2),
                            cb[:].rearrange("p t (a e) -> p t a e", a=1).to_broadcast([P, G, 2, E]), ALU.mult))
                        steps_done()
                        stepped(V.tensor_reduce(pos[:], pm[:], AX, ALU.add))
                        steps_done()
                        stepped(V.tensor_scalar(keep[:], pos[:], float(CAP), None, ALU.is_lt))
                        stepped(V.scalar_tensor_tensor(slot[:], ixf[:].rearrange("p t k -> p (t k)"), float(CAP), pos[:],
                                                       ALU.mult, ALU.add))
                        steps_done()
                        stepped(V.tensor_scalar(far[:], keep[:], -float(NOWHERE), float(NOWHERE), ALU.mult, ALU.add))
                        steps_done()
                        V.tensor_tensor(sidx[par][:], slot[:], far[:], ALU.add).then_inc(slot_done, 1)
                    if on(3):
                        dve.wait_ge(pv_ps, G * w + G)
                        dve.wait_ge(rden_done, w + 1)
                        after(dve, wo_ps, w)
                        V.tensor_tensor(att[:], p_o[:], rden[:], ALU.mult).then_inc(att_done, 1)

                pipelined(dve, body, 7, PAIR0)
                dve.wait_ge(cb_done, 2 * GROUPS)
                V.tensor_copy(s.counts[:], base[0:1, :]).then_inc(counted, 1)
                dve.wait_ge(counted, 1)


def phase3(nc, s, ins):
    UNIT = ((0, 1), (1, 1), (2, 2), (4, 4))
    NU = len(UNIT)
    BUFS = 4
    assert sum(n for _, n in UNIT) * P == CAP
    with ExitStack() as ctx:
        def sb(name, shape, dt=F32):
            return ctx.enter_context(nc.sbuf_tensor("c_" + name, shape, dt))

        def sem(name):
            return ctx.enter_context(nc.semaphore("c_" + name))

        b1 = sb("b1", [P, E * FC])
        w12 = [sb(f"w12_{i}", [P, 2 * FF + P]) for i in range(BUFS)]
        xin = [sb(f"xin{i}", [P, CAP // P, ROW]) for i in range(BUFS)]
        dest = [sb(f"dest{i}", [P, CAP // P], I32) for i in range(BUFS)]
        xt = [sb(f"xt{i}", [P, CAP]) for i in range(2)]
        ht = [sb(f"ht{i}", [P, FC, CAP]) for i in range(2)]
        y = [sb(f"y{i}", [P, CAP // P, P]) for i in range(2)]
        p_x, p_y = ([ctx.enter_context(nc.psum_tensor(f"c_{x}{i}", [P, 512], F32)) for i in range(2)] for x in ("px", "py"))
        p_h = [ctx.enter_context(nc.psum_tensor(f"c_ph{i}", [P, 512], F32)) for i in range(FC)]

        b_loaded = sem("b_loaded")
        w_loaded = [sem(f"w_loaded{i}") for i in range(BUFS)]
        x_loaded = [[sem(f"x_loaded{i}_{u}") for u in range(NU)] for i in range(BUFS)]
        sent = [sem(f"sent{u}") for u in range(NU)]
        buffers_sent = sem("buffers_sent")
        x_ps, xt_done, dest_done, h_ps, ht_done, y_ps, y_done = (
            sem(x) for x in ("x_ps", "xt", "dest", "h_ps", "ht", "y_ps", "y"))

        def experts(body, eng, lag):
            regs = [eng.alloc_register(f"rows{r}") for r in range(4)]

            def step(i, quad, ph, on):
                if on(0):
                    eng.load(regs[ph], s.counts[0:1, bass.ds(i, 1)])
                body(i, quad, ph, on, lambda l: regs[(ph - l) % 4])
            for i in range(4):
                step(i, i // 4, i % 4, lambda l, i=i: 0 <= i - l)
            with eng.Fori(1, E // 4) as quad:
                for ph in range(4):
                    step(quad * 4 + ph, quad, ph, lambda l: True)
            for i in range(E, E + lag):
                step(i, i // 4, i % 4, lambda l, i=i: i - l < E)

        def later_units(eng, count, work, skipped):
            with eng.If_cmp(count, UNIT[1][0] * P, "IS_GT"):
                work(1)
                with eng.If_cmp(count, UNIT[2][0] * P, "IS_GT"):
                    work(2)
                    with eng.If_cmp(count, UNIT[3][0] * P, "IS_GT"):
                        work(3)
                    with eng.Else():
                        skipped(3)
                with eng.Else():
                    skipped(2)
            with eng.Else():
                skipped(1)

        def counting(eng, done, e, steps=1):
            def skipped(u):
                eng.wait_ge(done, (e * NU + u) * steps)
                eng.sem_inc(done, (NU - u) * steps)
            return skipped

        with nc.Block() as block:
            @block.sync
            def _(sp):
                sp.dma_start(b1[:], ins["b1"]).then_inc(b_loaded, 16)

                def body(e, quad, ph, on, count):
                    after(sp, x_ps, NU * (e - BUFS) + NU)
                    after(sp, dest_done, NU * (e - BUFS) + NU)

                    def load(u):
                        first, n = UNIT[u]
                        sp.dma_start(xin[ph][:, first:first + n, :],
                                     ins["slots"][bass.ds(e * CAP + first * P, n * P)].rearrange("(p t) n -> p t n", t=n)
                                     ).then_inc(x_loaded[ph][u], 16)

                    def skipped(u):
                        for v in range(u, NU):
                            sp.sem_inc(x_loaded[ph][v], 16)
                    load(0)
                    after(sp, y_done, NU * (e - BUFS) + NU)
                    sp.dma_start(w12[ph][:],
                                 ins["w12"][bass.ds(e, 1)].rearrange("a p f -> p (a f)")).then_inc(w_loaded[ph], 16)
                    later_units(sp, count(0), load, skipped)

                experts(body, sp, 0)

            @block.tensor
            def _(pe):
                def body(i, quad, ph, on, count):
                    def turn(u):
                        e, b = i, ph
                        first, n = UNIT[u]
                        pe.wait_ge(x_loaded[b][u], 16 * quad + 16)
                        after(pe, xt_done, NU * e + u - 1)
                        for t in range(n):
                            last = nc.tensor.transpose(p_x[u % 2][:, t * P:(t + 1) * P], xin[b][:, first + t, 0:P], s.ident[:])
                        last.then_inc(x_ps, 1)

                    def layer1(u):
                        e, b = i - 1, (ph - 1) % 4
                        first, n = UNIT[u]
                        cols = slice(first * P, (first + n) * P)
                        pe.wait_ge(xt_done, NU * e + u + 1)
                        if u == 0:
                            pe.wait_ge(w_loaded[b], 16 * (quad + (ph - 1) // 4) + 16)
                            after(pe, ht_done, FC * NU * e)
                        for ch in range(FC):
                            if u > 0:
                                pe.wait_ge(ht_done, FC * (NU * e + u - 1) + ch + 1)
                            nc.tensor.matmul(p_h[ch][:, 0:n * P], w12[b][:, 0:FF].rearrange("p (f c) -> p c f", c=FC)[:, ch, :],
                                             xt[b % 2][:, cols], start=True, stop=True).then_inc(h_ps, 1)

                    def layer2(u):
                        e, b = i - 2, (ph - 2) % 4
                        first, n = UNIT[u]
                        pe.wait_ge(ht_done, FC * (NU * e + u) + FC)
                        after(pe, y_done, NU * e + u - 1)
                        for t in range(n):
                            for ch in range(FC):
                                last = nc.tensor.matmul(p_y[u % 2][:, t * P:(t + 1) * P],
                                                        ht[b % 2][:, ch, (first + t) * P:(first + t + 1) * P],
                                                        w12[b][:, FF + ch * P:FF + (ch + 1) * P], start=(ch == 0), stop=(ch == FC - 1))
                        last.then_inc(y_ps, 1)

                    if on(1):
                        layer1(0)
                    if on(2):
                        layer2(0)
                    if on(0):
                        turn(0)
                    if on(1):
                        later_units(pe, count(1), layer1, counting(pe, h_ps, i - 1, FC))
                    if on(2):
                        later_units(pe, count(2), layer2, counting(pe, y_ps, i - 2))
                    if on(0):
                        later_units(pe, count(0), turn, counting(pe, x_ps, i))

                experts(body, pe, 2)

            @block.scalar
            def _(act):
                act.wait_ge(b_loaded, 16)

                def body(i, quad, ph, on, count):
                    def gelu(u):
                        e, b = i - 1, (ph - 1) % 2
                        first, n = UNIT[u]
                        if u == 0:
                            after(act, y_ps, NU * (e - 2) + NU)
                        for ch in range(FC):
                            act.wait_ge(h_ps, FC * (NU * e + u) + ch + 1)
                            settle(act, s)
                            nc.scalar.activation(ht[b][:, ch, first * P:(first + n) * P], p_h[ch][:, 0:n * P],
                                                 ACT.Gelu_apprx_tanh, bias=b1[:, bass.ds(e * FC + ch, 1)]).then_inc(ht_done, 1)
                    if on(1):
                        gelu(0)
                        later_units(act, count(1), gelu, counting(act, ht_done, i - 1, FC))

                experts(body, act, 1)

            @block.vector
            def _(dve):
                def body(i, quad, ph, on, count):
                    def affine(u):
                        e, b = i, ph % 2
                        first, n = UNIT[u]
                        if u == 0:
                            after(dve, h_ps, FC * (NU * (e - 2) + NU))
                        dve.wait_ge(x_ps, NU * e + u + 1)
                        nc.vector.tensor_scalar(xt[b][:, first * P:(first + n) * P], p_x[u % 2][:, 0:n * P],
                                                s.vec[:, C_L2G:C_L2G + 1], s.vec[:, C_L2B:C_L2B + 1],
                                                ALU.mult, ALU.add).then_inc(xt_done, 1)

                    def result(u):
                        e, b = i - 2, (ph - 2) % 4
                        first, n = UNIT[u]
                        dve.wait_ge(y_ps, NU * e + u + 1)
                        if u == 0:
                            after(dve, buffers_sent, e - 1)
                        nc.vector.tensor_tensor(y[b % 2][:, first:first + n, :],
                                                p_y[u % 2][:, 0:n * P].rearrange("p (t n) -> p t n", t=n),
                                                w12[b][:, 2 * FF:].rearrange("p (t n) -> p t n", t=1).to_broadcast([P, n, P]),
                                                ALU.add).then_inc(y_done, 1)
                    if on(0):
                        affine(0)
                    if on(2):
                        result(0)
                    if on(2):
                        later_units(dve, count(2), result, counting(dve, y_done, i - 2))
                    if on(0):
                        later_units(dve, count(0), affine, counting(dve, xt_done, i))

                experts(body, dve, 2)

            @block.gpsimd
            def _(pool):
                issued = [pool.alloc_register(f"issued{u}") for u in range(NU)]
                for reg in issued:
                    pool.reg_mov(reg, 0)

                def body(i, quad, ph, on, count):
                    def keep_dest(u):
                        e, b = i, ph
                        first, n = UNIT[u]
                        pool.wait_ge(x_loaded[b][u], 16 * quad + 16)
                        settle(pool, s)
                        nc.gpsimd.tensor_copy(dest[b][:, first:first + n],
                                              xin[b][:, first:first + n, P:P + 1].bitcast(I32).rearrange("p t a -> p (t a)")
                                              ).then_inc(dest_done, 1)

                    def send(u):
                        e, b = i - 2, (ph - 2) % 4
                        first, n = UNIT[u]
                        pool.wait_ge(y_done, NU * e + u + 1)
                        pool.wait_ge(dest_done, NU * e + u + 1)
                        settle(pool, s)
                        for t in range(first, first + n):
                            nc.gpsimd.indirect_dma_start(
                                ins["back"], bass.IndirectOffsetOnAxis(ap=dest[b][:, t:t + 1], axis=0),
                                y[b % 2][:, t, :], None, bounds_check=2 * TOKENS - 1, oob_is_err=False).then_inc(sent[u], 16)
                        pool.reg_add(issued[u], issued[u], 16 * n)

                    def landed(u):
                        pool.wait_ge(sent[u], issued[u])
                        settle(pool, s)
                    if on(3):
                        landed(0)
                        later_units(pool, count(3), landed, lambda u: None)
                        pool.sem_inc(buffers_sent, 1)
                    if on(0):
                        keep_dest(0)
                        later_units(pool, count(0), keep_dest, counting(pool, dest_done, i))
                    if on(2):
                        send(0)
                        later_units(pool, count(2), send, lambda u: None)

                experts(body, pool, 3)


def phase4(nc, s, ins, out):
    BUFS = 4
    with ExitStack() as ctx:
        def sb(name, shape, dt=F32):
            return ctx.enter_context(nc.sbuf_tensor("d_" + name, shape, dt))

        def sem(name):
            return ctx.enter_context(nc.semaphore("d_" + name))

        got = [sb(f"got{i}", [P, G, 2, P]) for i in range(BUFS)]
        second = [sb(f"second{i}", [P, G, P]) for i in range(2)]
        part = [sb(f"part{i}", [P, G, P]) for i in range(2)]
        res = [sb(f"res{i}", [P, G, P]) for i in range(BUFS)]
        got_in = [sem(f"got_in{i}") for i in range(BUFS)]
        part_done, second_done, res_done = sem("part"), sem("second"), sem("res")
        stored = [sem(f"stored{i}") for i in range(BUFS)]

        def groups(eng, body):
            for i in range(BUFS):
                body(i, 0, i)
            with eng.Fori(1, GROUPS // BUFS) as quad:
                for ph in range(BUFS):
                    body(quad * BUFS + ph, quad, ph)

        with nc.Block() as block:
            @block.sync
            def _(sp):
                def body(i, quad, ph):
                    after(sp, res_done, i - BUFS + 1)
                    sp.dma_start(got[ph][:], ins["back_tokens"][:, bass.ds(i * G, G)]).then_inc(got_in[ph], 16)
                groups(sp, body)

            @block.scalar
            def _(act):
                def body(i, quad, ph):
                    act.wait_ge(got_in[ph], 16 * quad + 16)
                    after(act, res_done, i - 1)
                    for t in range(G):
                        last = nc.scalar.activation(second[ph % 2][:, t, :], got[ph][:, t, 1, :], ACT.Copy,
                                                    scale=s.gates[:, bass.ds(i * G + t, 1), 1])
                    last.then_inc(second_done, 1)
                groups(act, body)

            @block.vector
            def _(dve):
                def body(i, quad, ph):
                    dve.wait_ge(got_in[ph], 16 * quad + 16)
                    for t in range(G):
                        last = nc.vector.scalar_tensor_tensor(
                            part[ph % 2][:, t, :], got[ph][:, t, 0, :], s.gates[:, bass.ds(i * G + t, 1), 0],
                            s.h[:, bass.ds(i * G + t, 1), :].rearrange("p a n -> p (a n)"), ALU.mult, ALU.add)
                    last.then_inc(part_done, 1)
                    dve.wait_ge(part_done, i + 1)
                    dve.wait_ge(second_done, i + 1)
                    after(dve, stored[ph], 16 * quad)
                    nc.vector.tensor_tensor(res[ph][:], part[ph % 2][:], second[ph % 2][:], ALU.add).then_inc(res_done, 1)
                groups(dve, body)

            @block.gpsimd
            def _(pool):
                def body(i, quad, ph):
                    pool.wait_ge(res_done, i + 1)
                    settle(pool, s)
                    pool.dma_start(out[:, bass.ds(i * G, G)], res[ph][:]).then_inc(stored[ph], 16)
                groups(pool, body)
                for b in range(BUFS):
                    pool.wait_ge(stored[b], 16 * (GROUPS // BUFS))


_DRAM = ["table", "ids", "vecs", "Wh", "bh", "bo", "Wqk", "Wo", "wq", "wk", "wv", "wo", "wr", "w12", "b1"]


def build(nc, ins, out):
    slots = nc.dram_tensor("slots", [SLOTS, ROW], F32).ap()
    back = nc.dram_tensor("back", [2 * TOKENS, P], F32).ap()
    ins["slots"] = slots
    ins["slot_parts"] = slots.rearrange("(a r) n -> a r n", r=8)
    ins["back"] = back
    ins["back_parts"] = back.rearrange("(a r) n -> a (r n)", r=BACK_PART // P)
    ins["back_tokens"] = back.rearrange("(s p k) n -> p s k n", p=P, k=2)
    s = Shared()
    with ExitStack() as ctx:
        constants(nc, ctx, s, ins)
        phase1(nc, s, ins)
        phase2(nc, s, ins)
        phase3(nc, s, ins)
        phase4(nc, s, ins, out.rearrange("s p n -> p s n"))


def kernel(**inputs):
    import concourse.bacc as bacc
    from concourse.bass_utils import run_bass_kernel_spmd

    a = {k: np.asarray(v) for k, v in inputs.items()}
    c = np.ascontiguousarray
    gamma, beta, bh = a["L0_attn_gamma"], a["L0_attn_beta"], a["L0_attn_bh"]
    arrays = {
        "table": c(a["L0_tok_conv_w"].transpose(1, 2, 0).reshape(VOCAB, TAPS * P)),
        "ids": c(a["x"].T),
        "vecs": c(np.stack([a["L0_attn_ln_g"], a["L0_attn_ln_b"], a["L0_attn_bqk"], gamma[0], gamma[1], beta[0],
                            beta[1], bh[2 * P:3 * P], bh[3 * P:4 * P], a["L0_ffn_ln1_g"],
                            a["L0_ffn_ln1_b"], a["L0_ffn_ln2_g"], a["L0_ffn_ln2_b"]], axis=1)),
        "Wh": c(a["L0_attn_Wh"]), "bh": c(bh.reshape(1, -1)), "bo": c(a["L0_attn_bo"].reshape(1, -1)), "Wqk": c(a["L0_attn_Wqk"]), "Wo": c(a["L0_attn_Wo"]),
        "wq": c(a["L0_ffn_wq"]), "wk": c(a["L0_ffn_wk"]), "wv": c(a["L0_ffn_wv"]), "wo": c(a["L0_ffn_wo"]),
        "wr": c(a["L0_ffn_wr"]), 
        "w12": c(np.concatenate([a["L0_ffn_w1"], a["L0_ffn_w2"].reshape(E, P, FC * P),
                                 np.broadcast_to(a["L0_ffn_b2"][:, None, :], (E, P, P))], axis=2)),
        "b1": c(a["L0_ffn_b1"].reshape(E, P, FC).transpose(1, 0, 2).reshape(P, E * FC)),
    }
    nc = bacc.Bacc("TRN2", target_bir_lowering=False, num_devices=1)
    ins = {k: nc.dram_tensor("in_" + k, arrays[k].shape, mybir.dt.from_np(arrays[k].dtype), kind="ExternalInput").ap()
           for k in _DRAM}
    out = nc.dram_tensor("out", [SEQS, P, P], F32, kind="ExternalOutput").ap()
    build(nc, ins, out)
    got = run_bass_kernel_spmd(nc, [{"in_" + k: arrays[k] for k in _DRAM}], core_ids=[0])
    return got.results[0]["out"]
```
